# Optimizing a Trainium2 kernel written in Bass

```python
import numpy as np
import jax
import jax.numpy as jnp

def _softmax(x, axis=-1):
    return jax.nn.softmax(x, axis=axis)

def _gelu(x):
    return jax.nn.gelu(x, approximate=True)

def _silu(x):
    return jax.nn.silu(x)

def _sigmoid(x):
    return jax.nn.sigmoid(x)

def _layernorm(x, axis=-1, eps=1e-05):
    m = jnp.mean(x, axis=axis, keepdims=True)
    v = jnp.var(x, axis=axis, keepdims=True)
    return (x - m) / jnp.sqrt(v + eps)

def _scatter_add(tgt, idx, src, axis=0):
    return tgt.at[idx].add(src)

def _segment_sum(src, seg, n):
    return jax.ops.segment_sum(src, seg, n)
kernel_name = 'mk_decoder_preln_d2_seqx_r8_043bb2'

def setup_inputs(seed: int=0):
    np.random.seed(seed)
    _w = jnp.asarray

    def _rec_inputs():
        import jax
        import jax.numpy as jnp
        _rk = jax.random.key(seed)
        x = 0.0003765 + 1 * jax.random.normal(jax.random.fold_in(_rk, 1), (8, 128, 256), jnp.float32)
        _lenS = 128 - jax.random.randint(jax.random.fold_in(_rk, 7), (8,), 0, max(1, 128 // 4) + 1, jnp.int32)
        _lenS2 = 128 - jax.random.randint(jax.random.fold_in(_rk, 8), (8,), 0, max(1, 128 // 4) + 1, jnp.int32)
        _ctx_2048P = jax.random.normal(jax.random.fold_in(_rk, 11), (8, 16, 256), jnp.float32)
        _ctx_2048c = jax.random.dirichlet(jax.random.fold_in(_rk, 511), 0.3 * jnp.ones((16,), jnp.float32), (8, 128))
        _ctx_2048t = jnp.einsum('bsk,bkd->bsd', _ctx_2048c, _ctx_2048P)
        _ctx_2048t = _ctx_2048t * jax.lax.rsqrt(jnp.mean(jnp.square(_ctx_2048t)) + 1e-12) * 0.953939
        ctx_2048 = -0.000292821 + 1.00034 * (_ctx_2048t + 0.3 * jax.random.normal(jax.random.fold_in(_rk, 611), (8, 128, 256), jnp.float32))
        return (x, ctx_2048)
    x, ctx_2048 = _rec_inputs()

    def _L0_attn_setup():
        import jax, jax.numpy as jnp
        import numpy as np
        B, S, D = (2, 512, 256)
        H, DK, DV = (16, 128, 128)
        SEG = 64
        UPDATE = 'delta'
        CAUSAL = True
        key = jax.random.key(seed)
        ks = jax.random.split(key, 6)
        s = 0.02
        return {'x': jax.random.normal(ks[0], (B, S, D), jnp.float32), 'Wq': jax.random.normal(ks[1], (D, H * DK), jnp.float32) * s, 'Wk': jax.random.normal(ks[2], (D, H * DK), jnp.float32) * s, 'Wv': jax.random.normal(ks[3], (D, H * DV), jnp.float32) * s, 'Wo': jax.random.normal(ks[4], (H * DV, D), jnp.float32) * s, 'betas': jax.random.normal(ks[5], (1, H, 1, DV), jnp.float32)}
    _L0_attn_all = _L0_attn_setup()
    _L0_attn_in = {k: v for k, v in _L0_attn_all.items() if k in ('Wq', 'Wk', 'Wv', 'Wo', 'betas')}
    del _L0_attn_all

    def _L0_xattn_setup():
        import jax, jax.numpy as jnp
        import numpy as np
        key = jax.random.key(seed)
        k1, k2, k3, k4, k5 = jax.random.split(key, 5)
        B, D_MODEL, L = (2, 128, 256)
        HEAD_DIM = 8
        H = D_MODEL // HEAD_DIM
        return {'k': jax.random.normal(k1, (B, D_MODEL, L), dtype=jnp.float32), 'v': jax.random.normal(k2, (B, D_MODEL, L), dtype=jnp.float32), 'q': jax.random.normal(k3, (B, D_MODEL, L), dtype=jnp.float32), 'ssm_kernel': jax.random.normal(k4, (H, L), dtype=jnp.float32), 'D': jax.random.normal(k5, (H,), dtype=jnp.float32), 'head_dim': HEAD_DIM}
    _L0_xattn_all = _L0_xattn_setup()
    _L0_xattn_in = {k: v for k, v in _L0_xattn_all.items() if k in ('ssm_kernel', 'D')}
    del _L0_xattn_all

    def _L0_ffn_setup():
        import jax, jax.numpy as jnp
        import numpy as np
        D_MODEL = 256
        HIDDEN = 4 * D_MODEL
        N_EXPERTS = 8
        TOP_K = 2
        CAP_FACTOR = 1.0
        key = jax.random.key(seed)
        ks = jax.random.split(key, 6)
        x = jax.random.normal(ks[0], (4, 256, D_MODEL), dtype=jnp.float32)
        wg = jax.random.normal(ks[1], (D_MODEL, N_EXPERTS), dtype=jnp.float32) * (1.0 / np.sqrt(D_MODEL))
        fc1_w = jax.random.normal(ks[2], (N_EXPERTS, D_MODEL, HIDDEN), dtype=jnp.float32) * 0.02
        fc1_b = jnp.zeros((N_EXPERTS, HIDDEN), dtype=jnp.float32)
        fc2_w = jax.random.normal(ks[3], (N_EXPERTS, HIDDEN, D_MODEL), dtype=jnp.float32) * 0.02
        fc2_b = jnp.zeros((N_EXPERTS, D_MODEL), dtype=jnp.float32)
        return {'x': x, 'wg': wg, 'fc1_w': fc1_w, 'fc1_b': fc1_b, 'fc2_w': fc2_w, 'fc2_b': fc2_b}
    _L0_ffn_all = _L0_ffn_setup()
    _L0_ffn_in = {k: v for k, v in _L0_ffn_all.items() if k in ('wg', 'fc1_w', 'fc1_b', 'fc2_w', 'fc2_b')}
    del _L0_ffn_all

    def _L1_attn_setup():
        import jax, jax.numpy as jnp
        import numpy as np
        import math
        D_MODEL = 256
        NUM_HEADS = 16
        HEAD_DIM = D_MODEL // NUM_HEADS
        key = jax.random.key(seed)
        k_x, k_wqkv, k_bqkv, k_wo, k_bo = jax.random.split(key, 5)
        B, S = (2, 256)
        scale = 1.0 / math.sqrt(D_MODEL)
        return {'x': jax.random.normal(k_x, (B, S, D_MODEL), dtype=jnp.float32), 'w_qkv': jax.random.normal(k_wqkv, (3 * D_MODEL, D_MODEL), dtype=jnp.float32) * scale, 'b_qkv': jax.random.normal(k_bqkv, (3 * D_MODEL,), dtype=jnp.float32) * 0.01, 'w_out': jax.random.normal(k_wo, (D_MODEL, D_MODEL), dtype=jnp.float32) * scale, 'b_out': jax.random.normal(k_bo, (D_MODEL,), dtype=jnp.float32) * 0.01}
    _L1_attn_all = _L1_attn_setup()
    _L1_attn_in = {k: v for k, v in _L1_attn_all.items() if k in ('w_qkv', 'b_qkv', 'w_out', 'b_out')}
    del _L1_attn_all

    def _L1_xattn_setup():
        import jax, jax.numpy as jnp
        import numpy as np
        N, D, L = (8, 128, 256)
        key = jax.random.key(seed)
        ks = jax.random.split(key, 5)
        s = 1.0 / np.sqrt(D)
        return {'X1': jax.random.normal(ks[0], (N, D, L), dtype=jnp.float32), 'X2': jax.random.normal(ks[1], (N, D, L), dtype=jnp.float32), 'QW': jax.random.normal(ks[2], (D, D), dtype=jnp.float32) * s, 'Qb': jnp.zeros((D,), dtype=jnp.float32), 'KW': jax.random.normal(ks[3], (D, D), dtype=jnp.float32) * s, 'Kb': jnp.zeros((D,), dtype=jnp.float32), 'VW': jax.random.normal(ks[4], (D, D), dtype=jnp.float32) * s, 'Vb': jnp.zeros((D,), dtype=jnp.float32)}
    _L1_xattn_all = _L1_xattn_setup()
    _L1_xattn_in = {k: v for k, v in _L1_xattn_all.items() if k in ('QW', 'Qb', 'KW', 'Kb', 'VW', 'Vb')}
    del _L1_xattn_all

    def _L1_ffn_setup():
        import jax, jax.numpy as jnp
        import numpy as np
        DIM_IN = 256
        DIM_HIDDEN = 1024
        key = jax.random.key(seed)
        k_x, k_g, k_u, k_d = jax.random.split(key, 4)
        s_in = 1.0 / np.sqrt(DIM_IN)
        s_hid = 1.0 / np.sqrt(DIM_HIDDEN)
        x = jax.random.normal(k_x, (4, 256, DIM_IN), dtype=jnp.float32)
        w_gate = jax.random.uniform(k_g, (DIM_HIDDEN, DIM_IN), jnp.float32, -s_in, s_in)
        w_up = jax.random.uniform(k_u, (DIM_HIDDEN, DIM_IN), jnp.float32, -s_in, s_in)
        w_down = jax.random.uniform(k_d, (DIM_IN, DIM_HIDDEN), jnp.float32, -s_hid, s_hid)
        return {'x': x, 'w_gate': w_gate, 'w_up': w_up, 'w_down': w_down}
    _L1_ffn_all = _L1_ffn_setup()
    _L1_ffn_in = {k: v for k, v in _L1_ffn_all.items() if k in ('w_gate', 'w_up', 'w_down')}
    del _L1_ffn_all
    return {'x': x, 'ctx_2048': ctx_2048, 'L0_attn_Wq': _L0_attn_in['Wq'], 'L0_attn_Wk': _L0_attn_in['Wk'], 'L0_attn_Wv': _L0_attn_in['Wv'], 'L0_attn_Wo': _L0_attn_in['Wo'], 'L0_attn_betas': _L0_attn_in['betas'], 'L0_xattn_ssm_kernel': _L0_xattn_in['ssm_kernel'], 'L0_xattn_D': _L0_xattn_in['D'], 'L0_ffn_wg': _L0_ffn_in['wg'], 'L0_ffn_fc1_w': _L0_ffn_in['fc1_w'], 'L0_ffn_fc1_b': _L0_ffn_in['fc1_b'], 'L0_ffn_fc2_w': _L0_ffn_in['fc2_w'], 'L0_ffn_fc2_b': _L0_ffn_in['fc2_b'], 'L1_attn_w_qkv': _L1_attn_in['w_qkv'], 'L1_attn_b_qkv': _L1_attn_in['b_qkv'], 'L1_attn_w_out': _L1_attn_in['w_out'], 'L1_attn_b_out': _L1_attn_in['b_out'], 'L1_xattn_QW': _L1_xattn_in['QW'], 'L1_xattn_Qb': _L1_xattn_in['Qb'], 'L1_xattn_KW': _L1_xattn_in['KW'], 'L1_xattn_Kb': _L1_xattn_in['Kb'], 'L1_xattn_VW': _L1_xattn_in['VW'], 'L1_xattn_Vb': _L1_xattn_in['Vb'], 'L1_ffn_w_gate': _L1_ffn_in['w_gate'], 'L1_ffn_w_up': _L1_ffn_in['w_up'], 'L1_ffn_w_down': _L1_ffn_in['w_down']}

def reference(x, ctx_2048, L0_attn_Wq, L0_attn_Wk, L0_attn_Wv, L0_attn_Wo, L0_attn_betas, L0_xattn_ssm_kernel, L0_xattn_D, L0_ffn_wg, L0_ffn_fc1_w, L0_ffn_fc1_b, L0_ffn_fc2_w, L0_ffn_fc2_b, L1_attn_w_qkv, L1_attn_b_qkv, L1_attn_w_out, L1_attn_b_out, L1_xattn_QW, L1_xattn_Qb, L1_xattn_KW, L1_xattn_Kb, L1_xattn_VW, L1_xattn_Vb, L1_ffn_w_gate, L1_ffn_w_up, L1_ffn_w_down):
    import jax
    import jax.numpy as jnp

    def _L0_attn_ref(x, Wq, Wk, Wv, Wo, betas):
        import jax, jax.numpy as jnp
        import numpy as np
        B, S, D = (2, 512, 256)
        H, DK, DV = (16, 128, 128)
        SEG = 64
        UPDATE = 'delta'
        CAUSAL = True
        Bsz, seq, _ = x.shape
        nseg = seq // SEG
        q = (x @ Wq).reshape(Bsz, seq, H, DK).transpose(0, 2, 1, 3)
        k = (x @ Wk).reshape(Bsz, seq, H, DK).transpose(0, 2, 1, 3)
        v = (x @ Wv).reshape(Bsz, seq, H, DV).transpose(0, 2, 1, 3)
        qs = q.reshape(Bsz, H, nseg, SEG, DK).transpose(2, 0, 1, 3, 4)
        ks_ = k.reshape(Bsz, H, nseg, SEG, DK).transpose(2, 0, 1, 3, 4)
        vs = v.reshape(Bsz, H, nseg, SEG, DV).transpose(2, 0, 1, 3, 4)
        causal_mask = jnp.tril(jnp.ones((SEG, SEG), bool))
        scale = DK ** 0.5
        beta = jax.nn.sigmoid(betas)

        def step(carry, seg):
            mem, z = carry
            qq, kk, vv = seg
            sigma_q = jax.nn.elu(qq) + 1.0
            scores = jnp.einsum('bhsk,bhtk->bhst', qq, kk) / scale
            if CAUSAL:
                scores = jnp.where(causal_mask, scores, -jnp.inf)
            att_dot = jax.nn.softmax(scores, axis=-1) @ vv
            att_mem = sigma_q @ mem / (sigma_q @ z)
            sigma_k = jax.nn.elu(kk) + 1.0
            if UPDATE == 'linear':
                mem_new = mem + jnp.einsum('bhsk,bhsv->bhkv', sigma_k, vv)
            else:
                delta = vv - sigma_k @ mem / (sigma_k @ z)
                mem_new = mem + jnp.einsum('bhsk,bhsv->bhkv', sigma_k, delta)
            z_new = z + sigma_k.sum(axis=-2, keepdims=True).transpose(0, 1, 3, 2)
            att = beta * att_mem + (1.0 - beta) * att_dot
            out = att.reshape(Bsz, SEG, H * DV) @ Wo
            return ((mem_new, z_new), out)
        mem0 = jnp.zeros((Bsz, H, DK, DV), x.dtype)
        z0 = jnp.ones((Bsz, H, DK, 1), x.dtype) / DK
        _, outs = jax.lax.scan(step, (mem0, z0), (qs, ks_, vs))
        return outs.transpose(1, 0, 2, 3).reshape(Bsz, seq, D)

    def _L0_xattn_ref(k, v, q, ssm_kernel, D, head_dim):
        import jax, jax.numpy as jnp
        import numpy as np
        B, HD, L = k.shape
        H = HD // head_dim
        fft_size = 2 * L
        k_ = k.reshape(B, H, head_dim, L)
        v_ = v.reshape(B, H, head_dim, L)
        q_ = q.reshape(B, H, head_dim, L)
        kv = jnp.einsum('bhil,bhjl->bijhl', k_, v_)
        kv_f = jnp.fft.rfft(kv, n=fft_size)
        kernel_f = jnp.fft.rfft(ssm_kernel, n=fft_size)
        y = jnp.fft.irfft(kv_f * kernel_f, n=fft_size)[..., :L]
        out = y + kv * D[None, None, None, :, None]
        out = jnp.einsum('bijhl,bhil->bjhl', out, q_)
        out = jnp.transpose(out, (0, 2, 1, 3)).reshape(B, H * head_dim, L)
        return out.astype(k.dtype)

    def _L0_ffn_ref(x, wg, fc1_w, fc1_b, fc2_w, fc2_b):
        import jax, jax.numpy as jnp
        import numpy as np
        D_MODEL = 256
        HIDDEN = 4 * D_MODEL
        N_EXPERTS = 8
        TOP_K = 2
        CAP_FACTOR = 1.0
        B, L, D = x.shape
        S = B * L
        E = wg.shape[1]
        K = TOP_K
        C = int(K * S * CAP_FACTOR) // E
        xt = x.reshape(S, D)
        scores = jax.nn.softmax(xt.astype(jnp.float32) @ wg.astype(jnp.float32), axis=-1)
        gate_vals, idx = jax.lax.top_k(scores, K)
        gate_vals = gate_vals / jnp.clip(jnp.sum(gate_vals, axis=-1, keepdims=True), 1e-09)
        counts = jnp.zeros((E,), jnp.int32)
        disp = jnp.zeros((E, C, D), x.dtype)
        pos_safe_l, valid_l = ([], [])
        for s in range(K):
            mask = jax.nn.one_hot(idx[:, s], E, dtype=jnp.int32)
            loc = jnp.cumsum(mask, axis=0) - 1 + counts[None, :]
            pos = jnp.sum(loc * mask, axis=-1)
            counts = counts + jnp.sum(mask, axis=0)
            valid = pos < C
            pos_safe = jnp.where(valid, pos, 0)
            disp = disp.at[idx[:, s], pos_safe].add(xt * valid[:, None].astype(x.dtype))
            pos_safe_l.append(pos_safe)
            valid_l.append(valid)
        h = jax.nn.gelu(jnp.einsum('ecd,edh->ech', disp, fc1_w) + fc1_b[:, None, :], approximate=False)
        eo = jnp.einsum('ech,ehd->ecd', h, fc2_w) + fc2_b[:, None, :]
        y = jnp.zeros((S, D), x.dtype)
        for s in range(K):
            g = (gate_vals[:, s] * valid_l[s].astype(gate_vals.dtype)).astype(x.dtype)
            y = y + g[:, None] * eo[idx[:, s], pos_safe_l[s]]
        return y.reshape(B, L, D)

    def _L1_attn_ref(x, w_qkv, b_qkv, w_out, b_out):
        import jax, jax.numpy as jnp
        import numpy as np
        import math
        D_MODEL = 256
        NUM_HEADS = 16
        HEAD_DIM = D_MODEL // NUM_HEADS
        B, S, D = x.shape
        H, Hd = (NUM_HEADS, HEAD_DIM)
        qkv = jnp.einsum('bsd,ed->bse', x, w_qkv) + b_qkv
        qkv = qkv.reshape(B, S, 3, H, Hd)
        q = jnp.transpose(qkv[:, :, 0], (0, 2, 1, 3))
        k = jnp.transpose(qkv[:, :, 1], (0, 2, 1, 3))
        v = jnp.transpose(qkv[:, :, 2], (0, 2, 1, 3))
        scores = jnp.einsum('bhqd,bhkd->bhqk', q, k) / math.sqrt(Hd)
        causal = jnp.triu(jnp.full((S, S), -jnp.inf, dtype=scores.dtype), k=1)
        scores = scores + causal[None, None]
        attn = jax.nn.softmax(scores, axis=-1)
        out = jnp.einsum('bhqk,bhkd->bhqd', attn, v)
        out = jnp.transpose(out, (0, 2, 1, 3)).reshape(B, S, D)
        return jnp.einsum('bsd,ed->bse', out, w_out) + b_out

    def _L1_xattn_ref(X1, X2, QW, Qb, KW, Kb, VW, Vb):
        import jax, jax.numpy as jnp
        import numpy as np
        N, D, L = (8, 128, 256)
        q = jnp.einsum('ndl,ed->nle', X1, QW) + Qb
        k = jnp.einsum('ndl,ed->nle', X2, KW) + Kb
        v = jnp.einsum('ndl,ed->nle', X2, VW) + Vb
        scores = jnp.einsum('nqd,nkd->nqk', q, k)
        attn = jax.nn.softmax(scores, axis=-1)
        H = jnp.einsum('nqk,nkd->nqd', attn, v)
        return jnp.swapaxes(H, -1, -2)

    def _L1_ffn_ref(x, w_gate, w_up, w_down):
        import jax, jax.numpy as jnp
        import numpy as np
        DIM_IN = 256
        DIM_HIDDEN = 1024
        gate = jnp.einsum('bsd,hd->bsh', x, w_gate)
        up = jnp.einsum('bsd,hd->bsh', x, w_up)
        gated = jax.nn.silu(gate) * up
        return jnp.einsum('bsh,dh->bsd', gated, w_down)
    x = x + _L0_attn_ref(_layernorm(x, axis=-1), L0_attn_Wq, L0_attn_Wk, L0_attn_Wv, L0_attn_Wo, L0_attn_betas)
    x = x + _L0_xattn_ref(ctx_2048, ctx_2048, _layernorm(x, axis=-1), L0_xattn_ssm_kernel, L0_xattn_D, 8)
    x = x + _L0_ffn_ref(_layernorm(x, axis=-1), L0_ffn_wg, L0_ffn_fc1_w, L0_ffn_fc1_b, L0_ffn_fc2_w, L0_ffn_fc2_b)
    x = x + _L1_attn_ref(_layernorm(x, axis=-1), L1_attn_w_qkv, L1_attn_b_qkv, L1_attn_w_out, L1_attn_b_out)
    x = x + _L1_xattn_ref(_layernorm(x, axis=-1), ctx_2048, L1_xattn_QW, L1_xattn_Qb, L1_xattn_KW, L1_xattn_Kb, L1_xattn_VW, L1_xattn_Vb)
    x = x + _L1_ffn_ref(_layernorm(x, axis=-1), L1_ffn_w_gate, L1_ffn_w_up, L1_ffn_w_down)
    return x

_drawn_inputs = setup_inputs


def setup_inputs(seed=0):
    import zlib

    import numpy as np

    out = dict(_drawn_inputs(seed))
    spreads = {'L0_ffn_fc1_b': (0.0, 0.8),
     'L0_ffn_fc2_b': (0.0, 0.8),
     'L1_xattn_Qb': (0.0, 2.0),
     'L1_xattn_Kb': (0.0, 2.0),
     'L1_xattn_Vb': (0.0, 2.0)}
    factors = {'L0_attn_Wq': 8.0,
     'L0_attn_Wk': 8.0,
     'L0_attn_betas': 2.744,
     'L0_ffn_wg': 8.0,
     'L0_ffn_fc1_w': 8.0,
     'L0_ffn_fc2_w': 8.0,
     'L1_attn_w_qkv': 5.412,
     'L1_attn_b_qkv': 8.0,
     'L1_attn_w_out': 5.297,
     'L1_attn_b_out': 200.0,
     'L1_ffn_w_gate': 8.0,
     'L1_ffn_w_up': 8.0,
     'L1_ffn_w_down': 8.0}
    for name, (base, spread) in spreads.items():
        noise = np.random.default_rng([zlib.crc32(name.encode()), seed]).standard_normal(out[name].shape)
        drawn = base * np.exp(spread * noise) if base else spread * noise
        out[name] = jnp.asarray(drawn.astype(out[name].dtype))
    for name, factor in factors.items():
        out[name] = (out[name] * factor).astype(out[name].dtype)
    return out
```

```python
from contextlib import ExitStack

import concourse.bass as bass
from concourse import mybir

F32 = mybir.dt.float32
I32 = mybir.dt.int32
U32 = mybir.dt.uint32
ALU = mybir.AluOpType
ACT = mybir.ActivationFunctionType
AX = mybir.AxisListType

P = 128
B = 8
S = 128
D = 256
KC = D // P
T = B * S
EPS = 1e-5
NEG = -3.0e38

H0 = 16
DK = 128
SEG = 64
NJ = 16
HC = 16
HD = S // HC
E0 = 8
TOPK = 2
CAP = TOPK * T // E0
HID = 4 * D
MC = HID // P
BIG = 1 << 20
H1 = 16
HD1 = D // H1


class Core:
    pass


def bcast(ap, axis, n):
    shape = list(ap.shape)
    return ap.unsqueeze(axis).broadcast_to(shape[:axis] + [n] + shape[axis:])


def sb(nc, stack, name, shape, dt=F32):
    return stack.enter_context(nc.sbuf_tensor(name, shape, dt))


def sems(nc, stack, prefix, names):
    made = {n: stack.enter_context(nc.semaphore(prefix + n)) for n in names.split()}
    stack.callback(clear, nc, [x.num for x in made.values()])
    return made


def sem_row(nc, stack, prefix, n):
    made = [stack.enter_context(nc.semaphore(f"{prefix}{i}")) for i in range(n)]
    stack.callback(clear, nc, [x.num for x in made])
    return made


def clear(nc, nums):
    with nc.Block() as block:
        @block.sync
        def _(sp):
            sp.sem_clear(range(min(nums), max(nums) + 1))


def setup(nc, c, s):
    with nc.Block() as block:
        @block.sync
        def _(sp):
            sp.dma_start(c.X[:, :, :], c.x.rearrange("b p d -> p b d")).then_inc(s["x_loaded"], 16)
            sp.dma_start(c.CTX[:, :, :], c.ctx.rearrange("b p d -> p b d")).then_inc(s["ctx_loaded"], 16)
            sp.wait_ge(s["zeros_ready"], 1)
            for e in range(E0):
                sp.dma_start(c.disp[e * CAP:(e + 1) * CAP, :].rearrange("(t p) d -> p t d", p=P),
                             c.ZERO[:, :].rearrange("p (t d) -> p t d", t=CAP // P)).then_inc(s["disp_zeroed"], 16)

        @block.gpsimd
        def _(pool):
            pool.memset(c.IDN[:, :], 0.0).then_inc(s["const"], 1)
            pool.memset(c.MASK0[:, :], 0.0).then_inc(s["const"], 1)
            pool.memset(c.ZERO[:, :], 0.0).then_inc(s["zeros_ready"], 1)
            pool.wait_ge(s["const"], 2)
            pool.affine_select(out=c.IDN[:, :], in_=c.IDN[:, :], compare_op=ALU.not_equal, fill=1.0,
                               base=0, pattern=[[-1, P]], channel_multiplier=1).then_inc(s["const"], 1)
            for g in range(2):
                half = c.MASK0[g * SEG:(g + 1) * SEG, :]
                pool.wait_ge(s["const"], 3 + g)
                pool.affine_select(out=half, in_=half, compare_op=ALU.is_ge, fill=NEG, base=0,
                                   pattern=[[-1, SEG]], channel_multiplier=1).then_inc(s["const"], 1)


def layernorm(nc, c, pre, turned=True):
    with ExitStack() as st:
        s = sems(nc, st, pre, "stats aggr veps root rstd xn turned evac")
        stats = sb(nc, st, pre + "stats", [P, B, 6])
        mv = sb(nc, st, pre + "mv", [P, B, 2])
        rstd = sb(nc, st, pre + "rstd", [P, B])
        with nc.Block() as block:
            @block.vector
            def _(dve):
                dve.wait_ge(c.s["x_loaded"], 16)
                for b in range(B):
                    dve.bn_stats(stats[:, b, :], c.X[:, b, :]).then_inc(s["stats"], 1)
                for b in range(B):
                    dve.wait_ge(s["stats"], b + 1)
                    dve.bn_aggr(mv[:, b, :], stats[:, b, :]).then_inc(s["aggr"], 1)
                dve.wait_ge(s["aggr"], B)
                dve.tensor_scalar(rstd[:, :], mv[:, :, 1], EPS, None, ALU.add).then_inc(s["veps"], 1)
                dve.wait_ge(s["root"], 1)
                dve.reciprocal(rstd[:, :], rstd[:, :]).then_inc(s["rstd"], 1)
                dve.wait_ge(s["rstd"], 1)
                for b in range(B):
                    dve.tensor_scalar(c.XN[:, b, :], c.X[:, b, :], mv[:, b, 0:1], rstd[:, b:b + 1],
                                      ALU.subtract, ALU.mult).then_inc(s["xn"], 1)
                if turned:
                    for g in range(1, 4, 2):
                        dve.wait_ge(s["turned"], g + 1)
                        dve.tensor_copy(c.XNT[:, :, 2 * g * S:(2 * g + 2) * S],
                                        c.bank[g][:, :].rearrange("p (k t) -> p k t", k=KC)).then_inc(s["evac"], 1)

            @block.scalar
            def _(act):
                act.wait_ge(s["veps"], 1)
                act.activation(rstd[:, :], rstd[:, :], ACT.Sqrt).then_inc(s["root"], 1)
                if turned:
                    for g in range(0, 4, 2):
                        act.wait_ge(s["turned"], g + 1)
                        act.activation(c.XNT[:, :, 2 * g * S:(2 * g + 2) * S],
                                       c.bank[g][:, :].rearrange("p (k t) -> p k t", k=KC), ACT.Copy).then_inc(s["evac"], 1)

            if turned:
                @block.tensor
                def _(pe):
                    pe.wait_ge(c.s["const"], 3)
                    for g in range(4):
                        pe.wait_ge(s["xn"], 2 * g + 2)
                        for i in range(2):
                            for k in range(KC):
                                last = pe.transpose(c.bank[g][:, (2 * k + i) * S:(2 * k + i + 1) * S],
                                                    c.XN[:, 2 * g + i, k * P:(k + 1) * P], c.IDN[:, :])
                        last.then_inc(s["turned"], 1)


def infini_attention(nc, c):
    with ExitStack() as st:
        s = sems(nc, st, "ia_", "wqkv_ld0 wqkv_ld1 wo_ld beta_ld beta_e beta_1 beta_s beta_c const pj_done qk_ev v_ev "
                 "neg_done exp_done sig_done s_done s_free masked maxed shifted exped summed rsum "
                 "ad_done den rden p_pool p_mem p_free pt_done pts0 pts1 pv_done att_ev out_done x_add")
        WQ = [sb(nc, st, f"ia_wqkv{p}", [P, 3, KC, DK]) for p in range(2)]
        WO = sb(nc, st, "ia_wo", [P, H0, D])
        BTM = sb(nc, st, "ia_btm", [P, H0, DK])
        BTC = sb(nc, st, "ia_btc", [P, H0, DK])
        QT = sb(nc, st, "ia_qt", [P, B, S])
        KT = sb(nc, st, "ia_kt", [P, B, S])
        EQ = sb(nc, st, "ia_eq", [P, 2, B, SEG])
        SQ = sb(nc, st, "ia_sq", [P, B, SEG])
        SK = sb(nc, st, "ia_sk", [P, B, SEG + 1])
        SM = sb(nc, st, "ia_sm", [P, B, SEG])
        EX = sb(nc, st, "ia_ex", [P, B, SEG])
        MX = sb(nc, st, "ia_mx", [P, B])
        RS = sb(nc, st, "ia_rs", [P, B])
        RD = sb(nc, st, "ia_rd", [P, B])
        PR = sb(nc, st, "ia_pr", [P, B, S])
        PTS = sb(nc, st, "ia_pts", [P, B, S])
        VX = [sb(nc, st, f"ia_vx{p}", [P, B, DK]) for p in range(2)]
        VD = [sb(nc, st, f"ia_vd{p}", [SEG, B, DK]) for p in range(2)]
        ATT = sb(nc, st, "ia_att", [P, NJ, B, S])
        SC = c.bank[0]
        AD = [c.bank[1], c.bank[2]]
        PJ = [c.bank[3], c.bank[4], c.bank[5]]
        OB = [c.bank[6], c.bank[7]]
        scale = float(DK) ** -0.5
        HB = B // 2
        wsrc = [w.rearrange("(k p) (h n) -> h p k n", p=P, n=DK) for w in (c.Wq, c.Wk, c.Wv)]

        with nc.Block() as block:
            @block.sync
            def _(sp):
                def load_qkv(h, p):
                    for i in range(3):
                        src = wsrc[i][h] if isinstance(h, int) else wsrc[i][bass.ds(h, 1)].squeeze(0)
                        sp.dma_start(WQ[p][:, i, :, :], src).then_inc((s["wqkv_ld0"], s["wqkv_ld1"])[p], 16)

                for p in range(2):
                    load_qkv(p, p)
                sp.dma_start(BTC[:, :, :].rearrange("p h n -> p (h n)"),
                             c.betas.rearrange("a h b n -> (a b) (h n)").broadcast_to([P, H0 * DK])).then_inc(s["beta_ld"], 16)
                sp.dma_start(WO[:, :, :], c.Wo.rearrange("(h p) n -> p h n", p=DK)).then_inc(s["wo_ld"], 16)
                with sp.Fori(1, H0 // 2) as j:
                    for p in range(2):
                        sp.wait_ge(s["pj_done"], 12 * j + 6 * p - 6)
                        load_qkv(2 * j + p, p)

            @block.gpsimd
            def _(pool):
                pool.memset(PR[:, :, :], 0.0).then_inc(s["const"], 1)
                pool.memset(SK[:, :, SEG:SEG + 1], 1.0 / DK).then_inc(s["const"], 1)
                pool.wait_ge(s["const"], 2)

                def head(h):
                    pool.wait_ge(s["maxed"], h + 1)
                    pool.tensor_tensor(SM[:, :, :], SM[:, :, :], bcast(MX[:, :], 2, SEG), ALU.subtract).then_inc(s["shifted"], 1)
                    pool.wait_ge(s["rsum"], h + 1)
                    pool.wait_ge(s["p_free"], h + 1)
                    pool.tensor_tensor(PR[0:SEG, :, 0:SEG], EX[0:SEG, :, :], bcast(RS[0:SEG, :], 2, SEG), ALU.mult).then_inc(s["p_pool"], 1)
                    pool.wait_ge(s["p_pool"], 2 * h + 1)
                    pool.tensor_tensor(PR[SEG:P, :, SEG:S], EX[SEG:P, :, :], bcast(RS[SEG:P, :], 2, SEG), ALU.mult).then_inc(s["p_pool"], 1)
                    pool.wait_ge(s["p_pool"], 2 * h + 2)

                with pool.Fori(0, H0 // 2 - 1) as j:
                    head(2 * j)
                    head(2 * j + 1)
                head(H0 - 2)
                head(H0 - 1)

            @block.scalar
            def _(act):
                act.wait_ge(s["beta_ld"], 16)
                act.activation(BTM[:, :, :], BTC[:, :, :], ACT.Exp, scale=-1.0).then_inc(s["beta_e"], 1)

                def evac_qk(h):
                    for t in range(4):
                        act.wait_ge(s["pj_done"], 6 * h + t + 1)
                        dst = (QT, KT)[t // 2][:, (t % 2) * HB:(t % 2 + 1) * HB, :]
                        act.activation(dst, PJ[t % 3][:, :].rearrange("p (b t) -> p b t", b=HB), ACT.Copy).then_inc(s["qk_ev"], 1)

                def sigma_exp(h):
                    act.wait_ge(s["qk_ev"], 4 * h + 4)
                    act.activation(EQ[:, 0, :, :], QT[:, :, SEG:S], ACT.Relu, scale=-1.0).then_inc(s["neg_done"], 1)
                    act.activation(EQ[:, 1, :, :], KT[:, :, 0:SEG], ACT.Relu, scale=-1.0).then_inc(s["neg_done"], 1)
                    act.wait_ge(s["neg_done"], 2 * h + 2)
                    act.activation(EQ[:, :, :, :], EQ[:, :, :, :], ACT.Exp, scale=-1.0).then_inc(s["exp_done"], 1)

                def head(h, p, nxt=True):
                    act.wait_ge(s["shifted"], h + 1)
                    act.activation(EX[:, :, :], SM[:, :, :], ACT.Exp).then_inc(s["exped"], 1)
                    if nxt:
                        evac_qk(h + 1)
                    act.wait_ge(s["pt_done"], 2 * h + 1)
                    act.activation(PTS[:, 0:HB, :], AD[0][:, :].rearrange("p (b t) -> p b t", b=HB), ACT.Copy).then_inc(s["pts0"], 1)
                    if nxt:
                        sigma_exp(h + 1)
                    for g in range(2):
                        act.wait_ge(s["pv_done"], 2 * h + g + 1)
                        src = OB[g][:, :].rearrange("p (b i m j) -> p b i m j", b=HB, i=2, j=NJ)
                        for i in range(2):
                            at = 4 * h + i * SEG
                            rows = slice(at, at + 4) if isinstance(h, int) else bass.ds(at, 4)
                            act.activation(ATT[:, :, g * HB:(g + 1) * HB, rows].rearrange("p j b m -> p b m j"),
                                           src[:, :, i, :, :], ACT.Copy).then_inc(s["att_ev"], 1)

                act.sem_inc(s["att_ev"], 4)
                act.sem_inc(s["pts0"], 1)
                evac_qk(0)
                sigma_exp(0)
                with act.Fori(0, H0 // 2 - 1) as j:
                    head(2 * j, 0)
                    head(2 * j + 1, 1)
                head(H0 - 2, 0)
                head(H0 - 1, 1, False)

            @block.tensor
            def _(pe):
                def project_qk(h, p, n, first=False):
                    pe.wait_ge((s["wqkv_ld0"], s["wqkv_ld1"])[p], 48 * n)
                    for t in range(4):
                        if t == 0 and not first:
                            pe.wait_ge(s["qk_ev"], 4 * h)
                        if t in (1, 2) and not first:
                            pe.wait_ge(s["v_ev"], 4 * h - 4 + 2 * t)
                        if t == 3:
                            pe.wait_ge(s["qk_ev"], 4 * h + 1)
                        for k in range(KC):
                            mm = pe.matmul(PJ[t % 3][:, :], WQ[p][:, t // 2, k, :],
                                           c.XNT[:, k, (t % 2) * HB * S:(t % 2 + 1) * HB * S], start=(k == 0), stop=(k == KC - 1))
                        mm.then_inc(s["pj_done"], 1)

                def project_v(h, p):
                    for t in range(4, 6):
                        pe.wait_ge(s["qk_ev"], 4 * h + t - 2)
                        for i in range(HB):
                            b = (t - 4) * HB + i
                            for k in range(KC):
                                mm = pe.matmul(PJ[t % 3][:, i * DK:(i + 1) * DK], c.XNT[:, k, b * S:(b + 1) * S],
                                               WQ[p][:, 2, k, :], start=(k == 0), stop=(k == KC - 1))
                        mm.then_inc(s["pj_done"], 1)

                def head(h, p, n, nxt=True):
                    pe.wait_ge(s["qk_ev"], 4 * h + 4)
                    pe.wait_ge(s["s_free"], h + 1)
                    for b in range(B):
                        for g in range(2):
                            r = slice(g * SEG, (g + 1) * SEG)
                            mm = pe.matmul(SC[r, b * SEG:(b + 1) * SEG], QT[:, b, r], KT[:, b, r], start=True, stop=True)
                    mm.then_inc(s["s_done"], 1)
                    pe.wait_ge(s["sig_done"], 2 * h + 2)
                    pe.wait_ge(s["pts0"], h + 1)
                    pe.wait_ge(s["pts1"], h + 1)
                    for b in range(B):
                        mm = pe.matmul(AD[b // HB][SEG:P, (b % HB) * (SEG + 1):(b % HB + 1) * (SEG + 1)],
                                       SQ[:, b, :], SK[:, b, :], start=True, stop=True)
                    mm.then_inc(s["ad_done"], 1)
                    if nxt:
                        project_qk(h + 1, 1 - p, n)
                    pe.wait_ge(s["p_pool"], 2 * h + 2)
                    pe.wait_ge(s["p_mem"], 2 * h + 2)
                    for g in range(2):
                        for i in range(HB):
                            mm = pe.transpose(AD[g][:, i * S:(i + 1) * S], PR[:, g * HB + i, :], c.IDN[:, :])
                        mm.then_inc(s["pt_done"], 1)
                    pe.drain().then_inc(s["p_free"], 1)
                    if nxt:
                        project_v(h + 1, 1 - p)
                    pe.wait_ge(s["v_ev"], 4 * h + 4)
                    for g in range(2):
                        pe.wait_ge(s["pts0" if g == 0 else "pts1"], h + 2)
                        pe.wait_ge(s["att_ev"], 4 * h + 2 + 2 * g)
                        for i in range(HB):
                            b = g * HB + i
                            pe.matmul(OB[g][:, i * S:i * S + SEG], VD[p][:, b, :], PTS[0:SEG, b, 0:SEG], start=True, stop=True)
                            mm = pe.matmul(OB[g][:, i * S + SEG:(i + 1) * S], VX[p][:, b, :], PTS[:, b, SEG:S], start=True, stop=True)
                        mm.then_inc(s["pv_done"], 1)

                def project_out():
                    pe.wait_ge(s["wo_ld"], 16)
                    pe.wait_ge(s["att_ev"], 4 * H0 + 4)
                    for q in range(B // 2):
                        if q >= 2:
                            pe.wait_ge(s["x_add"], q - 1)
                        for i in range(2):
                            for j in range(NJ):
                                mm = pe.matmul(OB[q % 2][:, i * D:(i + 1) * D], ATT[:, j, 2 * q + i, :], WO[:, j, :],
                                               start=(j == 0), stop=(j == NJ - 1))
                        mm.then_inc(s["out_done"], 1)

                pe.sem_inc(s["p_free"], 1)
                pe.wait_ge(s["const"], 2)
                project_qk(0, 0, 1, True)
                project_v(0, 0)
                with pe.Fori(0, H0 // 2 - 1) as j:
                    head(2 * j, 0, j + 1)
                    head(2 * j + 1, 1, j + 2)
                head(H0 - 2, 0, H0 // 2)
                head(H0 - 1, 1, 0, False)
                project_out()

            @block.vector
            def _(dve):
                dve.wait_ge(s["beta_e"], 1)
                dve.tensor_scalar(BTM[:, :, :], BTM[:, :, :], 1.0, None, ALU.add).then_inc(s["beta_1"], 1)
                dve.wait_ge(s["beta_1"], 1)
                dve.reciprocal(BTM[:, :, :], BTM[:, :, :]).then_inc(s["beta_s"], 1)
                dve.wait_ge(s["beta_s"], 1)
                dve.tensor_scalar(BTC[:, :, :], BTM[:, :, :], -1.0, 1.0, ALU.mult, ALU.add).then_inc(s["beta_c"], 1)
                dve.wait_ge(s["beta_c"], 1)
                dve.tensor_copy(BTM[SEG:P, :, :], BTC[SEG:P, :, :]).then_inc(s["beta_c"], 1)
                dve.wait_ge(s["beta_c"], 2)

                def sigma(h):
                    dve.wait_ge(s["exp_done"], h + 1)
                    dve.scalar_tensor_tensor(SQ[:, :, :], QT[:, :, SEG:S], 0.0, EQ[:, 0, :, :], ALU.max, ALU.add).then_inc(s["sig_done"], 1)
                    dve.scalar_tensor_tensor(SK[:, :, 0:SEG], KT[:, :, 0:SEG], 0.0, EQ[:, 1, :, :], ALU.max, ALU.add).then_inc(s["sig_done"], 1)

                def evac_v(h, p):
                    for t in range(4, 6):
                        dve.wait_ge(s["pj_done"], 6 * h + t + 1)
                        b = slice((t - 4) * HB, (t - 3) * HB)
                        src = PJ[t % 3][:, :].rearrange("p (b n) -> p b n", b=HB)
                        if isinstance(h, int):
                            bm, bc = BTM[:, h, :], BTC[0:SEG, h, :]
                        else:
                            bm, bc = BTM[:, bass.ds(h, 1), :].squeeze(1), BTC[0:SEG, bass.ds(h, 1), :].squeeze(1)
                        dve.tensor_tensor(VX[p][:, b, :], src, bcast(bm, 1, HB), ALU.mult).then_inc(s["v_ev"], 1)
                        dve.tensor_tensor(VD[p][:, b, :], src[0:SEG], bcast(bc, 1, HB), ALU.mult).then_inc(s["v_ev"], 1)

                def head(h, p, nxt=True):
                    dve.wait_ge(s["s_done"], h + 1)
                    dve.scalar_tensor_tensor(SM[:, :, :], SC[:, :].rearrange("p (b k) -> p b k", b=B), scale,
                                             bcast(c.MASK0[:, :], 1, B), ALU.mult, ALU.add).then_inc(s["masked"], 1)
                    dve.wait_ge(s["masked"], h + 1)
                    dve.tensor_reduce(MX[:, :], SM[:, :, :], AX.X, ALU.max).then_inc(s["maxed"], 1)
                    dve.sem_inc(s["s_free"], 1)
                    dve.wait_ge(s["ad_done"], h + 1)
                    lin = [AD[g][SEG:P, 0:HB * (SEG + 1)].rearrange("p (b k) -> p b k", b=HB) for g in range(2)]
                    for g in range(2):
                        dve.tensor_reduce(RD[SEG:P, g * HB:(g + 1) * HB], lin[g], AX.X, ALU.add).then_inc(s["den"], 1)
                    dve.wait_ge(s["den"], 2 * h + 2)
                    dve.reciprocal(RD[SEG:P, :], RD[SEG:P, :]).then_inc(s["rden"], 1)
                    dve.wait_ge(s["rden"], h + 1)
                    dve.wait_ge(s["p_free"], h + 1)
                    for g in range(2):
                        dve.tensor_tensor(PR[SEG:P, g * HB:(g + 1) * HB, 0:SEG], lin[g][:, :, 0:SEG],
                                          bcast(RD[SEG:P, g * HB:(g + 1) * HB], 2, SEG), ALU.mult).then_inc(s["p_mem"], 1)
                    dve.wait_ge(s["exped"], h + 1)
                    dve.tensor_reduce(RS[:, :], EX[:, :, :], AX.X, ALU.add).then_inc(s["summed"], 1)
                    dve.wait_ge(s["summed"], h + 1)
                    dve.reciprocal(RS[:, :], RS[:, :]).then_inc(s["rsum"], 1)
                    dve.wait_ge(s["pt_done"], 2 * h + 2)
                    dve.tensor_copy(PTS[:, HB:B, :], AD[1][:, :].rearrange("p (b t) -> p b t", b=HB)).then_inc(s["pts1"], 1)
                    if nxt:
                        sigma(h + 1)
                        evac_v(h + 1, 1 - p)

                def add_out():
                    for q in range(B // 2):
                        dve.wait_ge(s["out_done"], q + 1)
                        xs = c.X[:, 2 * q:2 * q + 2, :]
                        dve.tensor_tensor(xs, xs, OB[q % 2][:, :].rearrange("p (b n) -> p b n", b=2), ALU.add).then_inc(s["x_add"], 1)

                dve.sem_inc(s["s_free"], 1)
                dve.sem_inc(s["pts1"], 1)
                dve.wait_ge(s["const"], 2)
                sigma(0)
                evac_v(0, 0)
                with dve.Fori(0, H0 // 2 - 1) as j:
                    head(2 * j, 0)
                    head(2 * j + 1, 1)
                head(H0 - 2, 0)
                head(H0 - 1, 1, False)
                add_out()


def long_conv(nc, c):
    with ExitStack() as st:
        s = sems(nc, st, "lc_", "pad_st toe_ld d_ld anti rev turned_c cr_ev toe0 toe1 kv y0 y1 prod red turned_o")
        TOE = sb(nc, st, "lc_toe", [P, HC, D])
        TB = [sb(nc, st, f"lc_tb{p}", [P, D]) for p in range(2)]
        DB = sb(nc, st, "lc_d", [P, HC])
        ANTI = sb(nc, st, "lc_anti", [P, P])
        CR = sb(nc, st, "lc_cr", [P, KC, B, S])
        CREV = sb(nc, st, "lc_crev", [P, B, D])
        KV = [sb(nc, st, f"lc_kv{p}", [P, KC, B, HD, HD]) for p in range(2)]
        PD = sb(nc, st, "lc_pd", [P, KC, B, HD * HD])
        OT = sb(nc, st, "lc_ot", [P, KC, B, S])
        with nc.Block() as block:
            @block.sync
            def _(sp):
                sp.dma_start(c.pad[:, 0:P - 1], c.ZERO[0:HC, 0:P - 1]).then_inc(s["pad_st"], 16)
                sp.dma_start(c.pad[:, P - 1:P - 1 + D], c.ssm).then_inc(s["pad_st"], 16)
                sp.dma_start(DB[:, :], c.convD.rearrange("(a h) -> a h", a=1).broadcast_to([P, HC])).then_inc(s["d_ld"], 16)
                sp.wait_ge(s["pad_st"], 32)
                sp.dma_start(TOE[:, :, :], bass.AP(tensor=c.pad.tensor, offset=0, ap=[[1, P], [384, HC], [1, D]])).then_inc(s["toe_ld"], 16)

            @block.gpsimd
            def _(pool):
                pool.memset(ANTI[:, :], 0.0).then_inc(s["anti"], 1)
                pool.wait_ge(s["anti"], 1)
                pool.affine_select(out=ANTI[:, :], in_=ANTI[:, :], compare_op=ALU.not_equal, fill=1.0,
                                   base=1 - P, pattern=[[1, P]], channel_multiplier=1).then_inc(s["anti"], 1)
                pool.wait_ge(s["cr_ev"], 8)

                pool.sem_inc(s["y1"], 2)
                with pool.Fori(0, HC // 2) as j:
                    for p in range(2):
                        h = 2 * j + p
                        pool.wait_ge(s["y1"], h + 1)
                        for k in range(KC):
                            pool.wait_ge(s["cr_ev"], 8)
                            v = CR[:, k, :, bass.ds(HD * h, HD)]
                            pool.tensor_tensor(KV[p][:, k, :, :, :], bcast(v, 3, HD), bcast(v, 2, HD), ALU.mult).then_inc(s["kv"], 1)

            @block.scalar
            def _(act):
                for g in range(0, 4):
                    act.wait_ge(s["turned_c"], g + 1)
                    act.activation(CR[:, :, 2 * g:2 * g + 2, :], c.bank[g][:, :].rearrange("p (k b t) -> p k b t", k=KC, b=2), ACT.Copy).then_inc(s["cr_ev"], 2)
                act.wait_ge(s["toe_ld"], 16)
                with act.Fori(0, HC // 2) as j:
                    for p in range(2):
                        act.wait_ge(s["y1"], 2 * j + p + 1)
                        act.activation(TB[p][:, P:D], TOE[:, bass.ds(2 * j + p, 1), P:D].squeeze(1), ACT.Copy).then_inc(s["toe1"], 1)

            @block.tensor
            def _(pe):
                for g in range(4):
                    pe.wait_ge(s["rev"], 2 * g + 2)
                    for i in range(2):
                        for k in range(KC):
                            mm = pe.transpose(c.bank[g][:, (2 * k + i) * S:(2 * k + i + 1) * S],
                                              CREV[:, 2 * g + i, k * P:(k + 1) * P], c.IDN[:, :])
                    mm.then_inc(s["turned_c"], 1)
                pe.wait_ge(s["cr_ev"], 8)
                with pe.Fori(0, HC // 2) as j:
                    for p in range(2):
                        h = 2 * j + p
                        y = [c.bank[2 * p], c.bank[2 * p + 1]]
                        kv = [KV[p][:, k, :, :, :].rearrange("p b j i -> p (b j i)") for k in range(KC)]
                        pe.wait_ge(s["kv"], 2 * h + 2)
                        pe.wait_ge(s["toe0"], h + 1)
                        pe.wait_ge(s["toe1"], h + 1)
                        pe.wait_ge(s["prod"], 2 * h + 1)
                        pe.matmul(y[0][:, :], TB[p][:, 0:P], kv[0], start=True, stop=True).then_inc(s["y0"], 1)
                        pe.wait_ge(s["prod"], 2 * h + 2)
                        pe.matmul(y[1][:, :], TB[p][:, P:D], kv[0], start=True, stop=False)
                        pe.matmul(y[1][:, :], TB[p][:, 0:P], kv[1], start=False, stop=True).then_inc(s["y1"], 1)
                pe.wait_ge(s["red"], 2 * HC)
                for q in range(B // 2):
                    for i in range(2):
                        for k in range(KC):
                            mm = pe.transpose(c.bank[4 + q][:, i * D + k * P:i * D + (k + 1) * P], OT[:, k, 2 * q + i, :], c.IDN[:, :])
                    mm.then_inc(s["turned_o"], 1)

            @block.vector
            def _(dve):
                dve.wait_ge(c.s["ctx_loaded"], 16)
                for b in range(B):
                    src = c.CTX[:, b, :].rearrange("p (k t) -> p k t", k=KC)[:, :, ::-1]
                    dve.tensor_copy(CREV[:, b, :].rearrange("p (k t) -> p k t", k=KC), src).then_inc(s["rev"], 1)
                dve.wait_ge(s["anti"], 2)
                dve.wait_ge(s["toe_ld"], 16)
                dve.wait_ge(s["d_ld"], 16)
                dve.sem_inc(s["prod"], 4)

                def toeplitz(h, p):
                    dve.wait_ge(s["y1"], h + 1)
                    dve.scalar_tensor_tensor(TB[p][:, 0:P], ANTI[:, :], DB[:, bass.ds(h, 1)], TOE[:, bass.ds(h, 1), 0:P].squeeze(1),
                                             ALU.mult, ALU.add).then_inc(s["toe0"], 1)

                q = c.XNT[:, :, :].rearrange("p k (b t) -> p k b t", b=B)
                with dve.Fori(0, HC // 2) as j:
                    for p in range(2):
                        toeplitz(2 * j + p, p)
                    for p in range(2):
                        h = 2 * j + p
                        for k in range(KC):
                            dve.wait_ge((s["y0"], s["y1"])[k], h + 1 + 2 * k)
                            pd = PD[:, k, :, :].rearrange("p b (j i) -> p b j i", j=HD)
                            dve.tensor_tensor(pd, c.bank[2 * p + k][:, :].rearrange("p (b j i) -> p b j i", b=B, j=HD),
                                              bcast(q[:, k, :, bass.ds(HD * h, HD)], 2, HD), ALU.mult).then_inc(s["prod"], 1)
                            dve.wait_ge(s["prod"], 2 * h + k + 5)
                            dve.tensor_reduce(OT[:, k, :, bass.ds(HD * h, HD)], pd, AX.X, ALU.add).then_inc(s["red"], 1)
                for g in range(B // 2):
                    dve.wait_ge(s["turned_o"], g + 1)
                    xs = c.X[:, 2 * g:2 * g + 2, :]
                    dve.tensor_tensor(xs, xs, c.bank[4 + g][:, :].rearrange("p (b n) -> p b n", b=2), ALU.add)


def moe(nc, c):
    NB = TOPK * B
    with ExitStack() as st:
        G = sb(nc, st, "mo_gate", [P, TOPK, B])
        GIX = sb(nc, st, "mo_gix", [P, TOPK, B], I32)
        w = sems(nc, st, "mw_", "f1 f2 bias0 bias1 ld0 ld1")
        F1 = [sb(nc, st, f"mo_f1{p}", [P, KC, HID]) for p in range(2)]
        F2 = [sb(nc, st, f"mo_f2{p}", [P, MC, D]) for p in range(2)]
        B1 = sb(nc, st, "mo_b1", [P, E0 * MC])
        B2 = [sb(nc, st, f"mo_b2{p}", [P, D]) for p in range(2)]
        fc1 = c.fc1.rearrange("e (k p) n -> e p k n", p=P)
        fc2 = c.fc2.rearrange("e (m p) n -> e p m n", p=P)

        def load_expert(sp, e, p):
            pick = (lambda a: a[e]) if isinstance(e, int) else (lambda a: a[bass.ds(e, 1)].squeeze(0))
            sp.dma_start(F1[p][:, :, :], pick(fc1)).then_inc((w["ld0"], w["ld1"])[p], 16)
            sp.dma_start(F2[p][:, :, :], pick(fc2)).then_inc((w["ld0"], w["ld1"])[p], 16)
            row = c.fc2b[e:e + 1, :] if isinstance(e, int) else c.fc2b[bass.ds(e, 1), :]
            sp.dma_start(B2[p][:, :], row.broadcast_to([P, D])).then_inc((w["ld0"], w["ld1"])[p], 16)

        route(nc, c, B1, G, GIX, lambda sp: [load_expert(sp, p, p) for p in range(2)])
        experts(nc, c, F1, F2, B1, B2, w, load_expert)
        combine(nc, c, G, GIX)


def route(nc, c, B1, G, GIX, first_loads):
    NB = TOPK * B
    with ExitStack() as st:
        s = sems(nc, st, "mr_", "b1_ld b1_t wg_ld const logits lg maxed shifted exped summed rsum prob top idx idxf onehot "
                 "gsum gsafe grec gate0 counted tot scan base pos0 pos1 pos valid slot0 slot1 big pv0 pv1 ready scattered")
        WG = sb(nc, st, "mr_wg", [P, KC, E0])
        B1R = sb(nc, st, "mr_b1r", [E0 * MC, P])
        TRI = sb(nc, st, "mr_tri", [P, P])
        ONES = sb(nc, st, "mr_ones", [P, P])
        IOTA = sb(nc, st, "mr_iota", [P, E0])
        RST = sb(nc, st, "mr_rst", [P, E0, NB])
        PRB = sb(nc, st, "mr_prb", [P, B, E0])
        MX = sb(nc, st, "mr_mx", [P, B])
        SU = sb(nc, st, "mr_su", [P, B])
        V8 = sb(nc, st, "mr_v8", [P, B, 8])
        I8 = sb(nc, st, "mr_i8", [P, B, 8], U32)
        EID = sb(nc, st, "mr_eid", [P, TOPK, B])
        OH = sb(nc, st, "mr_oh", [P, TOPK, B, E0])
        TOT = sb(nc, st, "mr_tot", [P, E0, NB])
        SCN = sb(nc, st, "mr_scn", [P, E0, NB])
        POE = sb(nc, st, "mr_poe", [P, NB, E0])
        POS = sb(nc, st, "mr_pos", [P, NB])
        VAL = sb(nc, st, "mr_val", [P, NB])
        SLT = sb(nc, st, "mr_slt", [P, NB])
        SLG = sb(nc, st, "mr_slg", [P, NB])
        SIX = sb(nc, st, "mr_six", [P, NB], I32)
        LGB, PRE, TTB = c.bank[0], c.bank[1], c.bank[2]
        with nc.Block() as block:
            @block.sync
            def _(sp):
                sp.dma_start(WG[:, :, :], c.wg.rearrange("(k p) e -> p k e", p=P)).then_inc(s["wg_ld"], 16)
                sp.dma_start(B1R[:, :], c.fc1b.rearrange("e (m p) -> (e m) p", p=P)).then_inc(s["b1_ld"], 16)
                first_loads(sp)

            @block.gpsimd
            def _(pool):
                pool.memset(TRI[:, :], 1.0).then_inc(s["const"], 1)
                pool.memset(ONES[:, :], 1.0).then_inc(s["const"], 1)
                pool.memset(RST[:, :, :], 1.0).then_inc(s["const"], 1)
                pool.iota(IOTA[:, :], [[1, E0]], base=0, channel_multiplier=0,
                          allow_small_or_imprecise_dtypes=True).then_inc(s["const"], 1)
                pool.wait_ge(s["const"], 4)
                pool.memset(RST[:, :, 0:1], 0.0).then_inc(s["const"], 1)
                pool.affine_select(out=TRI[:, :], in_=TRI[:, :], compare_op=ALU.is_gt, fill=0.0, base=0,
                                   pattern=[[1, P]], channel_multiplier=-1).then_inc(s["const"], 1)
                pool.wait_ge(s["ready"], 2)
                pool.wait_ge(c.s["disp_zeroed"], 16 * E0)
                for n in range(NB):
                    pool.indirect_dma_start(c.disp, bass.IndirectOffsetOnAxis(ap=SIX[:, n:n + 1], axis=0), c.XN[:, n % B, :], None,
                                            bounds_check=E0 * CAP - 1, oob_is_err=False).then_inc(s["scattered"], 16)
                pool.wait_ge(s["scattered"], 16 * NB)

            @block.scalar
            def _(act):
                act.wait_ge(s["shifted"], 1)
                act.activation(PRB[:, :, :], PRB[:, :, :], ACT.Exp).then_inc(s["exped"], 1)
                act.wait_ge(s["b1_t"], 1)
                act.activation(B1[:, :], c.bank[3][:, 0:E0 * MC], ACT.Copy)

            @block.tensor
            def _(pe):
                pe.wait_ge(s["wg_ld"], 16)
                for b in range(B):
                    for k in range(KC):
                        mm = pe.matmul(LGB[:, b * E0:(b + 1) * E0], c.XNT[:, k, b * S:(b + 1) * S], WG[:, k, :],
                                       start=(k == 0), stop=(k == KC - 1))
                mm.then_inc(s["logits"], 1)
                pe.wait_ge(s["b1_ld"], 16)
                pe.transpose(c.bank[3][:, 0:E0 * MC], B1R[:, :], c.IDN[0:E0 * MC, 0:E0 * MC]).then_inc(s["b1_t"], 1)
                pe.wait_ge(s["const"], 6)
                pe.wait_ge(s["onehot"], 2)
                oh = OH[:, :, :, :].rearrange("p s b e -> p (s b e)")
                pe.matmul(PRE[:, 0:NB * E0], TRI[:, :], oh, start=True, stop=True).then_inc(s["counted"], 1)
                pe.matmul(TTB[:, 0:NB * E0], ONES[:, :], oh, start=True, stop=True).then_inc(s["counted"], 1)

            @block.vector
            def _(dve):
                dve.wait_ge(s["logits"], 1)
                lg = LGB[:, 0:B * E0].rearrange("p (b e) -> p b e", b=B)
                dve.tensor_reduce(MX[:, :], lg, AX.X, ALU.max).then_inc(s["maxed"], 1)
                dve.wait_ge(s["maxed"], 1)
                dve.tensor_tensor(PRB[:, :, :], lg, bcast(MX[:, :], 2, E0), ALU.subtract).then_inc(s["shifted"], 1)
                dve.wait_ge(s["exped"], 1)
                dve.tensor_reduce(SU[:, :], PRB[:, :, :], AX.X, ALU.add).then_inc(s["summed"], 1)
                dve.wait_ge(s["summed"], 1)
                dve.reciprocal(SU[:, :], SU[:, :]).then_inc(s["rsum"], 1)
                dve.wait_ge(s["rsum"], 1)
                dve.tensor_tensor(PRB[:, :, :], PRB[:, :, :], bcast(SU[:, :], 2, E0), ALU.mult).then_inc(s["prob"], 1)
                dve.wait_ge(s["prob"], 1)
                for b in range(B):
                    dve.max(V8[:, b, :], PRB[:, b, :]).then_inc(s["top"], 1)
                for b in range(B):
                    dve.wait_ge(s["top"], b + 1)
                    dve.max_index(I8[:, b, :], V8[:, b, :], PRB[:, b, :]).then_inc(s["idx"], 1)
                dve.wait_ge(s["idx"], B)
                dve.wait_ge(s["const"], 6)
                for t in range(TOPK):
                    dve.tensor_copy(EID[:, t, :], I8[:, :, t]).then_inc(s["idxf"], 1)
                for t in range(TOPK):
                    dve.wait_ge(s["idxf"], t + 1)
                    dve.tensor_tensor(OH[:, t, :, :], bcast(IOTA[:, :], 1, B), bcast(EID[:, t, :], 2, E0), ALU.is_equal).then_inc(s["onehot"], 1)
                dve.tensor_tensor(MX[:, :], V8[:, :, 0], V8[:, :, 1], ALU.add).then_inc(s["gsum"], 1)
                dve.wait_ge(s["gsum"], 1)
                dve.tensor_scalar(MX[:, :], MX[:, :], 1e-9, None, ALU.max).then_inc(s["gsafe"], 1)
                dve.wait_ge(s["gsafe"], 1)
                dve.reciprocal(MX[:, :], MX[:, :]).then_inc(s["grec"], 1)
                dve.wait_ge(s["grec"], 1)
                for t in range(TOPK):
                    dve.tensor_tensor(G[:, t, :], V8[:, :, t], MX[:, :], ALU.mult).then_inc(s["gate0"], 1)
                dve.wait_ge(s["counted"], 2)
                tot = TTB[:, 0:NB * E0].rearrange("p (n e) -> p e n", e=E0)
                dve.tensor_copy(TOT[:, :, :], tot).then_inc(s["tot"], 1)
                dve.wait_ge(s["tot"], 1)
                flat = [a[:, :, :].rearrange("p e n -> p (e n)") for a in (SCN, RST, TOT)]
                dve.tensor_tensor_scan(flat[0], flat[1], flat[2], 0.0, ALU.mult, ALU.add).then_inc(s["scan"], 1)
                dve.wait_ge(s["scan"], 1)
                dve.tensor_tensor(SCN[:, :, :], SCN[:, :, :], TOT[:, :, :], ALU.subtract).then_inc(s["base"], 1)
                dve.wait_ge(s["base"], 1)
                dve.tensor_tensor(POE[:, :, :], PRE[:, 0:NB * E0].rearrange("p (n e) -> p n e", e=E0),
                                  SCN[:, :, :].rearrange("p e n -> p n e"), ALU.add).then_inc(s["pos0"], 1)
                dve.wait_ge(s["pos0"], 1)
                dve.tensor_tensor(POE[:, :, :], POE[:, :, :], OH[:, :, :, :].rearrange("p s b e -> p (s b) e"), ALU.mult).then_inc(s["pos1"], 1)
                dve.wait_ge(s["pos1"], 1)
                dve.tensor_reduce(POS[:, :], POE[:, :, :], AX.X, ALU.add).then_inc(s["pos"], 1)
                dve.wait_ge(s["pos"], 1)
                dve.tensor_scalar(VAL[:, :], POS[:, :], float(CAP), None, ALU.is_lt).then_inc(s["valid"], 1)
                eid = EID[:, :, :].rearrange("p s b -> p (s b)")
                dve.scalar_tensor_tensor(SLT[:, :], eid, float(CAP), POS[:, :], ALU.mult, ALU.add).then_inc(s["slot0"], 1)
                dve.wait_ge(s["valid"], 1)
                dve.tensor_tensor(SLG[:, :], POS[:, :], VAL[:, :], ALU.mult).then_inc(s["pv0"], 1)
                dve.wait_ge(s["pv0"], 1)
                dve.scalar_tensor_tensor(SLG[:, :], eid, float(CAP), SLG[:, :], ALU.mult, ALU.add).then_inc(s["pv1"], 1)
                dve.wait_ge(s["gate0"], TOPK)
                g = G[:, :, :].rearrange("p s b -> p (s b)")
                dve.tensor_tensor(g, g, VAL[:, :], ALU.mult).then_inc(s["gate0"], 1)
                dve.wait_ge(s["gate0"], TOPK + 1)
                dve.tensor_scalar(VAL[:, :], VAL[:, :], -float(BIG), float(BIG), ALU.mult, ALU.add).then_inc(s["big"], 1)
                dve.wait_ge(s["big"], 1)
                dve.wait_ge(s["slot0"], 1)
                dve.tensor_tensor(SLT[:, :], SLT[:, :], VAL[:, :], ALU.add).then_inc(s["slot1"], 1)
                dve.wait_ge(s["slot1"], 1)
                dve.tensor_copy(SIX[:, :], SLT[:, :]).then_inc(s["ready"], 1)
                dve.wait_ge(s["pv1"], 1)
                dve.tensor_copy(GIX[:, :, :].rearrange("p s b -> p (s b)"), SLG[:, :]).then_inc(s["ready"], 1)


def experts(nc, c, F1, F2, B1, B2, w, load_expert):
    CT = CAP // P
    with ExitStack() as st:
        s = sems(nc, st, "me_", "in0 in1 xt_done xt_ev h_done h_ev o_done o_ev st0 st1")
        XE = [sb(nc, st, f"me_xe{p}", [P, CT, D]) for p in range(2)]
        XET = sb(nc, st, "me_xet", [P, KC, CAP])
        HT = sb(nc, st, "me_ht", [P, MC, CAP])
        EO = [sb(nc, st, f"me_eo{p}", [P, CT, D]) for p in range(2)]
        disp = c.disp.rearrange("(e t p) d -> e p t d", p=P, t=CT)
        eo = c.eo.rearrange("(e t p) d -> e p t d", p=P, t=CT)
        XTB, OB = c.bank[0], c.bank[5]
        HB = [c.bank[1], c.bank[2], c.bank[3], c.bank[4]]
        pick = lambda a, e: a[e] if isinstance(e, int) else a[bass.ds(e, 1)].squeeze(0)
        with nc.Block() as block:
            @block.sync
            def _(sp):
                for p in range(2):
                    sp.dma_start(XE[p][:, :, :], pick(disp, p)).then_inc((s["in0"], s["in1"])[p], 16)
                with sp.Fori(1, E0 // 2) as j:
                    for p in range(2):
                        sp.wait_ge(s["xt_done"], 2 * j + p - 1)
                        sp.dma_start(XE[p][:, :, :], pick(disp, 2 * j + p)).then_inc((s["in0"], s["in1"])[p], 16)
                        sp.wait_ge(s["o_ev"], 2 * j + p)
                        load_expert(sp, 2 * j + p, p)

            @block.gpsimd
            def _(pool):
                with pool.Fori(0, E0 // 2) as j:
                    for p in range(2):
                        pool.wait_ge(s["o_ev"], 2 * j + p + 2)
                        pool.dma_start(pick(eo, 2 * j + p), EO[p][:, :, :]).then_inc((s["st0"], s["st1"])[p], 16)
                for p in range(2):
                    pool.wait_ge((s["st0"], s["st1"])[p], 16 * (E0 // 2))

            @block.tensor
            def _(pe):
                def turn(e, p, n):
                    pe.wait_ge((s["in0"], s["in1"])[p], 16 * n)
                    pe.wait_ge(s["xt_ev"], e + 1)
                    for k in range(KC):
                        for t in range(CT):
                            mm = pe.transpose(XTB[:, k * CAP + t * P:k * CAP + (t + 1) * P], XE[p][:, t, k * P:(k + 1) * P], c.IDN[:, :])
                    mm.then_inc(s["xt_done"], 1)

                def expert(e, p, n, nxt=True):
                    pe.wait_ge((w["ld0"], w["ld1"])[p], 48 * n)
                    pe.wait_ge(s["xt_ev"], e + 2)
                    for q in range(MC // 2):
                        pe.wait_ge(s["h_ev"], 8 * e + 2 * q + 2)
                        for i in range(2):
                            m = 2 * q + i
                            for k in range(KC):
                                mm = pe.matmul(HB[q][:, i * CAP:(i + 1) * CAP], F1[p][:, k, m * P:(m + 1) * P], XET[:, k, :],
                                               start=(k == 0), stop=(k == KC - 1))
                        mm.then_inc(s["h_done"], 1)
                    if nxt:
                        turn(e + 1, 1 - p, n + p)
                    pe.wait_ge(s["h_ev"], 8 * e + 16)
                    pe.wait_ge(s["o_ev"], e + 1)
                    for t in range(CT):
                        for m in range(MC):
                            mm = pe.matmul(OB[:, t * D:(t + 1) * D], HT[:, m, t * P:(t + 1) * P], F2[p][:, m, :],
                                           start=(m == 0), stop=(m == MC - 1))
                    mm.then_inc(s["o_done"], 1)

                turn(0, 0, 1)
                with pe.Fori(0, E0 // 2 - 1) as j:
                    expert(2 * j, 0, j + 1)
                    expert(2 * j + 1, 1, j + 1)
                expert(E0 - 2, 0, E0 // 2)
                expert(E0 - 1, 1, E0 // 2, False)

            @block.scalar
            def _(act):
                act.sem_inc(s["xt_ev"], 1)
                act.sem_inc(s["h_ev"], 8)

                def turned(e):
                    act.wait_ge(s["xt_done"], e + 1)
                    act.activation(XET[:, :, :], XTB[:, :].rearrange("p (k t) -> p k t", k=KC), ACT.Copy).then_inc(s["xt_ev"], 1)

                def expert(e, p, nxt=True):
                    for m in range(MC):
                        act.wait_ge(s["h_done"], 4 * e + m // 2 + 1)
                        act.activation(HT[:, m, :], HB[m // 2][:, (m % 2) * CAP:(m % 2 + 1) * CAP], ACT.Gelu,
                                       bias=B1[:, e * MC + m:e * MC + m + 1] if isinstance(e, int) else B1[:, bass.ds(e * MC + m, 1)]).then_inc(s["h_ev"], 1)
                    if nxt:
                        turned(e + 1)

                turned(0)
                with act.Fori(0, E0 // 2 - 1) as j:
                    expert(2 * j, 0)
                    expert(2 * j + 1, 1)
                expert(E0 - 2, 0)
                expert(E0 - 1, 1, False)

            @block.vector
            def _(dve):
                def expert(e, p, n):
                    dve.wait_ge(s["o_done"], e + 1)
                    if n is not None:
                        dve.wait_ge((s["st0"], s["st1"])[p], 16 * n)
                    dve.tensor_tensor(EO[p][:, :, :], OB[:, :].rearrange("p (t n) -> p t n", t=CT),
                                      bcast(B2[p][:, :], 1, CT), ALU.add).then_inc(s["o_ev"], 1)

                dve.sem_inc(s["o_ev"], 1)
                for p in range(2):
                    expert(p, p, None)
                with dve.Fori(1, E0 // 2) as j:
                    for p in range(2):
                        expert(2 * j + p, p, j)


def combine(nc, c, G, GIX):
    with ExitStack() as st:
        s = sems(nc, st, "mc_", "x_add0")
        got = sem_row(nc, st, "mc_got", B)
        GA = sb(nc, st, "mc_ga", [P, B, TOPK, D])
        with nc.Block() as block:
            @block.gpsimd
            def _(pool):
                for b in range(B):
                    for t in range(TOPK):
                        pool.indirect_dma_start(GA[:, b, t, :], None, c.eo, bass.IndirectOffsetOnAxis(ap=GIX[:, t, b:b + 1], axis=0),
                                                bounds_check=E0 * CAP - 1, oob_is_err=False).then_inc(got[b], 16)

            @block.vector
            def _(dve):
                for b in range(B):
                    dve.wait_ge(got[b], 16 * TOPK)
                    dve.scalar_tensor_tensor(c.X[:, b, :], GA[:, b, 0, :], G[:, 0, b:b + 1], c.X[:, b, :], ALU.mult, ALU.add).then_inc(s["x_add0"], 1)
                    dve.wait_ge(s["x_add0"], b + 1)
                    dve.scalar_tensor_tensor(c.X[:, b, :], GA[:, b, 1, :], G[:, 1, b:b + 1], c.X[:, b, :], ALU.mult, ALU.add)


def turn_weights(nc, c, prefix, jobs):
    with ExitStack() as st:
        n = len(jobs)
        s = sems(nc, st, prefix, "turned ev_a ev_d")
        ld = sem_row(nc, st, prefix + "ld", n)
        raw = [sb(nc, st, f"{prefix}raw{i}", [P, r, k * P]) for i, (_, r, k, _) in enumerate(jobs)]
        tiles = [(i, rr, kk) for i, (_, r, k, _) in enumerate(jobs) for rr in range(r) for kk in range(k)]
        groups = [tiles[g:g + 4] for g in range(0, len(tiles), 4)]
        with nc.Block() as block:
            @block.sync
            def _(sp):
                for i, (src, r, k, _) in enumerate(jobs):
                    sp.dma_start(raw[i][:, :, :], src.rearrange("(r p) d -> p r d", p=P)).then_inc(ld[i], 16)

            @block.tensor
            def _(pe):
                for g, group in enumerate(groups):
                    if g >= 8:
                        pe.wait_ge((s["ev_a"], s["ev_d"])[g % 2], (g - 8) // 2 + 1)
                    for m, (i, rr, kk) in enumerate(group):
                        pe.wait_ge(ld[i], 16)
                        mm = pe.transpose(c.bank[g % 8][:, m * P:(m + 1) * P], raw[i][:, rr, kk * P:(kk + 1) * P], c.IDN[:, :])
                    mm.then_inc(s["turned"], 1)

            def evacuate(eng, which, done, copy):
                for g, group in enumerate(groups):
                    if g % 2 != which:
                        continue
                    eng.wait_ge(s["turned"], g + 1)
                    for m, (i, rr, kk) in enumerate(group):
                        last = copy(jobs[i][3][:, kk, rr * P:(rr + 1) * P], c.bank[g % 8][:, m * P:(m + 1) * P])
                    last.then_inc(done, 1)

            @block.scalar
            def _(act):
                evacuate(act, 0, s["ev_a"], lambda o, i: act.activation(o, i, ACT.Copy))

            @block.vector
            def _(dve):
                evacuate(dve, 1, s["ev_d"], lambda o, i: dve.tensor_copy(o, i))


def attention1(nc, c):
    HPC = P // HD1
    VW = HD1 + 1
    with ExitStack() as st:
        WT = sb(nc, st, "at_wt", [P, KC, 3 * D])
        WOT = sb(nc, st, "at_wot", [P, KC, D])
        turn_weights(nc, c, "at_w_", [(c.wqkv, 3 * KC, KC, WT), (c.wout, KC, KC, WOT)])
        s = sems(nc, st, "at_", "bias_ld const xb qk_done qk_ev kx v_done v_ev sc_done masked maxed sub_d sub_p exped "
                 "pt_done pt_ev pv_done rsum norm ot_done ot_ev out_done x_add x_b")
        BQK = sb(nc, st, "at_bqk", [P, 4])
        BV = sb(nc, st, "at_bv", [P, D])
        BO = sb(nc, st, "at_bo", [P, D])
        OWN = sb(nc, st, "at_own", [P, HPC])
        MASK = sb(nc, st, "at_mask", [P, S])
        XB = [sb(nc, st, f"at_xb{p}", [P, KC, S]) for p in range(2)]
        QK = sb(nc, st, "at_qk", [P, 4, S])
        KX = sb(nc, st, "at_kx", [P, H1, S])
        VA = [sb(nc, st, f"at_v{p}", [P, H1, VW]) for p in range(2)]
        SM = [sb(nc, st, f"at_sm{p}", [P, H1, S]) for p in range(2)]
        MX = [sb(nc, st, f"at_mx{p}", [P, H1]) for p in range(2)]
        PT = sb(nc, st, "at_pt", [P, H1, S])
        RS = sb(nc, st, "at_rs", [P, H1])
        AO = sb(nc, st, "at_ao", [P, H1, HD1])
        AOT = sb(nc, st, "at_aot", [P, KC, S])
        SCB = c.bank[0:4]
        QKB, VOB = c.bank[4], c.bank[5]
        PTB = [c.bank[6], c.bank[7]]
        HH = H1 // 2
        with nc.Block() as block:
            @block.sync
            def _(sp):
                with nc.allow_non_contiguous_dma(reason="four columns"):
                    sp.dma_start(BQK[:, :], c.bqkv[0:2 * D].rearrange("(m p) -> p m", p=P)).then_inc(s["bias_ld"], 16)
                sp.dma_start(BV[:, :], c.bqkv[2 * D:3 * D].rearrange("(a n) -> a n", a=1).broadcast_to([P, D])).then_inc(s["bias_ld"], 16)
                sp.dma_start(BO[:, :], c.bout.rearrange("(a n) -> a n", a=1).broadcast_to([P, D])).then_inc(s["bias_ld"], 16)

            @block.gpsimd
            def _(pool):
                pool.memset(MASK[:, :], 0.0).then_inc(s["const"], 1)
                for p in range(2):
                    pool.memset(VA[p][:, :, HD1:VW], 1.0).then_inc(s["const"], 1)
                pool.wait_ge(s["const"], 3)
                pool.affine_select(out=MASK[:, :], in_=MASK[:, :], compare_op=ALU.is_ge, fill=NEG, base=0,
                                   pattern=[[-1, S]], channel_multiplier=1).then_inc(s["const"], 1)

                def take(b, p):
                    pool.wait_ge(s["const"], 3)
                    src = c.XNT[:, :, b * S:(b + 1) * S] if isinstance(b, int) else c.XNT[:, :, bass.ds(b * S, S)]
                    pool.tensor_copy(XB[p][:, :, :], src).then_inc(s["xb"], 1)

                def spread_keys(b):
                    pool.wait_ge(s["qk_ev"], 4 * b + 4)
                    if not isinstance(b, int) or b:
                        pool.wait_ge(s["sc_done"], b)
                    for ch in range(KC):
                        pool.tensor_tensor(KX[:, ch * HPC:(ch + 1) * HPC, :], bcast(QK[:, KC + ch, :], 1, HPC),
                                           bcast(OWN[:, :], 2, S), ALU.mult).then_inc(s["kx"], 1)

                def subtract(b, p):
                    pool.wait_ge(s["maxed"], b + 1)
                    pool.tensor_tensor(SM[p][:, HH:H1, :], SM[p][:, HH:H1, :], bcast(MX[p][:, HH:H1], 2, S), ALU.subtract).then_inc(s["sub_p"], 1)

                def batch(b, p, more=2, take_more=True):
                    if more > 1:
                        spread_keys(b + 2)
                    if more:
                        subtract(b + 1, 1 - p)
                    if take_more:
                        pool.wait_ge(s["v_done"], b + 2)
                        take(b + 3, 1 - p)

                take(0, 0)
                take(1, 1)
                pool.wait_ge(s["x_b"], 3)
                spread_keys(0)
                pool.wait_ge(s["v_done"], 1)
                take(2, 0)
                spread_keys(1)
                subtract(0, 0)
                with pool.Fori(0, B // 2 - 2) as j:
                    batch(2 * j, 0)
                    batch(2 * j + 1, 1)
                batch(B - 4, 0)
                batch(B - 3, 1, 2, False)
                batch(B - 2, 0, 1, False)

            @block.tensor
            def _(pe):
                def project_qk(b, p):
                    pe.wait_ge(s["xb"], b + 1)
                    if not isinstance(b, int) or b:
                        pe.wait_ge(s["qk_ev"], 4 * b)
                    for m in range(4):
                        for k in range(KC):
                            mm = pe.matmul(QKB[:, m * S:(m + 1) * S], WT[:, k, m * P:(m + 1) * P], XB[p][:, k, :],
                                           start=(k == 0), stop=(k == KC - 1))
                    mm.then_inc(s["qk_done"], 1)

                def project_v(b, p):
                    if isinstance(b, int) and b == 1:
                        pe.wait_ge(s["v_ev"], 1)
                    for k in range(KC):
                        mm = pe.matmul(PTB[0][:, 0:D], XB[p][:, k, :], WT[:, k, 2 * D:3 * D], start=(k == 0), stop=(k == KC - 1))
                    mm.then_inc(s["v_done"], 1)

                def scores(b):
                    pe.wait_ge(s["qk_ev"], 4 * b + 4)
                    pe.wait_ge(s["kx"], 2 * b + 2)
                    for j in range(4):
                        if not isinstance(b, int) or b:
                            pe.wait_ge(s["masked"], 4 * b + j - 3)
                        mm = pe.matmul(SCB[j][:, :], QK[:, j // 2, :], KX[:, 4 * j:4 * j + 4, :].rearrange("p h t -> p (h t)"),
                                       start=True, stop=True)
                    mm.then_inc(s["sc_done"], 1)

                def attend(b, p, v_next):
                    pe.wait_ge(s["v_ev"], b + 1 + v_next)
                    for g in range(4):
                        pe.wait_ge(s["exped"], 2 * b + 1 + g // 2)
                        pe.wait_ge(s["pt_ev"], 4 * b + g + 1)
                        for i in range(4):
                            mm = pe.transpose(PTB[g % 2][:, i * S:(i + 1) * S], SM[p][:, 4 * g + i, :], c.IDN[:, :])
                        mm.then_inc(s["pt_done"], 1)
                    pe.wait_ge(s["x_add"], b + 1)
                    for h in range(H1):
                        if h % 4 == 0:
                            pe.wait_ge(s["pt_ev"], 4 * b + h // 4 + 3)
                        mm = pe.matmul(VOB[:, h * VW:(h + 1) * VW], PT[:, h, :], VA[p][:, h, :], start=True, stop=True)
                    mm.then_inc(s["pv_done"], 1)

                def turn_result(b):
                    pe.wait_ge(s["norm"], b + 1)
                    for k in range(KC):
                        mm = pe.transpose(VOB[:, k * S:(k + 1) * S], AO[:, k * HPC:(k + 1) * HPC, :].rearrange("p h d -> p (h d)"), c.IDN[:, :])
                    mm.then_inc(s["ot_done"], 1)

                def output(b):
                    pe.wait_ge(s["ot_ev"], b + 1)
                    for k in range(KC):
                        mm = pe.matmul(VOB[:, 0:D], AOT[:, k, :], WOT[:, k, :], start=(k == 0), stop=(k == KC - 1))
                    mm.then_inc(s["out_done"], 1)

                def batch(b, p, more=2):
                    if more:
                        scores(b + 1)
                    if more > 1:
                        project_qk(b + 2, p)
                    attend(b, p, 1 if more else 0)
                    turn_result(b)
                    if more > 1:
                        project_v(b + 2, p)
                    output(b)

                pe.wait_ge(s["const"], 4)
                project_qk(0, 0)
                project_v(0, 0)
                scores(0)
                project_qk(1, 1)
                project_v(1, 1)
                with pe.Fori(0, B // 2 - 1) as j:
                    batch(2 * j, 0)
                    batch(2 * j + 1, 1)
                batch(B - 2, 0, 1)
                batch(B - 1, 1, 0)

            @block.scalar
            def _(act):
                act.sem_inc(s["pt_ev"], 2)
                act.wait_ge(s["bias_ld"], 48)

                def projected(b):
                    act.wait_ge(s["qk_done"], b + 1)
                    if not isinstance(b, int) or b > 0:
                        act.wait_ge(s["sc_done"], b)
                        act.wait_ge(s["kx"], 2 * b)
                    for m in (2, 3, 0, 1):
                        act.activation(QK[:, m, :], QKB[:, m * S:(m + 1) * S], ACT.Identity, bias=BQK[:, m:m + 1]).then_inc(s["qk_ev"], 1)

                def exps(b, p):
                    act.wait_ge(s["sub_d"], b + 1)
                    act.activation(SM[p][:, 0:HH, :], SM[p][:, 0:HH, :], ACT.Exp).then_inc(s["exped"], 1)
                    act.wait_ge(s["sub_p"], b + 1)
                    act.activation(SM[p][:, HH:H1, :], SM[p][:, HH:H1, :], ACT.Exp).then_inc(s["exped"], 1)

                def batch(b, p, more=2):
                    if more > 1:
                        projected(b + 2)
                    for g in range(4):
                        act.wait_ge(s["pt_done"], 4 * b + g + 1)
                        act.activation(PT[:, 4 * g:4 * g + 4, :], PTB[g % 2][:, :].rearrange("p (h t) -> p h t", h=4), ACT.Copy).then_inc(s["pt_ev"], 1)
                    act.wait_ge(s["ot_done"], b + 1)
                    act.activation(AOT[:, :, :], VOB[:, 0:KC * S].rearrange("p (k t) -> p k t", k=KC), ACT.Copy).then_inc(s["ot_ev"], 1)
                    if more:
                        exps(b + 1, 1 - p)

                projected(0)
                projected(1)
                exps(0, 0)
                with act.Fori(0, B // 2 - 1) as j:
                    batch(2 * j, 0)
                    batch(2 * j + 1, 1)
                batch(B - 2, 0, 1)
                batch(B - 1, 1, 0)

            @block.vector
            def _(dve):
                dve.sem_inc(s["x_add"], 1)
                dve.tensor_reduce(OWN[:, :], c.IDN[:, :].rearrange("p (h r) -> p h r", h=HPC), AX.X, ALU.add).then_inc(s["x_b"], 1)
                dve.wait_ge(s["bias_ld"], 48)
                dve.wait_ge(s["const"], 4)
                for g in range(2):
                    x = c.X[:, g * B // 2:(g + 1) * B // 2, :]
                    dve.tensor_tensor(x, x, bcast(BO[:, :], 1, B // 2), ALU.add).then_inc(s["x_b"], 1)
                dve.wait_ge(s["x_b"], 3)

                def values(b, p):
                    dve.wait_ge(s["v_done"], b + 1)
                    dve.tensor_tensor(VA[p][:, :, 0:HD1], PTB[0][:, 0:D].rearrange("p (h d) -> p h d", h=H1),
                                      BV[:, :].rearrange("p (h d) -> p h d", h=H1), ALU.add).then_inc(s["v_ev"], 1)

                def softmax(b, p):
                    dve.wait_ge(s["sc_done"], b + 1)
                    for j in range(4):
                        dve.scalar_tensor_tensor(SM[p][:, 4 * j:4 * j + 4, :], SCB[j][:, :].rearrange("p (h t) -> p h t", h=4),
                                                 float(HD1) ** -0.5, bcast(MASK[:, :], 1, 4), ALU.mult, ALU.add).then_inc(s["masked"], 1)
                    dve.wait_ge(s["masked"], 4 * b + 4)
                    dve.tensor_reduce(MX[p][:, :], SM[p][:, :, :], AX.X, ALU.max).then_inc(s["maxed"], 1)
                    dve.wait_ge(s["maxed"], b + 1)
                    dve.tensor_tensor(SM[p][:, 0:HH, :], SM[p][:, 0:HH, :], bcast(MX[p][:, 0:HH], 2, S), ALU.subtract).then_inc(s["sub_d"], 1)

                def batch(b, p, more=2):
                    if more:
                        softmax(b + 1, 1 - p)
                    dve.wait_ge(s["pv_done"], b + 1)
                    ov = VOB[:, 0:H1 * VW].rearrange("p (h d) -> p h d", h=H1)
                    dve.reciprocal(RS[:, :], ov[:, :, HD1]).then_inc(s["rsum"], 1)
                    dve.wait_ge(s["rsum"], b + 1)
                    dve.tensor_tensor(AO[:, :, :], ov[:, :, 0:HD1], bcast(RS[:, :], 2, HD1), ALU.mult).then_inc(s["norm"], 1)
                    if more > 1:
                        values(b + 2, p)
                    dve.wait_ge(s["out_done"], b + 1)
                    x = c.X[:, b, :] if isinstance(b, int) else c.X[:, bass.ds(b, 1), :].squeeze(1)
                    dve.tensor_tensor(x, x, VOB[:, 0:D], ALU.add).then_inc(s["x_add"], 1)

                values(0, 0)
                softmax(0, 0)
                values(1, 1)
                with dve.Fori(0, B // 2 - 1) as j:
                    batch(2 * j, 0)
                    batch(2 * j + 1, 1)
                batch(B - 2, 0, 1)
                batch(B - 1, 1, 0)


def cross1(nc, c):
    LT = D // P
    with ExitStack() as st:
        QWT = sb(nc, st, "cr_qwt", [P, 1, S])
        KWT = sb(nc, st, "cr_kwt", [P, 1, S])
        VWT = sb(nc, st, "cr_vwt", [P, 1, S])
        turn_weights(nc, c, "cr_w_", [(c.QW, 1, 1, QWT), (c.KW, 1, 1, KWT), (c.VW, 1, 1, VWT)])
        s = sems(nc, st, "cr_", "bias_ld cb q_done k_done v_done q_ev k_ev v_ev sc_ev sc_done maxed shifted exped summed "
                 "rsum norm pt_done pt_ev h_done x_add")
        BI = sb(nc, st, "cr_bi", [P, 3])
        CB = [sb(nc, st, f"cr_cb{p}", [P, D]) for p in range(2)]
        Q = sb(nc, st, "cr_q", [P, D])
        K = sb(nc, st, "cr_k", [P, D])
        V = [sb(nc, st, f"cr_v{p}", [P, LT, S]) for p in range(2)]
        PR = [sb(nc, st, f"cr_pr{p}", [P, LT, D]) for p in range(2)]
        MX = sb(nc, st, "cr_mx", [P, LT])
        RS = sb(nc, st, "cr_rs", [P, LT])
        PT = sb(nc, st, "cr_pt", [P, LT, D])
        QB, KB, VB, SB0, SB1, PTB, HB = c.bank[0], c.bank[1], c.bank[2], c.bank[3], c.bank[4], c.bank[5], c.bank[6]
        SCB = [SB0, SB1]
        with nc.Block() as block:
            @block.sync
            def _(sp):
                with nc.allow_non_contiguous_dma(reason="three columns"):
                    for i, bias in enumerate((c.Qb, c.Kb, c.Vb)):
                        sp.dma_start(BI[:, i:i + 1], bias.rearrange("(p a) -> p a", a=1)).then_inc(s["bias_ld"], 16)

            @block.gpsimd
            def _(pool):
                def take(b, p):
                    pool.wait_ge(c.s["ctx_loaded"], 16)
                    src = c.CTX[:, b, :] if isinstance(b, int) else c.CTX[:, bass.ds(b, 1), :].squeeze(1)
                    pool.tensor_copy(CB[p][:, :], src).then_inc(s["cb"], 1)

                def batch(b, p):
                    pool.wait_ge(s["sc_ev"], b + 1)
                    pool.wait_ge(s["maxed"], b + 1)
                    pool.tensor_tensor(PR[p][:, :, :], PR[p][:, :, :], bcast(MX[:, :], 2, D), ALU.subtract).then_inc(s["shifted"], 1)
                    pool.wait_ge(s["rsum"], b + 1)
                    pool.tensor_tensor(PR[p][:, :, :], PR[p][:, :, :], bcast(RS[:, :], 2, D), ALU.mult).then_inc(s["norm"], 1)

                take(0, 0)
                take(1, 1)
                with pool.Fori(0, B // 2 - 1) as j:
                    for p in range(2):
                        batch(2 * j + p, p)
                        pool.wait_ge(s["v_done"], 2 * j + p + 1)
                        take(2 * j + p + 2, p)
                batch(B - 2, 0)
                batch(B - 1, 1)

            @block.tensor
            def _(pe):
                def project(b, p):
                    pe.wait_ge(s["cb"], b + 1)
                    xn = c.XN[:, b, :] if isinstance(b, int) else c.XN[:, bass.ds(b, 1), :].squeeze(1)
                    pe.wait_ge(s["q_ev"], b + 1)
                    pe.matmul(QB[:, 0:D], QWT[:, 0, :], xn, start=True, stop=True).then_inc(s["q_done"], 1)
                    pe.wait_ge(s["k_ev"], b + 1)
                    pe.matmul(KB[:, 0:D], KWT[:, 0, :], CB[p][:, :], start=True, stop=True).then_inc(s["k_done"], 1)
                    pe.wait_ge(s["v_ev"], b + 1)
                    for t in range(LT):
                        mm = pe.matmul(VB[:, t * S:(t + 1) * S], CB[p][:, t * P:(t + 1) * P], VWT[:, 0, :], start=True, stop=True)
                    mm.then_inc(s["v_done"], 1)

                def scores(b, p):
                    pe.wait_ge(s["q_ev"], b + 2)
                    pe.wait_ge(s["k_ev"], b + 2)
                    for t in range(LT):
                        mm = pe.matmul(SCB[p][:, t * D:(t + 1) * D], Q[:, t * P:(t + 1) * P], K[:, :], start=True, stop=True)
                    mm.then_inc(s["sc_done"], 1)

                def attend(b, p):
                    pe.wait_ge(s["norm"], b + 1)
                    pe.wait_ge(s["pt_ev"], b + 1)
                    for u in range(LT):
                        for t in range(LT):
                            mm = pe.transpose(PTB[:, u * D + t * P:u * D + (t + 1) * P], PR[p][:, t, u * P:(u + 1) * P], c.IDN[:, :])
                    mm.then_inc(s["pt_done"], 1)

                def output(b, p):
                    pe.wait_ge(s["pt_ev"], b + 2)
                    pe.wait_ge(s["v_ev"], b + 2)
                    pe.wait_ge(s["x_add"], b + 1)
                    for u in range(LT):
                        mm = pe.matmul(HB[:, 0:D], V[p][:, u, :], PT[:, u, :], start=(u == 0), stop=(u == LT - 1))
                    mm.then_inc(s["h_done"], 1)

                def batch(b, p, nxt=True):
                    if nxt:
                        project(b + 1, 1 - p)
                        scores(b + 1, 1 - p)
                    attend(b, p)
                    output(b, p)

                project(0, 0)
                scores(0, 0)
                with pe.Fori(0, B // 2 - 1) as j:
                    batch(2 * j, 0)
                    batch(2 * j + 1, 1)
                batch(B - 2, 0)
                batch(B - 1, 1, False)

            @block.scalar
            def _(act):
                act.sem_inc(s["q_ev"], 1)
                act.sem_inc(s["k_ev"], 1)
                act.sem_inc(s["pt_ev"], 1)
                act.wait_ge(s["bias_ld"], 48)

                def project(b):
                    act.wait_ge(s["q_done"], b + 1)
                    act.activation(Q[:, :], QB[:, 0:D], ACT.Identity, bias=BI[:, 0:1]).then_inc(s["q_ev"], 1)
                    act.wait_ge(s["k_done"], b + 1)
                    act.activation(K[:, :], KB[:, 0:D], ACT.Identity, bias=BI[:, 1:2]).then_inc(s["k_ev"], 1)

                def exps(b, p):
                    act.wait_ge(s["shifted"], b + 1)
                    act.activation(PR[p][:, :, :], PR[p][:, :, :], ACT.Exp).then_inc(s["exped"], 1)

                def batch(b, p, nxt=True):
                    if nxt:
                        project(b + 1)
                    act.wait_ge(s["pt_done"], b + 1)
                    act.activation(PT[:, :, :], PTB[:, :].rearrange("p (u q) -> p u q", u=LT), ACT.Copy).then_inc(s["pt_ev"], 1)
                    if nxt:
                        exps(b + 1, 1 - p)

                project(0)
                exps(0, 0)
                with act.Fori(0, B // 2 - 1) as j:
                    batch(2 * j, 0)
                    batch(2 * j + 1, 1)
                batch(B - 2, 0)
                batch(B - 1, 1, False)

            @block.vector
            def _(dve):
                dve.sem_inc(s["v_ev"], 1)
                dve.sem_inc(s["x_add"], 1)
                dve.wait_ge(s["bias_ld"], 48)

                def scores(b, p):
                    dve.wait_ge(s["v_done"], b + 1)
                    dve.tensor_copy(V[p][:, :, :], VB[:, 0:LT * S].rearrange("p (t e) -> p t e", t=LT)).then_inc(s["v_ev"], 1)
                    dve.wait_ge(s["sc_done"], b + 1)
                    dve.tensor_copy(PR[p][:, :, :], SCB[p][:, :].rearrange("p (t k) -> p t k", t=LT)).then_inc(s["sc_ev"], 1)
                    dve.tensor_reduce(MX[:, :], SCB[p][:, :].rearrange("p (t k) -> p t k", t=LT), AX.X, ALU.max).then_inc(s["maxed"], 1)

                def sums(b, p):
                    dve.wait_ge(s["exped"], b + 1)
                    dve.tensor_reduce(RS[:, :], PR[p][:, :, :], AX.X, ALU.add).then_inc(s["summed"], 1)
                    dve.wait_ge(s["summed"], b + 1)
                    dve.reciprocal(RS[:, :], RS[:, :]).then_inc(s["rsum"], 1)

                def add(b):
                    dve.wait_ge(s["h_done"], b + 1)
                    x = c.X[:, b, :] if isinstance(b, int) else c.X[:, bass.ds(b, 1), :].squeeze(1)
                    dve.scalar_tensor_tensor(x, HB[:, 0:D], BI[:, 2:3], x, ALU.add, ALU.add).then_inc(s["x_add"], 1)

                def batch(b, p, nxt=True):
                    if nxt:
                        scores(b + 1, 1 - p)
                    add(b)
                    if nxt:
                        sums(b + 1, 1 - p)

                scores(0, 0)
                sums(0, 0)
                with dve.Fori(0, B // 2 - 1) as j:
                    batch(2 * j, 0)
                    batch(2 * j + 1, 1)
                batch(B - 2, 0)
                batch(B - 1, 1, False)


def swiglu(nc, c):
    NT = 256
    NQ = T // NT
    QT = NT // S
    with ExitStack() as st:
        WG = sb(nc, st, "sw_wg", [P, KC, HID])
        WU = sb(nc, st, "sw_wu", [P, KC, HID])
        WD = sb(nc, st, "sw_wd", [P, MC, D])
        turn_weights(nc, c, "sw_w_", [(c.wgate, MC, KC, WG), (c.wup, MC, KC, WU), (c.wdown, KC, MC, WD)])
        s = sems(nc, st, "sw_", "gu_done sig h_ev o_done x_add")
        SG = sb(nc, st, "sw_sg", [P, MC, NT])
        HT = sb(nc, st, "sw_ht", [P, MC, NT])
        OB = [c.bank[6], c.bank[7]]
        with nc.Block() as block:
            @block.tensor
            def _(pe):
                def hidden(n):
                    xn = c.XNT[:, :, 0:NT] if isinstance(n, int) else c.XNT[:, :, bass.ds(n * NT, NT)]
                    for m in range(MC):
                        pe.wait_ge(s["h_ev"], 8 * n + m + (7 if m < 2 else 1 if m < 6 else 3))
                        for i, w in enumerate((WG, WU)):
                            for k in range(KC):
                                mm = pe.matmul(c.bank[m % 6][:, i * NT:(i + 1) * NT], w[:, k, m * P:(m + 1) * P], xn[:, k, :],
                                               start=(k == 0), stop=(k == KC - 1))
                        mm.then_inc(s["gu_done"], 1)

                def down(n):
                    pe.wait_ge(s["h_ev"], 8 * n + 16)
                    pe.wait_ge(s["x_add"], n + 1)
                    for t in range(QT):
                        for m in range(MC):
                            mm = pe.matmul(OB[0][:, t * D:(t + 1) * D], HT[:, m, t * P:(t + 1) * P], WD[:, m, :],
                                           start=(m == 0), stop=(m == MC - 1))
                    mm.then_inc(s["o_done"], 1)

                with pe.Fori(0, NQ) as n:
                    hidden(n)
                    down(n)

            @block.scalar
            def _(act):
                with act.Fori(0, NQ) as n:
                    for m in range(MC):
                        act.wait_ge(s["gu_done"], 8 * n + m + 1)
                        act.wait_ge(s["h_ev"], 8 * n + m + 1)
                        act.activation(SG[:, m, :], c.bank[m % 6][:, 0:NT], ACT.Silu).then_inc(s["sig"], 1)

            @block.vector
            def _(dve):
                dve.sem_inc(s["h_ev"], 8)
                dve.sem_inc(s["x_add"], 1)
                with dve.Fori(0, NQ) as n:
                    for m in range(MC):
                        dve.wait_ge(s["sig"], 8 * n + m + 1)
                        dve.tensor_tensor(HT[:, m, :], SG[:, m, :], c.bank[m % 6][:, NT:2 * NT], ALU.mult).then_inc(s["h_ev"], 1)
                    dve.wait_ge(s["o_done"], n + 1)
                    x = c.X[:, bass.ds(n * QT, QT), :]
                    dve.tensor_tensor(x, x, OB[0][:, :].rearrange("p (t n) -> p t n", t=QT), ALU.add).then_inc(s["x_add"], 1)


def build(nc, c):
    with ExitStack() as stack:
        c.s = {n: stack.enter_context(nc.semaphore(n)) for n in
               "x_loaded ctx_loaded const zeros_ready disp_zeroed out".split()}
        c.bank = [stack.enter_context(nc.psum_tensor(f"bank{i}", [P, 512], F32)) for i in range(8)]
        c.X = sb(nc, stack, "X", [P, B, D])
        c.CTX = sb(nc, stack, "CTX", [P, B, D])
        c.XN = sb(nc, stack, "XN", [P, B, D])
        c.XNT = sb(nc, stack, "XNT", [P, KC, T])
        c.IDN = sb(nc, stack, "IDN", [P, P])
        c.MASK0 = sb(nc, stack, "MASK0", [P, SEG])
        c.ZERO = sb(nc, stack, "ZERO", [P, 2 * D])
        c.disp = nc.dram_tensor("disp", [E0 * CAP, D], F32, kind="Internal").ap()
        c.eo = nc.dram_tensor("eo", [E0 * CAP, D], F32, kind="Internal").ap()
        c.pad = nc.dram_tensor("pad", [HC, 384], F32, kind="Internal").ap()
        setup(nc, c, c.s)
        layernorm(nc, c, "ln1_")
        infini_attention(nc, c)
        layernorm(nc, c, "ln2_")
        long_conv(nc, c)
        layernorm(nc, c, "ln3_")
        moe(nc, c)
        layernorm(nc, c, "ln4_")
        attention1(nc, c)
        layernorm(nc, c, "ln5_", turned=False)
        cross1(nc, c)
        layernorm(nc, c, "ln6_")
        swiglu(nc, c)
        with nc.Block() as block:
            @block.sync
            def _(sp):
                sp.wait_ge(c.s["ctx_loaded"], 16)
                sp.wait_ge(c.s["disp_zeroed"], 16 * E0)
                sp.dma_start(c.out.rearrange("b p d -> p b d"), c.X[:, :, :]).then_inc(c.s["out"], 16)
                sp.wait_ge(c.s["out"], 16)


def kernel(**inputs):
    import numpy as _np
    import concourse.bacc as _bacc
    from concourse.bass_utils import run_bass_kernel_spmd as _run

    nc = _bacc.Bacc("TRN2", target_bir_lowering=False, num_devices=1)
    arrays = {}

    def given(name):
        a = _np.ascontiguousarray(inputs[name])
        arrays[f"in_{name}"] = a
        return nc.dram_tensor(f"in_{name}", a.shape, mybir.dt.from_np(a.dtype), kind="ExternalInput").ap()

    c = Core()
    c.x = given("x")
    c.ctx = given("ctx_2048")
    c.Wq = given("L0_attn_Wq")
    c.Wk = given("L0_attn_Wk")
    c.Wv = given("L0_attn_Wv")
    c.Wo = given("L0_attn_Wo")
    c.betas = given("L0_attn_betas")
    c.ssm = given("L0_xattn_ssm_kernel")
    c.convD = given("L0_xattn_D")
    c.wg = given("L0_ffn_wg")
    c.fc1 = given("L0_ffn_fc1_w")
    c.fc1b = given("L0_ffn_fc1_b")
    c.fc2 = given("L0_ffn_fc2_w")
    c.fc2b = given("L0_ffn_fc2_b")
    c.wqkv = given("L1_attn_w_qkv")
    c.bqkv = given("L1_attn_b_qkv")
    c.wout = given("L1_attn_w_out")
    c.bout = given("L1_attn_b_out")
    c.QW = given("L1_xattn_QW")
    c.Qb = given("L1_xattn_Qb")
    c.KW = given("L1_xattn_KW")
    c.Kb = given("L1_xattn_Kb")
    c.VW = given("L1_xattn_VW")
    c.Vb = given("L1_xattn_Vb")
    c.wgate = given("L1_ffn_w_gate")
    c.wup = given("L1_ffn_w_up")
    c.wdown = given("L1_ffn_w_down")
    c.out = nc.dram_tensor("out", (B, S, D), F32, kind="ExternalOutput").ap()
    build(nc, c)
    return _run(nc, [arrays], core_ids=[0]).results[0]["out"]
```

```python
from contextlib import ExitStack

import concourse.bass as bass
from concourse import mybir

F32 = mybir.dt.float32
I32 = mybir.dt.int32
U32 = mybir.dt.uint32
F32R = mybir.dt.float32r
ALU = mybir.AluOpType
ACT = mybir.ActivationFunctionType
AX = mybir.AxisListType

P = 128
B = 8
S = 128
D = 256
KC = D // P
T = B * S
EPS = 1e-5
NEG = -3.0e38

H0 = 16
DK = 128
SEG = 64
NJ = 16
HC = 16
HD = S // HC
E0 = 8
TOPK = 2
CAP = TOPK * T // E0
HID = 4 * D
MC = HID // P
BIG = 1 << 20
H1 = 16
HD1 = D // H1


class Core:
    pass


def bcast(ap, axis, n):
    shape = list(ap.shape)
    return ap.unsqueeze(axis).broadcast_to(shape[:axis] + [n] + shape[axis:])


def sb(nc, stack, name, shape, dt=F32):
    return stack.enter_context(nc.sbuf_tensor(name, shape, dt))


def sems(nc, stack, prefix, names):
    made = {n: stack.enter_context(nc.semaphore(prefix + n)) for n in names.split()}
    stack.callback(clear, nc, [x.num for x in made.values()])
    return made


def sem_row(nc, stack, prefix, n):
    made = [stack.enter_context(nc.semaphore(f"{prefix}{i}")) for i in range(n)]
    stack.callback(clear, nc, [x.num for x in made])
    return made


def clear(nc, nums):
    with nc.Block() as block:
        @block.sync
        def _(sp):
            left = sorted(nums)
            while left:
                n = 1
                while n < len(left) and left[n] == left[0] + n:
                    n += 1
                sp.sem_clear(range(left[0], left[0] + n))
                left = left[n:]


def attend_infini(nc, c):
    with ExitStack() as st:
        c.wqkv_ld = sem_row(nc, st, "wqkv_ld", 2)
        c.WQ = [sb(nc, st, f"ia_wqkv{p}", [P, 3, KC, DK]) for p in range(2)]
        c.BTM = sb(nc, st, "ia_btm", [P, H0, DK])
        c.BTR = sb(nc, st, "ia_btr", [P, H0, DK])
        c.SIGN = sb(nc, st, "ia_sign", [P, 1])
        c.XNTH = sb(nc, st, "xnth1", [P, KC, T], F32R)
        c.XNTL = sb(nc, st, "xntl1", [P, KC, T], F32R)
        norm = Norm(nc, c, st, "ln1_")
        setup(nc, c, c.s)

        def beta(act):
            act.wait_ge(c.s["beta_ld"], 16)
            act.wait_ge(c.s["sign"], 2)
            act.activation(c.BTM[:, :, :], c.BTR[:, :, :], ACT.Sigmoid, scale=c.SIGN[:, 0:1]).then_inc(c.s["beta"], 1)

        layernorm(nc, c, norm, split=True, whole=True, extra=beta, loads=lambda sp: later_loads(sp, c, c.s))
        infini_attention(nc, c)


def load_qkv(sp, c, h, p):
    for i, w in enumerate((c.Wq, c.Wk, c.Wv)):
        a = w.rearrange("(k p) (h n) -> h p k n", p=P, n=DK)
        src = a[h] if isinstance(h, int) else a[bass.ds(h, 1)].squeeze(0)
        sp.dma_start(c.WQ[p][:, i, :, :], src).then_inc(c.wqkv_ld[p], 16)


def later_loads(sp, c, s):
    load_qkv(sp, c, 1, 1)
    sp.dma_start(c.CTX[:, :, :], c.ctx.rearrange("b p d -> p b d")).then_inc(s["ctx_loaded"], 16)
    sp.dma_start(c.pad[:, P - 1:P - 1 + D], c.ssm).then_inc(s["pad_st"], 16)
    sp.wait_ge(s["zeros_ready"], 1)
    sp.dma_start(c.pad[:, 0:P - 1], c.ZERO[0:HC, 0:P - 1]).then_inc(s["pad_st"], 16)
    for e in range(E0):
        sp.dma_start(c.disp[e * CAP:(e + 1) * CAP, :].rearrange("(t p) d -> p t d", p=P),
                     c.ZERO[:, :].rearrange("p (t d) -> p t d", t=CAP // P)).then_inc(s["disp_zeroed"], 16)


def setup(nc, c, s):
    with nc.Block() as block:
        @block.sync
        def _(sp):
            sp.dma_start(c.X[:, :, :], c.x.rearrange("b p d -> p b d")).then_inc(s["x_loaded"], 16)
            load_qkv(sp, c, 0, 0)
            sp.dma_start(c.BTR[:, :, :].rearrange("p h n -> p (h n)"),
                         c.betas.rearrange("a h b n -> (a b) (h n)").broadcast_to([P, H0 * DK])).then_inc(s["beta_ld"], 16)

        @block.vector
        def _(dve):
            dve.memset(c.SIGN[0:SEG, :], 1.0).then_inc(s["sign"], 1)
            dve.memset(c.SIGN[SEG:P, :], -1.0).then_inc(s["sign"], 1)

        @block.gpsimd
        def _(pool):
            pool.memset(c.IDN[:, :], 0.0).then_inc(s["const"], 1)
            pool.memset(c.MASK0[:, :], 0.0).then_inc(s["const"], 1)
            pool.memset(c.ZERO[:, :], 0.0).then_inc(s["zeros_ready"], 1)
            pool.wait_ge(s["const"], 2)
            pool.affine_select(out=c.IDN[:, :], in_=c.IDN[:, :], compare_op=ALU.not_equal, fill=1.0,
                               base=0, pattern=[[-1, P]], channel_multiplier=1).then_inc(s["const"], 1)
            for g in range(2):
                half = c.MASK0[g * SEG:(g + 1) * SEG, :]
                pool.wait_ge(s["const"], 3 + g)
                pool.affine_select(out=half, in_=half, compare_op=ALU.is_ge, fill=NEG, base=0,
                                   pattern=[[-1, SEG]], channel_multiplier=1).then_inc(s["const"], 1)


def split_product(pe, out, lhs, rhs):
    n = len(lhs[0])
    for k in range(n):
        for i, (a, b) in enumerate(((0, 0), (0, 1), (1, 0))):
            mm = pe.matmul(out, lhs[a][k], rhs[b][k], start=(k == 0 and i == 0), stop=(k == n - 1 and i == 2))
    return mm


class Norm:

    def __init__(self, nc, c, st, pre):
        self.c = c
        self.s = sems(nc, st, pre, "stats aggr veps root rstd xn turned evac high low")
        self.st = sb(nc, st, pre + "stats", [P, B, 6])
        self.mv = sb(nc, st, pre + "mv", [P, B, 2])
        self.rstd = sb(nc, st, pre + "rstd", [P, B])

    def stats(self, dve, q):
        s, c = self.s, self.c
        for b in (2 * q, 2 * q + 1):
            dve.bn_stats(self.st[:, b, :], c.X[:, b, :]).then_inc(s["stats"], 1)
        self.join(dve, q)

    def moments(self, dve, b):
        x, st = [a[:, b, :] if isinstance(b, int) else a[:, bass.ds(b, 1), :].squeeze(1) for a in (self.c.X, self.st)]
        dve.bn_stats(st, x).then_inc(self.s["stats"], 1)

    def join(self, dve, q):
        s = self.s
        for b in (2 * q, 2 * q + 1):
            dve.wait_ge(s["stats"], b + 1)
            dve.bn_aggr(self.mv[:, b, :], self.st[:, b, :]).then_inc(s["aggr"], 1)
        dve.wait_ge(s["aggr"], 2 * q + 2)
        dve.tensor_scalar(self.rstd[:, 2 * q:2 * q + 2], self.mv[:, 2 * q:2 * q + 2, 1], EPS, None, ALU.add).then_inc(s["veps"], 1)

    def root(self, act, q):
        act.wait_ge(self.s["veps"], q + 1)
        r = self.rstd[:, 2 * q:2 * q + 2]
        act.activation(r, r, ACT.Sqrt).then_inc(self.s["root"], 1)

    def scale(self, dve, q):
        s, c, r = self.s, self.c, self.rstd
        dve.wait_ge(s["root"], q + 1)
        dve.reciprocal(r[:, 2 * q:2 * q + 2], r[:, 2 * q:2 * q + 2]).then_inc(s["rstd"], 1)
        dve.wait_ge(s["rstd"], q + 1)
        for b in (2 * q, 2 * q + 1):
            dve.tensor_scalar(c.XN[:, b, :], c.X[:, b, :], self.mv[:, b, 0:1], r[:, b:b + 1],
                              ALU.subtract, ALU.mult).then_inc(s["xn"], 1)

    def turn(self, pe, q, bank):
        pe.wait_ge(self.s["xn"], 2 * q + 2)
        for i in range(2):
            for k in range(KC):
                last = pe.transpose(bank[:, (2 * k + i) * S:(2 * k + i + 1) * S],
                                    self.c.XN[:, 2 * q + i, k * P:(k + 1) * P], self.c.IDN[:, :])
        last.then_inc(self.s["turned"], 1)

    def high(self, act, q, bank):
        act.wait_ge(self.s["turned"], q + 1)
        act.activation(self.c.XNTH[:, :, 2 * q * S:(2 * q + 2) * S], bank[:, :].rearrange("p (k t) -> p k t", k=KC),
                       ACT.Copy).then_inc(self.s["high"], 1)

    def low(self, dve, q, bank):
        at = slice(2 * q * S, (2 * q + 2) * S)
        dve.wait_ge(self.s["high"], q + 1)
        dve.tensor_tensor(self.c.XNTL[:, :, at], bank[:, :].rearrange("p (k t) -> p k t", k=KC),
                          self.c.XNTH[:, :, at].bitcast(F32), ALU.subtract).then_inc(self.s["low"], 1)

    def copy(self, act, q, bank):
        act.wait_ge(self.s["turned"], q + 1)
        act.activation(self.c.XNT[:, :, 2 * q * S:(2 * q + 2) * S], bank[:, :].rearrange("p (k t) -> p k t", k=KC),
                       ACT.Copy).then_inc(self.s["evac"], 1)


def layernorm(nc, c, n, turned=True, have_moments=False, split=False, whole=False, extra=None, loads=None):
    first = n.join if have_moments else n.stats
    with nc.Block() as block:
        @block.vector
        def _(dve):
            dve.wait_ge(c.s["x_loaded"], 16)
            for q in range(B // 2):
                first(dve, q)
            for q in range(B // 2):
                n.scale(dve, q)
            if split:
                for q in range(B // 2):
                    n.low(dve, q, c.bank[q])

        @block.scalar
        def _(act):
            for q in range(B // 2):
                n.root(act, q)
            if turned:
                for q in range(B // 2):
                    if whole or not split:
                        n.copy(act, q, c.bank[q])
                    if split:
                        n.high(act, q, c.bank[q])
            if extra is not None:
                extra(act)

        if loads is not None:
            @block.sync
            def _(sp):
                loads(sp)

        if turned:
            @block.tensor
            def _(pe):
                pe.wait_ge(c.s["const"], 3)
                for q in range(B // 2):
                    n.turn(pe, q, c.bank[q])


def infini_attention(nc, c):
    with ExitStack() as st:
        s = sems(nc, st, "ia_", "wo_ld beta_c w_hi w_lo const pj_done qk_ev v_ev "
                 "neg_done exp_done sig_done s_done s_free masked maxed shifted exped summed rsum "
                 "ad_done den rden p_pool p_mem p_free pt_done pts0 pts1 pv_done att_ev out_done x_add")
        WQ, BTM = c.WQ, c.BTM
        WH = sb(nc, st, "ia_wh", [P, 2, KC, DK], F32R)
        WL = sb(nc, st, "ia_wl", [P, 2, KC, DK], F32R)
        WO = sb(nc, st, "ia_wo", [P, H0, D])
        BTC = c.BTR
        QT = sb(nc, st, "ia_qt", [P, B, S])
        KT = sb(nc, st, "ia_kt", [P, B, S])
        EQ = sb(nc, st, "ia_eq", [P, 2, B, SEG])
        SQ = sb(nc, st, "ia_sq", [P, B, SEG])
        SK = sb(nc, st, "ia_sk", [P, B, SEG + 1])
        SM = sb(nc, st, "ia_sm", [P, B, SEG])
        EX = sb(nc, st, "ia_ex", [P, B, SEG])
        MX = sb(nc, st, "ia_mx", [P, B])
        RS = sb(nc, st, "ia_rs", [P, B])
        RD = sb(nc, st, "ia_rd", [P, B])
        PR = sb(nc, st, "ia_pr", [P, B, S])
        PTS = sb(nc, st, "ia_pts", [P, B, S])
        VX = [sb(nc, st, f"ia_vx{p}", [P, B, DK]) for p in range(2)]
        VD = [sb(nc, st, f"ia_vd{p}", [SEG, B, DK]) for p in range(2)]
        ATT = sb(nc, st, "ia_att", [P, NJ, B, S])
        SC = c.bank[0]
        AD = [c.bank[1], c.bank[2]]
        PJ = [c.bank[3], c.bank[4], c.bank[5]]
        OB = [c.bank[6], c.bank[7]]
        scale = float(DK) ** -0.5
        HB = B // 2
        norm = Norm(nc, c, st, "ln2_")
        NQ = B // 2

        with nc.Block() as block:
            @block.sync
            def _(sp):
                sp.dma_start(WO[:, :, :], c.Wo.rearrange("(h p) n -> p h n", p=DK)).then_inc(s["wo_ld"], 16)
                with sp.Fori(1, H0 // 2) as j:
                    for p in range(2):
                        sp.wait_ge(s["w_lo"], 2 * j + p - 1)
                        sp.wait_ge(s["pj_done"], 12 * j + 6 * p - 6)
                        load_qkv(sp, c, 2 * j + p, p)

            @block.gpsimd
            def _(pool):
                pool.memset(PR[:, :, :], 0.0).then_inc(s["const"], 1)
                pool.memset(SK[:, :, SEG:SEG + 1], 1.0 / DK).then_inc(s["const"], 1)
                pool.wait_ge(s["const"], 2)

                def split_low(h, p):
                    pool.wait_ge(s["w_hi"], h + 1)
                    pool.tensor_tensor(WL[:, :, :, :], WQ[p][:, 0:2, :, :], WH[:, :, :, :].bitcast(F32), ALU.subtract).then_inc(s["w_lo"], 1)

                def head(h, p, more=True):
                    pool.wait_ge(s["maxed"], h + 1)
                    pool.tensor_tensor(SM[:, :, :], SM[:, :, :], bcast(MX[:, :], 2, SEG), ALU.subtract).then_inc(s["shifted"], 1)
                    pool.wait_ge(s["rsum"], h + 1)
                    pool.wait_ge(s["p_free"], h + 1)
                    pool.tensor_tensor(PR[SEG:P, :, SEG:S], EX[SEG:P, :, :], bcast(RS[SEG:P, :], 2, SEG), ALU.mult).then_inc(s["p_pool"], 1)
                    pool.wait_ge(s["p_pool"], h + 1)
                    if more:
                        split_low(h + 2, p)

                split_low(0, 0)
                split_low(1, 1)
                with pool.Fori(0, H0 // 2 - 1) as j:
                    head(2 * j, 0)
                    head(2 * j + 1, 1)
                head(H0 - 2, 0, False)
                head(H0 - 1, 1, False)

            @block.scalar
            def _(act):
                def evac_qk(h):
                    for t in range(4):
                        act.wait_ge(s["pj_done"], 6 * h + t + 1)
                        dst = (QT, KT)[t // 2][:, (t % 2) * HB:(t % 2 + 1) * HB, :]
                        act.activation(dst, PJ[t % 3][:, :].rearrange("p (b t) -> p b t", b=HB), ACT.Copy).then_inc(s["qk_ev"], 1)

                def sigma_exp(h):
                    act.wait_ge(s["qk_ev"], 4 * h + 4)
                    act.activation(EQ[:, 0, :, :], QT[:, :, SEG:S], ACT.Relu, scale=-1.0).then_inc(s["neg_done"], 1)
                    act.activation(EQ[:, 1, :, :], KT[:, :, 0:SEG], ACT.Relu, scale=-1.0).then_inc(s["neg_done"], 1)
                    act.wait_ge(s["neg_done"], 2 * h + 2)
                    act.activation(EQ[:, :, :, :], EQ[:, :, :, :], ACT.Exp, scale=-1.0).then_inc(s["exp_done"], 1)

                def split_high(h, p, n):
                    act.wait_ge(c.wqkv_ld[p], 48 * n)
                    if not isinstance(h, int) or h:
                        act.wait_ge(s["pj_done"], 6 * h)
                    act.activation(WH[:, :, :, :], WQ[p][:, 0:2, :, :], ACT.Copy).then_inc(s["w_hi"], 1)

                def head(h, p, n=None, nxt=True):
                    act.wait_ge(s["shifted"], h + 1)
                    act.activation(EX[:, :, :], SM[:, :, :], ACT.Exp).then_inc(s["exped"], 1)
                    if nxt:
                        evac_qk(h + 1)
                    act.wait_ge(s["pt_done"], 2 * h + 1)
                    act.activation(PTS[:, 0:HB, :], AD[0][:, :].rearrange("p (b t) -> p b t", b=HB), ACT.Copy).then_inc(s["pts0"], 1)
                    if nxt:
                        sigma_exp(h + 1)
                    if n is not None:
                        split_high(h + 2, p, n)
                    for g in range(2):
                        act.wait_ge(s["pv_done"], 2 * h + g + 1)
                        src = OB[g][:, :].rearrange("p (b i m j) -> p b i m j", b=HB, i=2, j=NJ)
                        for i in range(2):
                            at = 4 * h + i * SEG
                            rows = slice(at, at + 4) if isinstance(h, int) else bass.ds(at, 4)
                            act.activation(ATT[:, :, g * HB:(g + 1) * HB, rows].rearrange("p j b m -> p b m j"),
                                           src[:, :, i, :, :], ACT.Copy).then_inc(s["att_ev"], 1)

                act.sem_inc(s["att_ev"], 4)
                act.sem_inc(s["pts0"], 1)
                split_high(0, 0, 1)
                evac_qk(0)
                sigma_exp(0)
                split_high(1, 1, 1)
                with act.Fori(0, H0 // 2 - 1) as j:
                    head(2 * j, 0, j + 2)
                    head(2 * j + 1, 1, j + 2)
                head(H0 - 2, 0)
                head(H0 - 1, 1, None, False)
                norm.root(act, 0)
                for q in range(1, NQ):
                    norm.root(act, q)
                    norm.copy(act, q - 1, c.bank[q - 1])
                norm.copy(act, NQ - 1, c.bank[NQ - 1])

            @block.tensor
            def _(pe):
                def project_qk(h, p, n, first=False):
                    pe.wait_ge(s["w_lo"], h + 1)
                    for t in range(4):
                        if t == 0 and not first:
                            pe.wait_ge(s["qk_ev"], 4 * h)
                        if t in (1, 2) and not first:
                            pe.wait_ge(s["v_ev"], 4 * h - 4 + 2 * t)
                        if t == 3:
                            pe.wait_ge(s["qk_ev"], 4 * h + 1)
                        half = slice((t % 2) * HB * S, (t % 2 + 1) * HB * S)
                        mm = split_product(pe, PJ[t % 3][:, :], [[w[:, t // 2, k, :] for k in range(KC)] for w in (WH, WL)],
                                           [[x[:, k, half] for k in range(KC)] for x in (c.XNTH, c.XNTL)])
                        mm.then_inc(s["pj_done"], 1)

                def project_v(h, p):
                    for t in range(4, 6):
                        pe.wait_ge(s["qk_ev"], 4 * h + t - 2)
                        for i in range(HB):
                            b = (t - 4) * HB + i
                            for k in range(KC):
                                mm = pe.matmul(PJ[t % 3][:, i * DK:(i + 1) * DK], c.XNT[:, k, b * S:(b + 1) * S],
                                               WQ[p][:, 2, k, :], start=(k == 0), stop=(k == KC - 1))
                        mm.then_inc(s["pj_done"], 1)

                def head(h, p, n, nxt=True):
                    pe.wait_ge(s["qk_ev"], 4 * h + 4)
                    pe.wait_ge(s["s_free"], h + 1)
                    for b in range(B):
                        for g in range(2):
                            r = slice(g * SEG, (g + 1) * SEG)
                            mm = pe.matmul(SC[r, b * SEG:(b + 1) * SEG], QT[:, b, r], KT[:, b, r], start=True, stop=True)
                    mm.then_inc(s["s_done"], 1)
                    pe.wait_ge(s["sig_done"], 2 * h + 2)
                    pe.wait_ge(s["pts0"], h + 1)
                    pe.wait_ge(s["pts1"], h + 1)
                    for b in range(B):
                        mm = pe.matmul(AD[b // HB][SEG:P, (b % HB) * (SEG + 1):(b % HB + 1) * (SEG + 1)],
                                       SQ[:, b, :], SK[:, b, :], start=True, stop=True)
                    mm.then_inc(s["ad_done"], 1)
                    if nxt:
                        project_qk(h + 1, 1 - p, n)
                    pe.wait_ge(s["p_pool"], h + 1)
                    pe.wait_ge(s["p_mem"], 3 * h + 3)
                    for g in range(2):
                        for i in range(HB):
                            mm = pe.transpose(AD[g][:, i * S:(i + 1) * S], PR[:, g * HB + i, :], c.IDN[:, :])
                        mm.then_inc(s["pt_done"], 1)
                    pe.drain().then_inc(s["p_free"], 1)
                    if nxt:
                        project_v(h + 1, 1 - p)
                    pe.wait_ge(s["v_ev"], 4 * h + 4)
                    for g in range(2):
                        pe.wait_ge(s["pts0" if g == 0 else "pts1"], h + 2)
                        pe.wait_ge(s["att_ev"], 4 * h + 2 + 2 * g)
                        for i in range(HB):
                            b = g * HB + i
                            pe.matmul(OB[g][:, i * S:i * S + SEG], VD[p][:, b, :], PTS[0:SEG, b, 0:SEG], start=True, stop=True)
                            mm = pe.matmul(OB[g][:, i * S + SEG:(i + 1) * S], VX[p][:, b, :], PTS[:, b, SEG:S], start=True, stop=True)
                        mm.then_inc(s["pv_done"], 1)

                def project_out():
                    pe.wait_ge(s["wo_ld"], 16)
                    pe.wait_ge(s["att_ev"], 4 * H0 + 4)
                    for q in range(B // 2):
                        if q >= 2:
                            pe.wait_ge(s["x_add"], q - 1)
                        for i in range(2):
                            for j in range(NJ):
                                mm = pe.matmul(OB[q % 2][:, i * D:(i + 1) * D], ATT[:, j, 2 * q + i, :], WO[:, j, :],
                                               start=(j == 0), stop=(j == NJ - 1))
                        mm.then_inc(s["out_done"], 1)
                        if q:
                            norm.turn(pe, q - 1, c.bank[q - 1])
                    norm.turn(pe, NQ - 1, c.bank[NQ - 1])

                pe.sem_inc(s["p_free"], 1)
                pe.wait_ge(s["const"], 2)
                project_qk(0, 0, 1, True)
                project_v(0, 0)
                with pe.Fori(0, H0 // 2 - 1) as j:
                    head(2 * j, 0, j + 1)
                    head(2 * j + 1, 1, j + 2)
                head(H0 - 2, 0, H0 // 2)
                head(H0 - 1, 1, 0, False)
                project_out()

            @block.vector
            def _(dve):
                def sigma(h):
                    dve.wait_ge(s["exp_done"], h + 1)
                    dve.scalar_tensor_tensor(SQ[:, :, :], QT[:, :, SEG:S], 0.0, EQ[:, 0, :, :], ALU.max, ALU.add).then_inc(s["sig_done"], 1)
                    dve.scalar_tensor_tensor(SK[:, :, 0:SEG], KT[:, :, 0:SEG], 0.0, EQ[:, 1, :, :], ALU.max, ALU.add).then_inc(s["sig_done"], 1)

                def evac_v(h, p):
                    for t in range(4, 6):
                        dve.wait_ge(s["pj_done"], 6 * h + t + 1)
                        b = slice((t - 4) * HB, (t - 3) * HB)
                        src = PJ[t % 3][:, :].rearrange("p (b n) -> p b n", b=HB)
                        if isinstance(h, int):
                            bm, bc = BTM[:, h, :], BTC[0:SEG, h, :]
                        else:
                            bm, bc = BTM[:, bass.ds(h, 1), :].squeeze(1), BTC[0:SEG, bass.ds(h, 1), :].squeeze(1)
                        dve.tensor_tensor(VX[p][:, b, :], src, bcast(bm, 1, HB), ALU.mult).then_inc(s["v_ev"], 1)
                        dve.tensor_tensor(VD[p][:, b, :], src[0:SEG], bcast(bc, 1, HB), ALU.mult).then_inc(s["v_ev"], 1)

                def head(h, p, nxt=True):
                    dve.wait_ge(s["s_done"], h + 1)
                    dve.scalar_tensor_tensor(SM[:, :, :], SC[:, :].rearrange("p (b k) -> p b k", b=B), scale,
                                             bcast(c.MASK0[:, :], 1, B), ALU.mult, ALU.add).then_inc(s["masked"], 1)
                    dve.wait_ge(s["masked"], h + 1)
                    dve.tensor_reduce(MX[:, :], SM[:, :, :], AX.X, ALU.max).then_inc(s["maxed"], 1)
                    dve.sem_inc(s["s_free"], 1)
                    dve.wait_ge(s["ad_done"], h + 1)
                    lin = [AD[g][SEG:P, 0:HB * (SEG + 1)].rearrange("p (b k) -> p b k", b=HB) for g in range(2)]
                    for g in range(2):
                        dve.tensor_reduce(RD[SEG:P, g * HB:(g + 1) * HB], lin[g], AX.X, ALU.add).then_inc(s["den"], 1)
                    dve.wait_ge(s["den"], 2 * h + 2)
                    dve.reciprocal(RD[SEG:P, :], RD[SEG:P, :]).then_inc(s["rden"], 1)
                    dve.wait_ge(s["rden"], h + 1)
                    dve.wait_ge(s["p_free"], h + 1)
                    for g in range(2):
                        dve.tensor_tensor(PR[SEG:P, g * HB:(g + 1) * HB, 0:SEG], lin[g][:, :, 0:SEG],
                                          bcast(RD[SEG:P, g * HB:(g + 1) * HB], 2, SEG), ALU.mult).then_inc(s["p_mem"], 1)
                    dve.wait_ge(s["exped"], h + 1)
                    dve.tensor_reduce(RS[:, :], EX[:, :, :], AX.X, ALU.add).then_inc(s["summed"], 1)
                    dve.wait_ge(s["summed"], h + 1)
                    dve.reciprocal(RS[:, :], RS[:, :]).then_inc(s["rsum"], 1)
                    dve.wait_ge(s["rsum"], h + 1)
                    dve.tensor_tensor(PR[0:SEG, :, 0:SEG], EX[0:SEG, :, :], bcast(RS[0:SEG, :], 2, SEG), ALU.mult).then_inc(s["p_mem"], 1)
                    dve.wait_ge(s["pt_done"], 2 * h + 2)
                    dve.tensor_copy(PTS[:, HB:B, :], AD[1][:, :].rearrange("p (b t) -> p b t", b=HB)).then_inc(s["pts1"], 1)
                    if nxt:
                        sigma(h + 1)
                        evac_v(h + 1, 1 - p)

                def add_out():
                    for q in range(B // 2):
                        dve.wait_ge(s["out_done"], q + 1)
                        xs = c.X[:, 2 * q:2 * q + 2, :]
                        dve.tensor_tensor(xs, xs, OB[q % 2][:, :].rearrange("p (b n) -> p b n", b=2), ALU.add).then_inc(s["x_add"], 1)
                        dve.wait_ge(s["x_add"], q + 1)
                        norm.stats(dve, q)
                        norm.scale(dve, q)

                dve.sem_inc(s["s_free"], 1)
                dve.sem_inc(s["pts1"], 1)
                dve.wait_ge(s["const"], 2)
                dve.wait_ge(c.s["beta"], 1)
                dve.tensor_scalar(BTC[0:SEG, :, :], BTM[0:SEG, :, :], -1.0, 1.0, ALU.mult, ALU.add).then_inc(s["beta_c"], 1)
                sigma(0)
                dve.wait_ge(s["beta_c"], 1)
                evac_v(0, 0)
                with dve.Fori(0, H0 // 2 - 1) as j:
                    head(2 * j, 0)
                    head(2 * j + 1, 1)
                head(H0 - 2, 0)
                head(H0 - 1, 1, False)
                add_out()


def later_weights(nc, c, st):
    c.WT = sb(nc, st, "at_wt", [P, KC, 3 * D])
    c.WOT = sb(nc, st, "at_wot", [P, KC, D])
    c.QWT = sb(nc, st, "cr_qwt", [P, 1, S])
    c.KWT = sb(nc, st, "cr_kwt", [P, 1, S])
    c.VWT = sb(nc, st, "cr_vwt", [P, 1, S])
    c.WG = [sb(nc, st, f"sw_wg{n}", [P, KC, HID], F32R) for n in range(2)]
    c.WU = [sb(nc, st, f"sw_wu{n}", [P, KC, HID], F32R) for n in range(2)]
    c.WD = [sb(nc, st, f"sw_wd{n}", [P, MC, D], F32R) for n in range(2)]
    c.ROUTER = sb(nc, st, "mo_wg", [P, KC, E0])
    c.B1R = sb(nc, st, "mo_b1r", [E0 * MC, P])
    c.jobs = [(c.wqkv, 3 * KC, KC, c.WT), (c.wout, KC, KC, c.WOT), (c.QW, 1, 1, c.QWT), (c.KW, 1, 1, c.KWT),
              (c.VW, 1, 1, c.VWT), (c.wgate, MC, KC, c.WG), (c.wup, MC, KC, c.WU), (c.wdown, KC, MC, c.WD)]
    c.raw = [sb(nc, st, f"raw{i}", [P, r, k * P]) for i, (_, r, k, _) in enumerate(c.jobs)]
    c.raw_ld = [st.enter_context(nc.semaphore(f"raw_ld{i}")) for i in range(len(c.jobs))]
    c.groups = []
    for i, (_, r, k, _) in enumerate(c.jobs):
        nk = min(k, 2 if r > 2 else 4)
        nr = min(r, 4 // nk)
        c.groups += [(i, k0, nk, r0, nr) for r0 in range(0, r, nr) for k0 in range(0, k, nk)]


def load_later_weights(sp, c):
    sp.dma_start(c.ROUTER[:, :, :], c.wg.rearrange("(k p) e -> p k e", p=P)).then_inc(c.s["router_ld"], 16)
    sp.dma_start(c.B1R[:, :], c.fc1b.rearrange("e (m p) -> (e m) p", p=P)).then_inc(c.s["b1_ld"], 16)
    for i, (src, r, k, _) in enumerate(c.jobs):
        sp.dma_start(c.raw[i][:, :, :], src.rearrange("(r p) d -> p r d", p=P)).then_inc(c.raw_ld[i], 16)


def turn_weights(pe, c, s):
    for g, (i, k0, nk, r0, nr) in enumerate(c.groups):
        if g >= 4:
            pe.wait_ge(s["w_out"], g - 3)
        pe.wait_ge(c.raw_ld[i], 16)
        for k in range(nk):
            for r in range(nr):
                mm = pe.transpose(c.bank[4 + g % 4][:, (k * nr + r) * P:(k * nr + r + 1) * P],
                                  c.raw[i][:, r0 + r, (k0 + k) * P:(k0 + k + 1) * P], c.IDN[:, :])
        mm.then_inc(s["w_turned"], 1)


def group_views(c, g, dst):
    i, k0, nk, r0, nr = c.groups[g]
    return (dst[:, k0:k0 + nk, r0 * P:(r0 + nr) * P],
            c.bank[4 + g % 4][:, 0:nk * nr * P].rearrange("p (k t) -> p k t", k=nk))


def turned_high(act, c, s):
    for g, group in enumerate(c.groups):
        dst = c.jobs[group[0]][3]
        if isinstance(dst, list):
            act.wait_ge(s["w_turned"], g + 1)
            act.activation(*group_views(c, g, dst[0]), ACT.Copy).then_inc(s["w_high"], 1)


def turned_rest(dve, c, s):
    n = 0
    for g, group in enumerate(c.groups):
        dst = c.jobs[group[0]][3]
        if isinstance(dst, list):
            n += 1
            dve.wait_ge(s["w_high"], n)
            low, turned = group_views(c, g, dst[1])
            dve.tensor_tensor(low, turned, group_views(c, g, dst[0])[0].bitcast(F32), ALU.subtract).then_inc(s["w_out"], 1)
        else:
            dve.wait_ge(s["w_turned"], g + 1)
            dve.tensor_copy(*group_views(c, g, dst)).then_inc(s["w_out"], 1)


def long_conv(nc, c):
    with ExitStack() as st:
        s = sems(nc, st, "lc_", "toe_ld0 toe_ld1 d_ld anti rev turned_c cr_ev toe0 toe1 kv y0 y1 prod red turned_o x_add")
        norm = Norm(nc, c, st, "ln3_")
        TOE = sb(nc, st, "lc_toe", [P, HC, D])
        TB = [sb(nc, st, f"lc_tb{p}", [P, D]) for p in range(2)]
        DB = sb(nc, st, "lc_d", [P, HC])
        ANTI = sb(nc, st, "lc_anti", [P, P])
        CR = sb(nc, st, "lc_cr", [P, KC, B, S])
        CREV = sb(nc, st, "lc_crev", [P, B, D])
        KV = [sb(nc, st, f"lc_kv{p}", [P, KC, B, HD, HD]) for p in range(2)]
        PD = sb(nc, st, "lc_pd", [P, KC, B, HD * HD])
        OT = sb(nc, st, "lc_ot", [P, KC, B, S])
        with nc.Block() as block:
            @block.sync
            def _(sp):
                sp.wait_ge(c.s["pad_st"], 32)
                for n, (h0, h1) in enumerate(((0, 2), (2, HC))):
                    sp.dma_start(TOE[:, h0:h1, :], bass.AP(tensor=c.pad.tensor, offset=384 * h0, ap=[[1, P], [384, h1 - h0], [1, D]])
                                 ).then_inc((s["toe_ld0"], s["toe_ld1"])[n], 16)
                sp.dma_start(DB[:, :], c.convD.rearrange("(a h) -> a h", a=1).broadcast_to([P, HC])).then_inc(s["d_ld"], 16)
                load_later_weights(sp, c)

            @block.gpsimd
            def _(pool):
                pool.memset(ANTI[:, :], 0.0).then_inc(s["anti"], 1)
                pool.wait_ge(s["anti"], 1)
                pool.affine_select(out=ANTI[:, :], in_=ANTI[:, :], compare_op=ALU.not_equal, fill=1.0,
                                   base=1 - P, pattern=[[1, P]], channel_multiplier=1).then_inc(s["anti"], 1)
                pool.wait_ge(s["cr_ev"], 8)

                pool.sem_inc(s["y1"], 2)
                with pool.Fori(0, HC // 2) as j:
                    for p in range(2):
                        h = 2 * j + p
                        pool.wait_ge(s["y1"], h + 1)
                        for k in range(KC):
                            pool.wait_ge(s["cr_ev"], 8)
                            v = CR[:, k, :, bass.ds(HD * h, HD)]
                            pool.tensor_tensor(KV[p][:, k, :, :, :], bcast(v, 3, HD), bcast(v, 2, HD), ALU.mult).then_inc(s["kv"], 1)

            @block.scalar
            def _(act):
                for g in range(0, 4):
                    act.wait_ge(s["turned_c"], g + 1)
                    act.activation(CR[:, :, 2 * g:2 * g + 2, :], c.bank[g][:, :].rearrange("p (k b t) -> p k b t", k=KC, b=2), ACT.Copy).then_inc(s["cr_ev"], 2)

                def toeplitz(h, p):
                    act.wait_ge(s["y1"], h + 1)
                    src = TOE[:, h, P:D] if isinstance(h, int) else TOE[:, bass.ds(h, 1), P:D].squeeze(1)
                    act.activation(TB[p][:, P:D], src, ACT.Copy).then_inc(s["toe1"], 1)

                act.wait_ge(s["toe_ld0"], 16)
                toeplitz(0, 0)
                toeplitz(1, 1)
                act.wait_ge(s["toe_ld1"], 16)
                with act.Fori(1, HC // 2) as j:
                    for p in range(2):
                        toeplitz(2 * j + p, p)
                for q in range(B // 2):
                    norm.root(act, q)
                for q in range(B // 2):
                    norm.copy(act, q, c.bank[q])

            @block.tensor
            def _(pe):
                for g in range(4):
                    pe.wait_ge(s["rev"], 2 * g + 2)
                    for i in range(2):
                        for k in range(KC):
                            mm = pe.transpose(c.bank[g][:, (2 * k + i) * S:(2 * k + i + 1) * S],
                                              CREV[:, 2 * g + i, k * P:(k + 1) * P], c.IDN[:, :])
                    mm.then_inc(s["turned_c"], 1)
                pe.wait_ge(s["cr_ev"], 8)
                with pe.Fori(0, HC // 2) as j:
                    for p in range(2):
                        h = 2 * j + p
                        y = [c.bank[2 * p], c.bank[2 * p + 1]]
                        kv = [KV[p][:, k, :, :, :].rearrange("p b j i -> p (b j i)") for k in range(KC)]
                        pe.wait_ge(s["kv"], 2 * h + 2)
                        pe.wait_ge(s["toe0"], h + 1)
                        pe.wait_ge(s["toe1"], h + 1)
                        pe.wait_ge(s["prod"], 2 * h + 1)
                        pe.matmul(y[0][:, :], TB[p][:, 0:P], kv[0], start=True, stop=True).then_inc(s["y0"], 1)
                        pe.wait_ge(s["prod"], 2 * h + 2)
                        pe.matmul(y[1][:, :], TB[p][:, P:D], kv[0], start=True, stop=False)
                        pe.matmul(y[1][:, :], TB[p][:, 0:P], kv[1], start=False, stop=True).then_inc(s["y1"], 1)
                pe.wait_ge(s["red"], 2 * HC + 2)
                for q in range(B // 2):
                    for i in range(2):
                        for k in range(KC):
                            mm = pe.transpose(c.bank[4 + q][:, i * D + k * P:i * D + (k + 1) * P], OT[:, k, 2 * q + i, :], c.IDN[:, :])
                    mm.then_inc(s["turned_o"], 1)
                for q in range(B // 2):
                    norm.turn(pe, q, c.bank[q])

            @block.vector
            def _(dve):
                dve.wait_ge(c.s["ctx_loaded"], 16)
                for b in range(B):
                    src = c.CTX[:, b, :].rearrange("p (k t) -> p k t", k=KC)[:, :, ::-1]
                    dve.tensor_copy(CREV[:, b, :].rearrange("p (k t) -> p k t", k=KC), src).then_inc(s["rev"], 1)
                dve.wait_ge(s["anti"], 2)
                dve.wait_ge(s["toe_ld0"], 16)
                dve.wait_ge(s["d_ld"], 16)
                dve.sem_inc(s["prod"], 4)
                dve.sem_inc(s["red"], 2)

                def toeplitz(h, p):
                    dve.wait_ge(s["y1"], h + 1)
                    at, d = (TOE[:, h, 0:P], DB[:, h:h + 1]) if isinstance(h, int) else \
                        (TOE[:, bass.ds(h, 1), 0:P].squeeze(1), DB[:, bass.ds(h, 1)])
                    dve.scalar_tensor_tensor(TB[p][:, 0:P], ANTI[:, :], d, at, ALU.mult, ALU.add).then_inc(s["toe0"], 1)

                q = c.XNT[:, :, :].rearrange("p k (b t) -> p k b t", b=B)

                def head(h, p, more=True):
                    rows = slice(HD * h, HD * h + HD) if isinstance(h, int) else bass.ds(HD * h, HD)
                    pd = [PD[:, k, :, :].rearrange("p b (j i) -> p b j i", j=HD) for k in range(KC)]
                    for k in range(KC):
                        dve.wait_ge(s["red"], 2 * h + k + 1)
                        dve.wait_ge((s["y0"], s["y1"])[k], h + 1 + 2 * k)
                        dve.tensor_tensor(pd[k], c.bank[2 * p + k][:, :].rearrange("p (b j i) -> p b j i", b=B, j=HD),
                                          bcast(q[:, k, :, rows], 2, HD), ALU.mult).then_inc(s["prod"], 1)
                    if more:
                        toeplitz(h + 2, p)
                    for k in range(KC):
                        dve.wait_ge(s["prod"], 2 * h + k + 5)
                        dve.tensor_reduce(OT[:, k, :, rows], pd[k], AX.X, ALU.add).then_inc(s["red"], 1)

                toeplitz(0, 0)
                toeplitz(1, 1)
                dve.wait_ge(s["toe_ld1"], 16)
                with dve.Fori(0, HC // 2 - 1) as j:
                    head(2 * j, 0)
                    head(2 * j + 1, 1)
                head(HC - 2, 0, False)
                head(HC - 1, 1, False)
                for g in range(B // 2):
                    dve.wait_ge(s["turned_o"], g + 1)
                    xs = c.X[:, 2 * g:2 * g + 2, :]
                    dve.tensor_tensor(xs, xs, c.bank[4 + g][:, :].rearrange("p (b n) -> p b n", b=2), ALU.add).then_inc(s["x_add"], 1)
                    dve.wait_ge(s["x_add"], g + 1)
                    norm.stats(dve, g)
                    if g:
                        norm.scale(dve, g - 1)
                norm.scale(dve, B // 2 - 1)


def moe(nc, c):
    NB = TOPK * B
    with ExitStack() as st:
        G = sb(nc, st, "mo_gate", [P, TOPK, B])
        GIX = sb(nc, st, "mo_gix", [P, TOPK, B], I32)
        w = sems(nc, st, "mw_", "f1 f2 bias0 bias1 ld0 ld1")
        F1 = [sb(nc, st, f"mo_f1{p}", [P, KC, HID]) for p in range(2)]
        F2 = [sb(nc, st, f"mo_f2{p}", [P, MC, D]) for p in range(2)]
        B1 = sb(nc, st, "mo_b1", [P, E0 * MC])
        B2 = [sb(nc, st, f"mo_b2{p}", [P, D]) for p in range(2)]
        fc1 = c.fc1.rearrange("e (k p) n -> e p k n", p=P)
        fc2 = c.fc2.rearrange("e (m p) n -> e p m n", p=P)

        def load_expert(sp, e, p):
            pick = (lambda a: a[e]) if isinstance(e, int) else (lambda a: a[bass.ds(e, 1)].squeeze(0))
            sp.dma_start(F1[p][:, :, :], pick(fc1)).then_inc((w["ld0"], w["ld1"])[p], 16)
            sp.dma_start(F2[p][:, :, :], pick(fc2)).then_inc((w["ld0"], w["ld1"])[p], 16)
            row = c.fc2b[e:e + 1, :] if isinstance(e, int) else c.fc2b[bass.ds(e, 1), :]
            sp.dma_start(B2[p][:, :], row.broadcast_to([P, D])).then_inc((w["ld0"], w["ld1"])[p], 16)

        route(nc, c, B1, G, GIX, lambda sp: [load_expert(sp, p, p) for p in range(2)])
        experts(nc, c, F1, F2, B1, B2, w, load_expert)
        combine(nc, c, G, GIX)


def route(nc, c, B1, G, GIX, first_loads):
    NB = TOPK * B
    with ExitStack() as st:
        s = sems(nc, st, "mr_", "w_out w_high w_turned b1_t const logits lg maxed shifted exped summed rsum prob top idx idxf onehot "
                 "gsum gsafe grec gate0 counted tot scan base pos0 pos1 pos valid slot0 slot1 big pv0 pv1 ready")
        TRI = sb(nc, st, "mr_tri", [P, P])
        ONES = sb(nc, st, "mr_ones", [P, P])
        IOTA = sb(nc, st, "mr_iota", [P, E0])
        RST = sb(nc, st, "mr_rst", [P, E0, NB])
        PRB = sb(nc, st, "mr_prb", [P, B, E0])
        MX = sb(nc, st, "mr_mx", [P, B])
        SU = sb(nc, st, "mr_su", [P, B])
        V8 = sb(nc, st, "mr_v8", [P, B, 8])
        I8 = sb(nc, st, "mr_i8", [P, B, 8], U32)
        EID = sb(nc, st, "mr_eid", [P, TOPK, B])
        OH = sb(nc, st, "mr_oh", [P, TOPK, B, E0])
        TOT = sb(nc, st, "mr_tot", [P, E0, NB])
        SCN = sb(nc, st, "mr_scn", [P, E0, NB])
        POE = sb(nc, st, "mr_poe", [P, NB, E0])
        POS = sb(nc, st, "mr_pos", [P, NB])
        VAL = sb(nc, st, "mr_val", [P, NB])
        SLT = sb(nc, st, "mr_slt", [P, NB])
        SLG = sb(nc, st, "mr_slg", [P, NB])
        SIX = sb(nc, st, "mr_six", [P, NB], I32)
        LGB, PRE, TTB = c.bank[0], c.bank[1], c.bank[2]
        with nc.Block() as block:
            @block.sync
            def _(sp):
                first_loads(sp)

            @block.gpsimd
            def _(pool):
                pool.memset(TRI[:, :], 1.0).then_inc(s["const"], 1)
                pool.memset(ONES[:, :], 1.0).then_inc(s["const"], 1)
                pool.memset(RST[:, :, :], 1.0).then_inc(s["const"], 1)
                pool.iota(IOTA[:, :], [[1, E0]], base=0, channel_multiplier=0,
                          allow_small_or_imprecise_dtypes=True).then_inc(s["const"], 1)
                pool.wait_ge(s["const"], 4)
                pool.memset(RST[:, :, 0:1], 0.0).then_inc(s["const"], 1)
                pool.affine_select(out=TRI[:, :], in_=TRI[:, :], compare_op=ALU.is_gt, fill=0.0, base=0,
                                   pattern=[[1, P]], channel_multiplier=-1).then_inc(s["const"], 1)
                pool.wait_ge(s["ready"], 2)
                pool.wait_ge(c.s["disp_zeroed"], 16 * E0)
                for n in range(NB):
                    pool.indirect_dma_start(c.disp, bass.IndirectOffsetOnAxis(ap=SIX[:, n:n + 1], axis=0), c.XN[:, n % B, :], None,
                                            bounds_check=E0 * CAP - 1, oob_is_err=False).then_inc(c.s["scattered"], 16)
                pool.wait_ge(c.s["scattered"], 16 * NB)

            @block.scalar
            def _(act):
                act.wait_ge(s["shifted"], 1)
                act.activation(PRB[:, :, :], PRB[:, :, :], ACT.Exp).then_inc(s["exped"], 1)
                act.wait_ge(s["b1_t"], 1)
                act.activation(B1[:, :], c.bank[3][:, 0:E0 * MC], ACT.Copy)
                turned_high(act, c, s)

            @block.tensor
            def _(pe):
                pe.wait_ge(c.s["router_ld"], 16)
                for b in range(B):
                    for k in range(KC):
                        mm = pe.matmul(LGB[:, b * E0:(b + 1) * E0], c.XNT[:, k, b * S:(b + 1) * S], c.ROUTER[:, k, :],
                                       start=(k == 0), stop=(k == KC - 1))
                mm.then_inc(s["logits"], 1)
                pe.wait_ge(c.s["b1_ld"], 16)
                pe.transpose(c.bank[3][:, 0:E0 * MC], c.B1R[:, :], c.IDN[0:E0 * MC, 0:E0 * MC]).then_inc(s["b1_t"], 1)
                pe.wait_ge(s["const"], 6)
                pe.wait_ge(s["onehot"], 2)
                oh = OH[:, :, :, :].rearrange("p s b e -> p (s b e)")
                pe.matmul(PRE[:, 0:NB * E0], TRI[:, :], oh, start=True, stop=True).then_inc(s["counted"], 1)
                pe.matmul(TTB[:, 0:NB * E0], ONES[:, :], oh, start=True, stop=True).then_inc(s["counted"], 1)
                turn_weights(pe, c, s)

            @block.vector
            def _(dve):
                dve.wait_ge(s["logits"], 1)
                lg = LGB[:, 0:B * E0].rearrange("p (b e) -> p b e", b=B)
                dve.tensor_reduce(MX[:, :], lg, AX.X, ALU.max).then_inc(s["maxed"], 1)
                dve.wait_ge(s["maxed"], 1)
                dve.tensor_tensor(PRB[:, :, :], lg, bcast(MX[:, :], 2, E0), ALU.subtract).then_inc(s["shifted"], 1)
                dve.wait_ge(s["exped"], 1)
                dve.tensor_reduce(SU[:, :], PRB[:, :, :], AX.X, ALU.add).then_inc(s["summed"], 1)
                dve.wait_ge(s["summed"], 1)
                dve.reciprocal(SU[:, :], SU[:, :]).then_inc(s["rsum"], 1)
                dve.wait_ge(s["rsum"], 1)
                dve.tensor_tensor(PRB[:, :, :], PRB[:, :, :], bcast(SU[:, :], 2, E0), ALU.mult).then_inc(s["prob"], 1)
                dve.wait_ge(s["prob"], 1)
                for b in range(B):
                    dve.max(V8[:, b, :], PRB[:, b, :]).then_inc(s["top"], 1)
                for b in range(B):
                    dve.wait_ge(s["top"], b + 1)
                    dve.max_index(I8[:, b, :], V8[:, b, :], PRB[:, b, :]).then_inc(s["idx"], 1)
                dve.wait_ge(s["idx"], B)
                dve.wait_ge(s["const"], 6)
                for t in range(TOPK):
                    dve.tensor_copy(EID[:, t, :], I8[:, :, t]).then_inc(s["idxf"], 1)
                for t in range(TOPK):
                    dve.wait_ge(s["idxf"], t + 1)
                    dve.tensor_tensor(OH[:, t, :, :], bcast(IOTA[:, :], 1, B), bcast(EID[:, t, :], 2, E0), ALU.is_equal).then_inc(s["onehot"], 1)
                dve.tensor_tensor(MX[:, :], V8[:, :, 0], V8[:, :, 1], ALU.add).then_inc(s["gsum"], 1)
                dve.wait_ge(s["gsum"], 1)
                dve.tensor_scalar(MX[:, :], MX[:, :], 1e-9, None, ALU.max).then_inc(s["gsafe"], 1)
                dve.wait_ge(s["gsafe"], 1)
                dve.reciprocal(MX[:, :], MX[:, :]).then_inc(s["grec"], 1)
                dve.wait_ge(s["grec"], 1)
                for t in range(TOPK):
                    dve.tensor_tensor(G[:, t, :], V8[:, :, t], MX[:, :], ALU.mult).then_inc(s["gate0"], 1)
                dve.wait_ge(s["counted"], 2)
                tot = TTB[:, 0:NB * E0].rearrange("p (n e) -> p e n", e=E0)
                dve.tensor_copy(TOT[:, :, :], tot).then_inc(s["tot"], 1)
                dve.wait_ge(s["tot"], 1)
                flat = [a[:, :, :].rearrange("p e n -> p (e n)") for a in (SCN, RST, TOT)]
                dve.tensor_tensor_scan(flat[0], flat[1], flat[2], 0.0, ALU.mult, ALU.add).then_inc(s["scan"], 1)
                dve.wait_ge(s["scan"], 1)
                dve.tensor_tensor(SCN[:, :, :], SCN[:, :, :], TOT[:, :, :], ALU.subtract).then_inc(s["base"], 1)
                dve.wait_ge(s["base"], 1)
                dve.tensor_tensor(POE[:, :, :], PRE[:, 0:NB * E0].rearrange("p (n e) -> p n e", e=E0),
                                  SCN[:, :, :].rearrange("p e n -> p n e"), ALU.add).then_inc(s["pos0"], 1)
                dve.wait_ge(s["pos0"], 1)
                dve.tensor_tensor(POE[:, :, :], POE[:, :, :], OH[:, :, :, :].rearrange("p s b e -> p (s b) e"), ALU.mult).then_inc(s["pos1"], 1)
                dve.wait_ge(s["pos1"], 1)
                dve.tensor_reduce(POS[:, :], POE[:, :, :], AX.X, ALU.add).then_inc(s["pos"], 1)
                dve.wait_ge(s["pos"], 1)
                dve.tensor_scalar(VAL[:, :], POS[:, :], float(CAP), None, ALU.is_lt).then_inc(s["valid"], 1)
                eid = EID[:, :, :].rearrange("p s b -> p (s b)")
                dve.scalar_tensor_tensor(SLT[:, :], eid, float(CAP), POS[:, :], ALU.mult, ALU.add).then_inc(s["slot0"], 1)
                dve.wait_ge(s["valid"], 1)
                dve.tensor_tensor(SLG[:, :], POS[:, :], VAL[:, :], ALU.mult).then_inc(s["pv0"], 1)
                dve.wait_ge(s["pv0"], 1)
                dve.scalar_tensor_tensor(SLG[:, :], eid, float(CAP), SLG[:, :], ALU.mult, ALU.add).then_inc(s["pv1"], 1)
                dve.wait_ge(s["gate0"], TOPK)
                g = G[:, :, :].rearrange("p s b -> p (s b)")
                dve.tensor_tensor(g, g, VAL[:, :], ALU.mult).then_inc(s["gate0"], 1)
                dve.wait_ge(s["gate0"], TOPK + 1)
                dve.tensor_scalar(VAL[:, :], VAL[:, :], -float(BIG), float(BIG), ALU.mult, ALU.add).then_inc(s["big"], 1)
                dve.wait_ge(s["big"], 1)
                dve.wait_ge(s["slot0"], 1)
                dve.tensor_tensor(SLT[:, :], SLT[:, :], VAL[:, :], ALU.add).then_inc(s["slot1"], 1)
                dve.wait_ge(s["slot1"], 1)
                dve.tensor_copy(SIX[:, :], SLT[:, :]).then_inc(s["ready"], 1)
                dve.wait_ge(s["pv1"], 1)
                dve.tensor_copy(GIX[:, :, :].rearrange("p s b -> p (s b)"), SLG[:, :]).then_inc(s["ready"], 1)
                turned_rest(dve, c, s)


def experts(nc, c, F1, F2, B1, B2, w, load_expert):
    CT = CAP // P
    with ExitStack() as st:
        s = sems(nc, st, "me_", "in0 in1 xt_done xt_ev h_done h_ev o_done o_ev")
        XE = [sb(nc, st, f"me_xe{p}", [P, CT, D]) for p in range(2)]
        XET = sb(nc, st, "me_xet", [P, KC, CAP])
        HT = sb(nc, st, "me_ht", [P, MC, CAP])
        EO = [sb(nc, st, f"me_eo{p}", [P, CT, D]) for p in range(2)]
        disp = c.disp.rearrange("(e t p) d -> e p t d", p=P, t=CT)
        eo = c.eo.rearrange("(e t p) d -> e p t d", p=P, t=CT)
        XTB, OB = c.bank[0], c.bank[5]
        HB = [c.bank[1], c.bank[2], c.bank[3], c.bank[4]]
        pick = lambda a, e: a[e] if isinstance(e, int) else a[bass.ds(e, 1)].squeeze(0)
        with nc.Block() as block:
            @block.sync
            def _(sp):
                for p in range(2):
                    sp.dma_start(XE[p][:, :, :], pick(disp, p)).then_inc((s["in0"], s["in1"])[p], 16)
                with sp.Fori(1, E0 // 2) as j:
                    for p in range(2):
                        sp.wait_ge(s["xt_done"], 2 * j + p - 1)
                        sp.dma_start(XE[p][:, :, :], pick(disp, 2 * j + p)).then_inc((s["in0"], s["in1"])[p], 16)
                        sp.wait_ge(s["o_ev"], 2 * j + p)
                        load_expert(sp, 2 * j + p, p)

            @block.gpsimd
            def _(pool):
                with pool.Fori(0, E0 // 2) as j:
                    for p in range(2):
                        pool.wait_ge(s["o_ev"], 2 * j + p + 2)
                        pool.dma_start(pick(eo, 2 * j + p), EO[p][:, :, :]).then_inc((c.s["st0"], c.s["st1"])[p], 16)
                for p in range(2):
                    pool.wait_ge((c.s["st0"], c.s["st1"])[p], 16 * (E0 // 2))

            @block.tensor
            def _(pe):
                def turn(e, p, n):
                    pe.wait_ge((s["in0"], s["in1"])[p], 16 * n)
                    pe.wait_ge(s["xt_ev"], e + 1)
                    for k in range(KC):
                        for t in range(CT):
                            mm = pe.transpose(XTB[:, k * CAP + t * P:k * CAP + (t + 1) * P], XE[p][:, t, k * P:(k + 1) * P], c.IDN[:, :])
                    mm.then_inc(s["xt_done"], 1)

                def expert(e, p, n, nxt=True):
                    pe.wait_ge((w["ld0"], w["ld1"])[p], 48 * n)
                    pe.wait_ge(s["xt_ev"], e + 2)
                    for q in range(MC // 2):
                        pe.wait_ge(s["h_ev"], 8 * e + 2 * q + 2)
                        for i in range(2):
                            m = 2 * q + i
                            for k in range(KC):
                                mm = pe.matmul(HB[q][:, i * CAP:(i + 1) * CAP], F1[p][:, k, m * P:(m + 1) * P], XET[:, k, :],
                                               start=(k == 0), stop=(k == KC - 1))
                        mm.then_inc(s["h_done"], 1)
                    if nxt:
                        turn(e + 1, 1 - p, n + p)
                    pe.wait_ge(s["h_ev"], 8 * e + 16)
                    pe.wait_ge(s["o_ev"], e + 1)
                    for t in range(CT):
                        for m in range(MC):
                            mm = pe.matmul(OB[:, t * D:(t + 1) * D], HT[:, m, t * P:(t + 1) * P], F2[p][:, m, :],
                                           start=(m == 0), stop=(m == MC - 1))
                    mm.then_inc(s["o_done"], 1)

                turn(0, 0, 1)
                with pe.Fori(0, E0 // 2 - 1) as j:
                    expert(2 * j, 0, j + 1)
                    expert(2 * j + 1, 1, j + 1)
                expert(E0 - 2, 0, E0 // 2)
                expert(E0 - 1, 1, E0 // 2, False)

            @block.scalar
            def _(act):
                act.sem_inc(s["xt_ev"], 1)
                act.sem_inc(s["h_ev"], 8)

                def turned(e):
                    act.wait_ge(s["xt_done"], e + 1)
                    act.activation(XET[:, :, :], XTB[:, :].rearrange("p (k t) -> p k t", k=KC), ACT.Copy).then_inc(s["xt_ev"], 1)

                def expert(e, p, nxt=True):
                    for m in range(MC):
                        act.wait_ge(s["h_done"], 4 * e + m // 2 + 1)
                        act.activation(HT[:, m, :], HB[m // 2][:, (m % 2) * CAP:(m % 2 + 1) * CAP], ACT.Gelu,
                                       bias=B1[:, e * MC + m:e * MC + m + 1] if isinstance(e, int) else B1[:, bass.ds(e * MC + m, 1)]).then_inc(s["h_ev"], 1)
                    if nxt:
                        turned(e + 1)

                turned(0)
                with act.Fori(0, E0 // 2 - 1) as j:
                    expert(2 * j, 0)
                    expert(2 * j + 1, 1)
                expert(E0 - 2, 0)
                expert(E0 - 1, 1, False)

            @block.vector
            def _(dve):
                def expert(e, p, n):
                    dve.wait_ge(s["o_done"], e + 1)
                    if n is not None:
                        dve.wait_ge((c.s["st0"], c.s["st1"])[p], 16 * n)
                    dve.tensor_tensor(EO[p][:, :, :], OB[:, :].rearrange("p (t n) -> p t n", t=CT),
                                      bcast(B2[p][:, :], 1, CT), ALU.add).then_inc(s["o_ev"], 1)

                dve.sem_inc(s["o_ev"], 1)
                for p in range(2):
                    expert(p, p, None)
                with dve.Fori(1, E0 // 2) as j:
                    for p in range(2):
                        expert(2 * j + p, p, j)


def combine(nc, c, G, GIX):
    with ExitStack() as st:
        s = sems(nc, st, "mc_", "x_add0 x_add1")
        norm = Norm(nc, c, st, "ln4_")
        got = c.got
        GA = sb(nc, st, "mc_ga", [P, B, TOPK, D])
        with nc.Block() as block:
            @block.gpsimd
            def _(pool):
                for b in range(B):
                    for t in range(TOPK):
                        pool.indirect_dma_start(GA[:, b, t, :], None, c.eo, bass.IndirectOffsetOnAxis(ap=GIX[:, t, b:b + 1], axis=0),
                                                bounds_check=E0 * CAP - 1, oob_is_err=False).then_inc(got[b], 16)

            @block.vector
            def _(dve):
                for b in range(B):
                    dve.wait_ge(got[b], 16 * TOPK)
                    dve.scalar_tensor_tensor(c.X[:, b, :], GA[:, b, 0, :], G[:, 0, b:b + 1], c.X[:, b, :], ALU.mult, ALU.add).then_inc(s["x_add0"], 1)
                    dve.wait_ge(s["x_add0"], b + 1)
                    dve.scalar_tensor_tensor(c.X[:, b, :], GA[:, b, 1, :], G[:, 1, b:b + 1], c.X[:, b, :], ALU.mult, ALU.add).then_inc(s["x_add1"], 1)
                    if b % 2:
                        dve.wait_ge(s["x_add1"], b + 1)
                        norm.stats(dve, b // 2)
                        norm.scale(dve, b // 2)

            @block.scalar
            def _(act):
                for q in range(B // 2):
                    norm.root(act, q)
                    if q:
                        norm.copy(act, q - 1, c.bank[q - 1])
                norm.copy(act, B // 2 - 1, c.bank[B // 2 - 1])

            @block.tensor
            def _(pe):
                for q in range(B // 2):
                    norm.turn(pe, q, c.bank[q])


def attention1(nc, c, norm):
    HPC = P // HD1
    VW = HD1 + 1
    with ExitStack() as st:
        WT, WOT = c.WT, c.WOT
        s = sems(nc, st, "at_", "bias_ld const xb qk_done qk_ev kx v_done v_ev sc_done masked maxed sub_d sub_p exped "
                 "pt_done pt_ev pv_done rsum norm ot_done ot_ev out_done x_add x_b")
        BQK = sb(nc, st, "at_bqk", [P, 4])
        BV = sb(nc, st, "at_bv", [P, D])
        BO = sb(nc, st, "at_bo", [P, D])
        OWN = sb(nc, st, "at_own", [P, HPC])
        MASK = sb(nc, st, "at_mask", [P, S])
        XB = [sb(nc, st, f"at_xb{p}", [P, KC, S]) for p in range(2)]
        QK = sb(nc, st, "at_qk", [P, 4, S])
        KX = sb(nc, st, "at_kx", [P, H1, S])
        VA = [sb(nc, st, f"at_v{p}", [P, H1, VW]) for p in range(2)]
        SM = [sb(nc, st, f"at_sm{p}", [P, H1, S]) for p in range(2)]
        MX = [sb(nc, st, f"at_mx{p}", [P, H1]) for p in range(2)]
        PT = sb(nc, st, "at_pt", [P, H1, S])
        RS = sb(nc, st, "at_rs", [P, H1])
        AO = sb(nc, st, "at_ao", [P, H1, HD1])
        AOT = sb(nc, st, "at_aot", [P, KC, S])
        SCB = c.bank[0:4]
        QKB, VOB = c.bank[4], c.bank[5]
        PTB = [c.bank[6], c.bank[7]]
        HH = H1 // 2
        with nc.Block() as block:
            @block.sync
            def _(sp):
                with nc.allow_non_contiguous_dma(reason="four columns"):
                    sp.dma_start(BQK[:, :], c.bqkv[0:2 * D].rearrange("(m p) -> p m", p=P)).then_inc(s["bias_ld"], 16)
                sp.dma_start(BV[:, :], c.bqkv[2 * D:3 * D].rearrange("(a n) -> a n", a=1).broadcast_to([P, D])).then_inc(s["bias_ld"], 16)
                sp.dma_start(BO[:, :], c.bout.rearrange("(a n) -> a n", a=1).broadcast_to([P, D])).then_inc(s["bias_ld"], 16)

            @block.gpsimd
            def _(pool):
                pool.memset(MASK[:, :], 0.0).then_inc(s["const"], 1)
                for p in range(2):
                    pool.memset(VA[p][:, :, HD1:VW], 1.0).then_inc(s["const"], 1)
                pool.wait_ge(s["const"], 3)
                pool.affine_select(out=MASK[:, :], in_=MASK[:, :], compare_op=ALU.is_ge, fill=NEG, base=0,
                                   pattern=[[-1, S]], channel_multiplier=1).then_inc(s["const"], 1)

                def take(b, p):
                    pool.wait_ge(s["const"], 3)
                    src = c.XNT[:, :, b * S:(b + 1) * S] if isinstance(b, int) else c.XNT[:, :, bass.ds(b * S, S)]
                    pool.tensor_copy(XB[p][:, :, :], src).then_inc(s["xb"], 1)

                def spread_keys(b):
                    pool.wait_ge(s["qk_ev"], 4 * b + 4)
                    if not isinstance(b, int) or b:
                        pool.wait_ge(s["sc_done"], b)
                    for ch in range(KC):
                        pool.tensor_tensor(KX[:, ch * HPC:(ch + 1) * HPC, :], bcast(QK[:, KC + ch, :], 1, HPC),
                                           bcast(OWN[:, :], 2, S), ALU.mult).then_inc(s["kx"], 1)

                def subtract(b, p):
                    pool.wait_ge(s["maxed"], b + 1)
                    pool.tensor_tensor(SM[p][:, HH:H1, :], SM[p][:, HH:H1, :], bcast(MX[p][:, HH:H1], 2, S), ALU.subtract).then_inc(s["sub_p"], 1)

                def batch(b, p, more=2, take_more=True):
                    if more > 1:
                        spread_keys(b + 2)
                    if more:
                        subtract(b + 1, 1 - p)
                    if take_more:
                        pool.wait_ge(s["v_done"], b + 2)
                        take(b + 3, 1 - p)

                take(0, 0)
                take(1, 1)
                pool.wait_ge(s["x_b"], 3)
                spread_keys(0)
                pool.wait_ge(s["v_done"], 1)
                take(2, 0)
                spread_keys(1)
                subtract(0, 0)
                with pool.Fori(0, B // 2 - 2) as j:
                    batch(2 * j, 0)
                    batch(2 * j + 1, 1)
                batch(B - 4, 0)
                batch(B - 3, 1, 2, False)
                batch(B - 2, 0, 1, False)

            @block.tensor
            def _(pe):
                def project_qk(b, p):
                    pe.wait_ge(s["xb"], b + 1)
                    if not isinstance(b, int) or b:
                        pe.wait_ge(s["qk_ev"], 4 * b)
                    for m in range(4):
                        for k in range(KC):
                            mm = pe.matmul(QKB[:, m * S:(m + 1) * S], WT[:, k, m * P:(m + 1) * P], XB[p][:, k, :],
                                           start=(k == 0), stop=(k == KC - 1))
                    mm.then_inc(s["qk_done"], 1)

                def project_v(b, p):
                    if isinstance(b, int) and b == 1:
                        pe.wait_ge(s["v_ev"], 1)
                    for k in range(KC):
                        mm = pe.matmul(PTB[0][:, 0:D], XB[p][:, k, :], WT[:, k, 2 * D:3 * D], start=(k == 0), stop=(k == KC - 1))
                    mm.then_inc(s["v_done"], 1)

                def scores(b):
                    pe.wait_ge(s["qk_ev"], 4 * b + 4)
                    pe.wait_ge(s["kx"], 2 * b + 2)
                    for j in range(4):
                        if not isinstance(b, int) or b:
                            pe.wait_ge(s["masked"], 4 * b + j - 3)
                        mm = pe.matmul(SCB[j][:, :], QK[:, j // 2, :], KX[:, 4 * j:4 * j + 4, :].rearrange("p h t -> p (h t)"),
                                       start=True, stop=True)
                    mm.then_inc(s["sc_done"], 1)

                def attend(b, p, v_next):
                    pe.wait_ge(s["v_ev"], b + 1 + v_next)
                    for g in range(4):
                        pe.wait_ge(s["exped"], 2 * b + 1 + g // 2)
                        pe.wait_ge(s["pt_ev"], 4 * b + g + 1)
                        for i in range(4):
                            mm = pe.transpose(PTB[g % 2][:, i * S:(i + 1) * S], SM[p][:, 4 * g + i, :], c.IDN[:, :])
                        mm.then_inc(s["pt_done"], 1)
                    pe.wait_ge(s["x_add"], b + 1)
                    for h in range(H1):
                        if h % 4 == 0:
                            pe.wait_ge(s["pt_ev"], 4 * b + h // 4 + 3)
                        mm = pe.matmul(VOB[:, h * VW:(h + 1) * VW], PT[:, h, :], VA[p][:, h, :], start=True, stop=True)
                    mm.then_inc(s["pv_done"], 1)

                def turn_result(b):
                    pe.wait_ge(s["norm"], b + 1)
                    for k in range(KC):
                        mm = pe.transpose(VOB[:, k * S:(k + 1) * S], AO[:, k * HPC:(k + 1) * HPC, :].rearrange("p h d -> p (h d)"), c.IDN[:, :])
                    mm.then_inc(s["ot_done"], 1)

                def output(b):
                    pe.wait_ge(s["ot_ev"], b + 1)
                    for k in range(KC):
                        mm = pe.matmul(VOB[:, 0:D], AOT[:, k, :], WOT[:, k, :], start=(k == 0), stop=(k == KC - 1))
                    mm.then_inc(s["out_done"], 1)

                def batch(b, p, more=2):
                    if more:
                        scores(b + 1)
                    if more > 1:
                        project_qk(b + 2, p)
                    attend(b, p, 1 if more else 0)
                    turn_result(b)
                    if more > 1:
                        project_v(b + 2, p)
                    output(b)

                pe.wait_ge(s["const"], 4)
                project_qk(0, 0)
                project_v(0, 0)
                scores(0)
                project_qk(1, 1)
                project_v(1, 1)
                with pe.Fori(0, B // 2 - 1) as j:
                    batch(2 * j, 0)
                    batch(2 * j + 1, 1)
                batch(B - 2, 0, 1)
                batch(B - 1, 1, 0)

            @block.scalar
            def _(act):
                act.sem_inc(s["pt_ev"], 2)
                act.wait_ge(s["bias_ld"], 48)

                def projected(b):
                    act.wait_ge(s["qk_done"], b + 1)
                    if not isinstance(b, int) or b > 0:
                        act.wait_ge(s["sc_done"], b)
                        act.wait_ge(s["kx"], 2 * b)
                    for m in (2, 3, 0, 1):
                        act.activation(QK[:, m, :], QKB[:, m * S:(m + 1) * S], ACT.Identity, bias=BQK[:, m:m + 1]).then_inc(s["qk_ev"], 1)

                def exps(b, p):
                    act.wait_ge(s["sub_d"], b + 1)
                    act.activation(SM[p][:, 0:HH, :], SM[p][:, 0:HH, :], ACT.Exp).then_inc(s["exped"], 1)
                    act.wait_ge(s["sub_p"], b + 1)
                    act.activation(SM[p][:, HH:H1, :], SM[p][:, HH:H1, :], ACT.Exp).then_inc(s["exped"], 1)

                def batch(b, p, more=2):
                    if more > 1:
                        projected(b + 2)
                    for g in range(4):
                        act.wait_ge(s["pt_done"], 4 * b + g + 1)
                        act.activation(PT[:, 4 * g:4 * g + 4, :], PTB[g % 2][:, :].rearrange("p (h t) -> p h t", h=4), ACT.Copy).then_inc(s["pt_ev"], 1)
                    act.wait_ge(s["ot_done"], b + 1)
                    act.activation(AOT[:, :, :], VOB[:, 0:KC * S].rearrange("p (k t) -> p k t", k=KC), ACT.Copy).then_inc(s["ot_ev"], 1)
                    if more:
                        exps(b + 1, 1 - p)

                projected(0)
                projected(1)
                exps(0, 0)
                with act.Fori(0, B // 2 - 1) as j:
                    batch(2 * j, 0)
                    batch(2 * j + 1, 1)
                batch(B - 2, 0, 1)
                batch(B - 1, 1, 0)

            @block.vector
            def _(dve):
                dve.sem_inc(s["x_add"], 1)
                dve.tensor_reduce(OWN[:, :], c.IDN[:, :].rearrange("p (h r) -> p h r", h=HPC), AX.X, ALU.add).then_inc(s["x_b"], 1)
                dve.wait_ge(s["bias_ld"], 48)
                dve.wait_ge(s["const"], 4)
                for g in range(2):
                    x = c.X[:, g * B // 2:(g + 1) * B // 2, :]
                    dve.tensor_tensor(x, x, bcast(BO[:, :], 1, B // 2), ALU.add).then_inc(s["x_b"], 1)
                dve.wait_ge(s["x_b"], 3)

                def values(b, p):
                    dve.wait_ge(s["v_done"], b + 1)
                    dve.tensor_tensor(VA[p][:, :, 0:HD1], PTB[0][:, 0:D].rearrange("p (h d) -> p h d", h=H1),
                                      BV[:, :].rearrange("p (h d) -> p h d", h=H1), ALU.add).then_inc(s["v_ev"], 1)

                def softmax(b, p):
                    dve.wait_ge(s["sc_done"], b + 1)
                    for j in range(4):
                        dve.scalar_tensor_tensor(SM[p][:, 4 * j:4 * j + 4, :], SCB[j][:, :].rearrange("p (h t) -> p h t", h=4),
                                                 float(HD1) ** -0.5, bcast(MASK[:, :], 1, 4), ALU.mult, ALU.add).then_inc(s["masked"], 1)
                    dve.wait_ge(s["masked"], 4 * b + 4)
                    dve.tensor_reduce(MX[p][:, :], SM[p][:, :, :], AX.X, ALU.max).then_inc(s["maxed"], 1)
                    dve.wait_ge(s["maxed"], b + 1)
                    dve.tensor_tensor(SM[p][:, 0:HH, :], SM[p][:, 0:HH, :], bcast(MX[p][:, 0:HH], 2, S), ALU.subtract).then_inc(s["sub_d"], 1)

                def batch(b, p, more=2):
                    if more:
                        softmax(b + 1, 1 - p)
                    dve.wait_ge(s["pv_done"], b + 1)
                    ov = VOB[:, 0:H1 * VW].rearrange("p (h d) -> p h d", h=H1)
                    dve.reciprocal(RS[:, :], ov[:, :, HD1]).then_inc(s["rsum"], 1)
                    dve.wait_ge(s["rsum"], b + 1)
                    dve.tensor_tensor(AO[:, :, :], ov[:, :, 0:HD1], bcast(RS[:, :], 2, HD1), ALU.mult).then_inc(s["norm"], 1)
                    if more > 1:
                        values(b + 2, p)
                    dve.wait_ge(s["out_done"], b + 1)
                    x = c.X[:, b, :] if isinstance(b, int) else c.X[:, bass.ds(b, 1), :].squeeze(1)
                    dve.tensor_tensor(x, x, VOB[:, 0:D], ALU.add).then_inc(s["x_add"], 1)
                    dve.wait_ge(s["x_add"], b + 2)
                    norm.moments(dve, b)

                values(0, 0)
                softmax(0, 0)
                values(1, 1)
                with dve.Fori(0, B // 2 - 1) as j:
                    batch(2 * j, 0)
                    batch(2 * j + 1, 1)
                batch(B - 2, 0, 1)
                batch(B - 1, 1, 0)


def cross1(nc, c, norm):
    LT = D // P
    with ExitStack() as st:
        QWT, KWT, VWT = c.QWT, c.KWT, c.VWT
        s = sems(nc, st, "cr_", "bias_ld cb q_done k_done v_done q_ev k_ev v_ev sc_done maxed negated exped "
                 "rsum norm pt_done pt_ev h_done x_add")
        BI = sb(nc, st, "cr_bi", [P, 3])
        CB = [sb(nc, st, f"cr_cb{p}", [P, D]) for p in range(2)]
        Q = sb(nc, st, "cr_q", [P, D])
        K = sb(nc, st, "cr_k", [P, D])
        V = [sb(nc, st, f"cr_v{p}", [P, LT, S]) for p in range(2)]
        PR = [sb(nc, st, f"cr_pr{p}", [P, LT, D]) for p in range(2)]
        MX = sb(nc, st, "cr_mx", [P, LT])
        NM = [sb(nc, st, f"cr_nm{p}", [P, LT]) for p in range(2)]
        RS = [sb(nc, st, f"cr_rs{p}", [P, LT]) for p in range(2)]
        PT = sb(nc, st, "cr_pt", [P, LT, D])
        QB, KB, VB, SB0, SB1, PTB, HB = c.bank[0], c.bank[1], c.bank[2], c.bank[3], c.bank[4], c.bank[5], c.bank[6]
        SCB = [SB0, SB1]
        with nc.Block() as block:
            @block.sync
            def _(sp):
                with nc.allow_non_contiguous_dma(reason="three columns"):
                    for i, bias in enumerate((c.Qb, c.Kb, c.Vb)):
                        sp.dma_start(BI[:, i:i + 1], bias.rearrange("(p a) -> p a", a=1)).then_inc(s["bias_ld"], 16)

            @block.gpsimd
            def _(pool):
                def take(b, p):
                    src = c.CTX[:, b, :] if isinstance(b, int) else c.CTX[:, bass.ds(b, 1), :].squeeze(1)
                    pool.tensor_copy(CB[p][:, :], src).then_inc(s["cb"], 1)

                pool.wait_ge(c.s["ctx_loaded"], 16)
                take(0, 0)
                take(1, 1)
                with pool.Fori(1, B // 2) as j:
                    for p in range(2):
                        pool.wait_ge(s["v_done"], 2 * j + p - 1)
                        take(2 * j + p, p)

            @block.tensor
            def _(pe):
                def project(b, p):
                    pe.wait_ge(s["cb"], b + 1)
                    xn = c.XN[:, b, :] if isinstance(b, int) else c.XN[:, bass.ds(b, 1), :].squeeze(1)
                    pe.wait_ge(s["q_ev"], b + 1)
                    pe.matmul(QB[:, 0:D], QWT[:, 0, :], xn, start=True, stop=True).then_inc(s["q_done"], 1)
                    pe.wait_ge(s["k_ev"], b + 1)
                    pe.matmul(KB[:, 0:D], KWT[:, 0, :], CB[p][:, :], start=True, stop=True).then_inc(s["k_done"], 1)
                    pe.wait_ge(s["v_ev"], b + 1)
                    for t in range(LT):
                        mm = pe.matmul(VB[:, t * S:(t + 1) * S], CB[p][:, t * P:(t + 1) * P], VWT[:, 0, :], start=True, stop=True)
                    mm.then_inc(s["v_done"], 1)

                def scores(b, p):
                    pe.wait_ge(s["q_ev"], b + 2)
                    pe.wait_ge(s["k_ev"], b + 2)
                    for t in range(LT):
                        mm = pe.matmul(SCB[p][:, t * D:(t + 1) * D], Q[:, t * P:(t + 1) * P], K[:, :], start=True, stop=True)
                    mm.then_inc(s["sc_done"], 1)

                def attend(b, p):
                    pe.wait_ge(s["norm"], 2 * b + 2)
                    pe.wait_ge(s["pt_ev"], b + 1)
                    for u in range(LT):
                        for t in range(LT):
                            mm = pe.transpose(PTB[:, u * D + t * P:u * D + (t + 1) * P], PR[p][:, t, u * P:(u + 1) * P], c.IDN[:, :])
                    mm.then_inc(s["pt_done"], 1)

                def output(b, p):
                    pe.wait_ge(s["pt_ev"], b + 2)
                    pe.wait_ge(s["v_ev"], b + 2)
                    pe.wait_ge(s["x_add"], b + 1)
                    for u in range(LT):
                        mm = pe.matmul(HB[:, 0:D], V[p][:, u, :], PT[:, u, :], start=(u == 0), stop=(u == LT - 1))
                    mm.then_inc(s["h_done"], 1)

                def batch(b, p, more=True):
                    if more:
                        project(b + 2, p)
                    attend(b, p)
                    if more:
                        scores(b + 2, p)
                    output(b, p)

                for b in range(2):
                    project(b, b)
                    scores(b, b)
                with pe.Fori(0, B // 2 - 1) as j:
                    batch(2 * j, 0)
                    batch(2 * j + 1, 1)
                batch(B - 2, 0, False)
                batch(B - 1, 1, False)

            @block.scalar
            def _(act):
                act.sem_inc(s["q_ev"], 1)
                act.sem_inc(s["k_ev"], 1)
                act.sem_inc(s["pt_ev"], 1)
                act.wait_ge(s["bias_ld"], 48)

                def project(b):
                    act.wait_ge(s["q_done"], b + 1)
                    if not isinstance(b, int) or b:
                        act.wait_ge(s["sc_done"], b)
                    act.activation(Q[:, :], QB[:, 0:D], ACT.Identity, bias=BI[:, 0:1]).then_inc(s["q_ev"], 1)
                    act.wait_ge(s["k_done"], b + 1)
                    act.activation(K[:, :], KB[:, 0:D], ACT.Identity, bias=BI[:, 1:2]).then_inc(s["k_ev"], 1)

                def exps(b, p):
                    act.wait_ge(s["negated"], b + 1)
                    for t in range(LT):
                        act.activation(PR[p][:, t, :], SCB[p][:, t * D:(t + 1) * D], ACT.Exp, bias=NM[p][:, t:t + 1],
                                       accum_out=RS[p][:, t:t + 1]).then_inc(s["exped"], 1)

                def batch(b, p, more=True):
                    if more:
                        project(b + 2)
                    act.wait_ge(s["pt_done"], b + 1)
                    act.activation(PT[:, :, :], PTB[:, :].rearrange("p (u q) -> p u q", u=LT), ACT.Copy).then_inc(s["pt_ev"], 1)
                    if more:
                        exps(b + 2, p)

                for b in range(2):
                    project(b)
                    exps(b, b)
                with act.Fori(0, B // 2 - 1) as j:
                    batch(2 * j, 0)
                    batch(2 * j + 1, 1)
                batch(B - 2, 0, False)
                batch(B - 1, 1, False)

            @block.vector
            def _(dve):
                dve.sem_inc(s["v_ev"], 1)
                dve.sem_inc(s["x_add"], 1)
                dve.wait_ge(s["bias_ld"], 48)

                def greatest(b, p):
                    dve.wait_ge(s["sc_done"], b + 1)
                    dve.tensor_reduce(MX[:, :], SCB[p][:, :].rearrange("p (t k) -> p t k", t=LT), AX.X, ALU.max).then_inc(s["maxed"], 1)
                    dve.wait_ge(s["maxed"], b + 1)
                    dve.tensor_scalar(NM[p][:, :], MX[:, :], -1.0, None, ALU.mult).then_inc(s["negated"], 1)

                def values(b, p):
                    dve.wait_ge(s["v_done"], b + 1)
                    dve.tensor_copy(V[p][:, :, :], VB[:, 0:LT * S].rearrange("p (t e) -> p t e", t=LT)).then_inc(s["v_ev"], 1)

                def normalise(b, p):
                    dve.wait_ge(s["exped"], 2 * b + 2)
                    dve.reciprocal(RS[p][:, :], RS[p][:, :]).then_inc(s["rsum"], 1)
                    dve.wait_ge(s["rsum"], b + 1)
                    for t in range(LT):
                        dve.tensor_scalar(PR[p][:, t, :], PR[p][:, t, :], RS[p][:, t:t + 1], None, ALU.mult).then_inc(s["norm"], 1)

                def add(b):
                    dve.wait_ge(s["h_done"], b + 1)
                    x = c.X[:, b, :] if isinstance(b, int) else c.X[:, bass.ds(b, 1), :].squeeze(1)
                    dve.scalar_tensor_tensor(x, HB[:, 0:D], BI[:, 2:3], x, ALU.add, ALU.add).then_inc(s["x_add"], 1)

                def batch(b, p, more=True):
                    if more:
                        greatest(b + 2, p)
                    add(b)
                    if more:
                        values(b + 2, p)
                        normalise(b + 2, p)
                    dve.wait_ge(s["x_add"], b + 2)
                    norm.moments(dve, b)

                for b in range(2):
                    values(b, b)
                    greatest(b, b)
                    normalise(b, b)
                with dve.Fori(0, B // 2 - 1) as j:
                    batch(2 * j, 0)
                    batch(2 * j + 1, 1)
                batch(B - 2, 0, False)
                batch(B - 1, 1, False)


def layer1(nc, c):
    with ExitStack() as st:
        ln5 = Norm(nc, c, st, "ln5_")
        attention1(nc, c, ln5)
        layernorm(nc, c, ln5, turned=False, have_moments=True)
    with ExitStack() as outer:
        c.XNTH = sb(nc, outer, "xnth6", [P, KC, T], F32R)
        c.XNTL = sb(nc, outer, "xntl6", [P, KC, T], F32R)
        with ExitStack() as st:
            ln6 = Norm(nc, c, st, "ln6_")
            cross1(nc, c, ln6)
            layernorm(nc, c, ln6, have_moments=True, split=True)
        swiglu(nc, c)


def swiglu(nc, c):
    NT = 256
    NQ = T // NT
    QT = NT // S
    with ExitStack() as st:
        s = sems(nc, st, "sw_", "gu_done sig h_ev h_high h_low o_done x_add")
        SG = sb(nc, st, "sw_sg", [P, MC, NT])
        HF = sb(nc, st, "sw_hf", [P, MC, NT])
        HH = [sb(nc, st, f"sw_hh{p}", [P, MC, NT], F32R) for p in range(2)]
        HL = [sb(nc, st, f"sw_hl{p}", [P, MC, NT], F32R) for p in range(2)]
        OB = c.bank[6]
        with nc.Block() as block:
            @block.tensor
            def _(pe):
                def hidden(n):
                    at = slice(n * NT, (n + 1) * NT) if isinstance(n, int) else bass.ds(n * NT, NT)
                    x = [a[:, :, at] for a in (c.XNTH, c.XNTL)]
                    for m in range(MC):
                        pe.wait_ge(s["h_ev"], 8 * n + m + 5)
                        for i, w in enumerate((c.WG, c.WU)):
                            mm = split_product(pe, c.bank[m % 4][:, i * NT:(i + 1) * NT],
                                               [[a[:, k, m * P:(m + 1) * P] for k in range(KC)] for a in w],
                                               [[a[:, k, :] for k in range(KC)] for a in x])
                        mm.then_inc(s["gu_done"], 1)

                def down(n, p):
                    pe.wait_ge(s["h_low"], 8 * n + 16)
                    pe.wait_ge(s["x_add"], n + 1)
                    for t in range(QT):
                        mm = split_product(pe, OB[:, t * D:(t + 1) * D],
                                           [[a[:, m, t * P:(t + 1) * P] for m in range(MC)] for a in (HH[p], HL[p])],
                                           [[a[:, m, :] for m in range(MC)] for a in c.WD])
                    mm.then_inc(s["o_done"], 1)

                hidden(0)
                with pe.Fori(0, NQ // 2 - 1) as j:
                    hidden(2 * j + 1)
                    down(2 * j, 0)
                    hidden(2 * j + 2)
                    down(2 * j + 1, 1)
                hidden(NQ - 1)
                down(NQ - 2, 0)
                down(NQ - 1, 1)

            @block.scalar
            def _(act):
                def high(n, m, p):
                    act.wait_ge(s["h_ev"], 8 * n + m + 9)
                    act.activation(HH[p][:, m, :], HF[:, m, :], ACT.Copy).then_inc(s["h_high"], 1)

                with act.Fori(0, NQ // 2) as j:
                    for p in range(2):
                        n = 2 * j + p
                        for m in range(MC):
                            act.wait_ge(s["gu_done"], 8 * n + m + 1)
                            act.wait_ge(s["h_ev"], 8 * n + m + 1)
                            act.activation(SG[:, m, :], c.bank[m % 4][:, 0:NT], ACT.Silu).then_inc(s["sig"], 1)
                            if m:
                                high(n, m - 1, p)
                        high(n, MC - 1, p)

            @block.gpsimd
            def _(pool):
                pool.sem_inc(s["h_low"], 8)
                with pool.Fori(0, NQ // 2) as j:
                    for p in range(2):
                        for m in range(MC):
                            pool.wait_ge(s["h_high"], 16 * j + 8 * p + m + 1)
                            pool.tensor_tensor(HL[p][:, m, :], HF[:, m, :], HH[p][:, m, :].bitcast(F32), ALU.subtract).then_inc(s["h_low"], 1)

            @block.vector
            def _(dve):
                dve.sem_inc(s["h_ev"], 8)
                dve.sem_inc(s["x_add"], 1)

                def quarter(n):
                    for m in range(MC):
                        dve.wait_ge(s["sig"], 8 * n + m + 1)
                        dve.wait_ge(s["h_low"], 8 * n + m + 1)
                        dve.tensor_tensor(HF[:, m, :], SG[:, m, :], c.bank[m % 4][:, NT:2 * NT], ALU.mult).then_inc(s["h_ev"], 1)

                def add(n):
                    dve.wait_ge(s["o_done"], n + 1)
                    x = c.X[:, n * QT:(n + 1) * QT, :] if isinstance(n, int) else c.X[:, bass.ds(n * QT, QT), :]
                    dve.tensor_tensor(x, x, OB[:, :].rearrange("p (t n) -> p t n", t=QT), ALU.add).then_inc(s["x_add"], 1)

                quarter(0)
                with dve.Fori(0, NQ - 1) as n:
                    quarter(n + 1)
                    add(n)
                add(NQ - 1)


def build(nc, c):
    with ExitStack() as stack:
        c.s = {n: stack.enter_context(nc.semaphore(n)) for n in
               "x_loaded ctx_loaded const zeros_ready disp_zeroed pad_st beta_ld sign beta router_ld b1_ld scattered st0 st1 out".split()}
        c.got = [stack.enter_context(nc.semaphore(f"got{b}")) for b in range(B)]
        c.bank = [stack.enter_context(nc.psum_tensor(f"bank{i}", [P, 512], F32)) for i in range(8)]
        c.X = sb(nc, stack, "X", [P, B, D])
        c.CTX = sb(nc, stack, "CTX", [P, B, D])
        c.XN = sb(nc, stack, "XN", [P, B, D])
        c.XNT = sb(nc, stack, "XNT", [P, KC, T])
        c.IDN = sb(nc, stack, "IDN", [P, P])
        c.MASK0 = sb(nc, stack, "MASK0", [P, SEG])
        c.ZERO = sb(nc, stack, "ZERO", [P, 2 * D])
        c.disp = nc.dram_tensor("disp", [E0 * CAP, D], F32, kind="Internal").ap()
        c.eo = nc.dram_tensor("eo", [E0 * CAP, D], F32, kind="Internal").ap()
        c.pad = nc.dram_tensor("pad", [HC, 384], F32, kind="Internal").ap()
        attend_infini(nc, c)
        later_weights(nc, c, stack)
        long_conv(nc, c)
        moe(nc, c)
        layer1(nc, c)
        with nc.Block() as block:
            @block.sync
            def _(sp):
                sp.wait_ge(c.s["ctx_loaded"], 16)
                sp.wait_ge(c.s["disp_zeroed"], 16 * E0)
                sp.dma_start(c.out.rearrange("b p d -> p b d"), c.X[:, :, :]).then_inc(c.s["out"], 16)
                sp.wait_ge(c.s["out"], 16)


def kernel(**inputs):
    import numpy as _np
    import concourse.bacc as _bacc
    from concourse.bass_utils import run_bass_kernel_spmd as _run

    nc = _bacc.Bacc("TRN2", target_bir_lowering=False, num_devices=1)
    arrays = {}

    def given(name):
        a = _np.ascontiguousarray(inputs[name])
        arrays[f"in_{name}"] = a
        return nc.dram_tensor(f"in_{name}", a.shape, mybir.dt.from_np(a.dtype), kind="ExternalInput").ap()

    c = Core()
    c.x = given("x")
    c.ctx = given("ctx_2048")
    c.Wq = given("L0_attn_Wq")
    c.Wk = given("L0_attn_Wk")
    c.Wv = given("L0_attn_Wv")
    c.Wo = given("L0_attn_Wo")
    c.betas = given("L0_attn_betas")
    c.ssm = given("L0_xattn_ssm_kernel")
    c.convD = given("L0_xattn_D")
    c.wg = given("L0_ffn_wg")
    c.fc1 = given("L0_ffn_fc1_w")
    c.fc1b = given("L0_ffn_fc1_b")
    c.fc2 = given("L0_ffn_fc2_w")
    c.fc2b = given("L0_ffn_fc2_b")
    c.wqkv = given("L1_attn_w_qkv")
    c.bqkv = given("L1_attn_b_qkv")
    c.wout = given("L1_attn_w_out")
    c.bout = given("L1_attn_b_out")
    c.QW = given("L1_xattn_QW")
    c.Qb = given("L1_xattn_Qb")
    c.KW = given("L1_xattn_KW")
    c.Kb = given("L1_xattn_Kb")
    c.VW = given("L1_xattn_VW")
    c.Vb = given("L1_xattn_Vb")
    c.wgate = given("L1_ffn_w_gate")
    c.wup = given("L1_ffn_w_up")
    c.wdown = given("L1_ffn_w_down")
    c.out = nc.dram_tensor("out", (B, S, D), F32, kind="ExternalOutput").ap()
    build(nc, c)
    return _run(nc, [arrays], core_ids=[0]).results[0]["out"]
```

```python
from contextlib import ExitStack

import concourse.bass as bass
from concourse import mybir

F32 = mybir.dt.float32
I32 = mybir.dt.int32
U32 = mybir.dt.uint32
F32R = mybir.dt.float32r
ALU = mybir.AluOpType
ACT = mybir.ActivationFunctionType
AX = mybir.AxisListType

P = 128
B = 8
S = 128
D = 256
KC = D // P
T = B * S
EPS = 1e-5
NEG = -3.0e38

H0 = 16
DK = 128
SEG = 64
NJ = 16
HC = 16
HD = S // HC
E0 = 8
TOPK = 2
CAP = TOPK * T // E0
HID = 4 * D
MC = HID // P
BIG = 1 << 20
H1 = 16
HD1 = D // H1


class Core:
    pass


def bcast(ap, axis, n):
    shape = list(ap.shape)
    return ap.unsqueeze(axis).broadcast_to(shape[:axis] + [n] + shape[axis:])


def sb(nc, stack, name, shape, dt=F32):
    return stack.enter_context(nc.sbuf_tensor(name, shape, dt))


def sems(nc, stack, prefix, names):
    made = {n: stack.enter_context(nc.semaphore(prefix + n)) for n in names.split()}
    stack.callback(clear, nc, [x.num for x in made.values()])
    return made


def sem_row(nc, stack, prefix, n):
    made = [stack.enter_context(nc.semaphore(f"{prefix}{i}")) for i in range(n)]
    stack.callback(clear, nc, [x.num for x in made])
    return made


def clear(nc, nums):
    with nc.Block() as block:
        @block.sync
        def _(sp):
            left = sorted(nums)
            while left:
                n = 1
                while n < len(left) and left[n] == left[0] + n:
                    n += 1
                sp.sem_clear(range(left[0], left[0] + n))
                left = left[n:]


def attend_infini(nc, c):
    with ExitStack() as st:
        c.wqkv_ld = sem_row(nc, st, "wqkv_ld", 2)
        c.WQ = [sb(nc, st, f"ia_wqkv{p}", [P, 3, KC, DK]) for p in range(2)]
        c.BTM = sb(nc, st, "ia_btm", [P, H0, DK])
        c.BTR = sb(nc, st, "ia_btr", [P, H0, DK])
        c.SIGN = sb(nc, st, "ia_sign", [P, 1])
        c.XNTH = sb(nc, st, "xnth1", [P, KC, T], F32R)
        c.XNTL = sb(nc, st, "xntl1", [P, KC, T], F32R)
        norm = Norm(nc, c, st, "ln1_")
        setup(nc, c, c.s)

        infini_attention(nc, c, norm)


def load_qkv(sp, c, h, p):
    for i, w in enumerate((c.Wq, c.Wk, c.Wv)):
        a = w.rearrange("(k p) (h n) -> h p k n", p=P, n=DK)
        src = a[h] if isinstance(h, int) else a[bass.ds(h, 1)].squeeze(0)
        sp.dma_start(c.WQ[p][:, i, :, :], src).then_inc(c.wqkv_ld[p], 16)


def later_loads(sp, c, s):
    load_qkv(sp, c, 1, 1)
    sp.dma_start(c.CTX[:, :, :], c.ctx.rearrange("b p d -> p b d")).then_inc(s["ctx_loaded"], 16)
    sp.dma_start(c.pad[:, P - 1:P - 1 + D], c.ssm).then_inc(s["pad_st"], 16)
    sp.wait_ge(s["zeros_ready"], 1)
    sp.dma_start(c.pad[:, 0:P - 1], c.ZERO[0:HC, 0:P - 1]).then_inc(s["pad_st"], 16)
    for e in range(E0):
        sp.dma_start(c.disp[e * CAP:(e + 1) * CAP, :].rearrange("(t p) d -> p t d", p=P),
                     c.ZERO[:, :].rearrange("p (t d) -> p t d", t=CAP // P)).then_inc(s["disp_zeroed"], 16)


def setup(nc, c, s):
    with nc.Block() as block:
        @block.sync
        def _(sp):
            sp.dma_start(c.X[:, :, :], c.x.rearrange("b p d -> p b d")).then_inc(s["x_loaded"], 16)
            load_qkv(sp, c, 0, 0)
            sp.dma_start(c.BTR[:, :, :].rearrange("p h n -> p (h n)"),
                         c.betas.rearrange("a h b n -> (a b) (h n)").broadcast_to([P, H0 * DK])).then_inc(s["beta_ld"], 16)

        @block.vector
        def _(dve):
            dve.memset(c.SIGN[0:SEG, :], 1.0).then_inc(s["sign"], 1)
            dve.memset(c.SIGN[SEG:P, :], -1.0).then_inc(s["sign"], 1)

        @block.gpsimd
        def _(pool):
            pool.memset(c.IDN[:, :], 0.0).then_inc(s["const"], 1)
            pool.memset(c.MASK0[:, :], 0.0).then_inc(s["const"], 1)
            pool.memset(c.ZERO[:, :], 0.0).then_inc(s["zeros_ready"], 1)
            pool.wait_ge(s["const"], 2)
            pool.affine_select(out=c.IDN[:, :], in_=c.IDN[:, :], compare_op=ALU.not_equal, fill=1.0,
                               base=0, pattern=[[-1, P]], channel_multiplier=1).then_inc(s["const"], 1)
            for g in range(2):
                half = c.MASK0[g * SEG:(g + 1) * SEG, :]
                pool.wait_ge(s["const"], 3 + g)
                pool.affine_select(out=half, in_=half, compare_op=ALU.is_ge, fill=NEG, base=0,
                                   pattern=[[-1, SEG]], channel_multiplier=1).then_inc(s["const"], 1)


def split_product(pe, out, lhs, rhs, first=True, last=True):
    n = len(lhs[0])
    for k in range(n):
        for i, (a, b) in enumerate(((0, 0), (0, 1), (1, 0))):
            mm = pe.matmul(out, lhs[a][k], rhs[b][k], start=(first and k == 0 and i == 0), stop=(last and k == n - 1 and i == 2))
    return mm


class Norm:

    def __init__(self, nc, c, st, pre):
        self.c = c
        self.s = sems(nc, st, pre, "stats aggr veps root rstd xn turned evac high low")
        self.st = sb(nc, st, pre + "stats", [P, B, 6])
        self.mv = sb(nc, st, pre + "mv", [P, B, 2])
        self.rstd = sb(nc, st, pre + "rstd", [P, B])

    def stats(self, dve, q):
        s, c = self.s, self.c
        for b in (2 * q, 2 * q + 1):
            dve.bn_stats(self.st[:, b, :], c.X[:, b, :]).then_inc(s["stats"], 1)
        self.join(dve, q)

    def moments(self, dve, b):
        x, st = [a[:, b, :] if isinstance(b, int) else a[:, bass.ds(b, 1), :].squeeze(1) for a in (self.c.X, self.st)]
        dve.bn_stats(st, x).then_inc(self.s["stats"], 1)

    def join(self, dve, q):
        s = self.s
        for b in (2 * q, 2 * q + 1):
            dve.wait_ge(s["stats"], b + 1)
            dve.bn_aggr(self.mv[:, b, :], self.st[:, b, :]).then_inc(s["aggr"], 1)
        dve.wait_ge(s["aggr"], 2 * q + 2)
        dve.tensor_scalar(self.rstd[:, 2 * q:2 * q + 2], self.mv[:, 2 * q:2 * q + 2, 1], EPS, None, ALU.add).then_inc(s["veps"], 1)

    def root(self, act, q):
        act.wait_ge(self.s["veps"], q + 1)
        r = self.rstd[:, 2 * q:2 * q + 2]
        act.activation(r, r, ACT.Sqrt).then_inc(self.s["root"], 1)

    def scale(self, dve, q):
        s, c, r = self.s, self.c, self.rstd
        dve.wait_ge(s["root"], q + 1)
        dve.reciprocal(r[:, 2 * q:2 * q + 2], r[:, 2 * q:2 * q + 2]).then_inc(s["rstd"], 1)
        dve.wait_ge(s["rstd"], q + 1)
        for b in (2 * q, 2 * q + 1):
            dve.tensor_scalar(c.XN[:, b, :], c.X[:, b, :], self.mv[:, b, 0:1], r[:, b:b + 1],
                              ALU.subtract, ALU.mult).then_inc(s["xn"], 1)

    def turn(self, pe, q, bank):
        pe.wait_ge(self.s["xn"], 2 * q + 2)
        for i in range(2):
            for k in range(KC):
                last = pe.transpose(bank[:, (2 * k + i) * S:(2 * k + i + 1) * S],
                                    self.c.XN[:, 2 * q + i, k * P:(k + 1) * P], self.c.IDN[:, :])
        last.then_inc(self.s["turned"], 1)

    def high(self, act, q, bank):
        act.wait_ge(self.s["turned"], q + 1)
        act.activation(self.c.XNTH[:, :, 2 * q * S:(2 * q + 2) * S], bank[:, :].rearrange("p (k t) -> p k t", k=KC),
                       ACT.Copy).then_inc(self.s["high"], 1)

    def low(self, dve, q, bank):
        at = slice(2 * q * S, (2 * q + 2) * S)
        dve.wait_ge(self.s["high"], q + 1)
        dve.tensor_tensor(self.c.XNTL[:, :, at], bank[:, :].rearrange("p (k t) -> p k t", k=KC),
                          self.c.XNTH[:, :, at].bitcast(F32), ALU.subtract).then_inc(self.s["low"], 1)

    def copy(self, act, q, bank):
        act.wait_ge(self.s["turned"], q + 1)
        act.activation(self.c.XNT[:, :, 2 * q * S:(2 * q + 2) * S], bank[:, :].rearrange("p (k t) -> p k t", k=KC),
                       ACT.Copy).then_inc(self.s["evac"], 1)


def infini_attention(nc, c, before):
    with ExitStack() as st:
        s = sems(nc, st, "ia_", "wo_ld beta_c w_hi w_lo const pj_done qk_ev v_ev "
                 "neg_done exp_done sig_done s_done s_free masked maxed shifted exped summed rsum "
                 "ad_done den rden p_pool p_mem p_free pt_done pts0 pts1 pv_done att_ev out_done x_add")
        WQ, BTM = c.WQ, c.BTM
        WH = sb(nc, st, "ia_wh", [P, 2, KC, DK], F32R)
        WL = sb(nc, st, "ia_wl", [P, 2, KC, DK], F32R)
        WO = sb(nc, st, "ia_wo", [P, H0, D])
        BTC = c.BTR
        QT = sb(nc, st, "ia_qt", [P, B, S])
        KT = sb(nc, st, "ia_kt", [P, B, S])
        EQ = sb(nc, st, "ia_eq", [P, 2, B, SEG])
        SQ = sb(nc, st, "ia_sq", [P, B, SEG])
        SK = sb(nc, st, "ia_sk", [P, B, SEG + 1])
        SM = sb(nc, st, "ia_sm", [P, B, SEG])
        EX = sb(nc, st, "ia_ex", [P, B, SEG])
        MX = sb(nc, st, "ia_mx", [P, B])
        RS = sb(nc, st, "ia_rs", [P, B])
        RD = sb(nc, st, "ia_rd", [P, B])
        PR = sb(nc, st, "ia_pr", [P, B, S])
        PTS = sb(nc, st, "ia_pts", [P, B, S])
        VX = [sb(nc, st, f"ia_vx{p}", [P, B, DK]) for p in range(2)]
        VD = [sb(nc, st, f"ia_vd{p}", [SEG, B, DK]) for p in range(2)]
        ATT = sb(nc, st, "ia_att", [P, NJ, B, S])
        SC = c.bank[0]
        AD = [c.bank[1], c.bank[2]]
        PJ = [c.bank[3], c.bank[4], c.bank[5]]
        OB = [c.bank[6], c.bank[7]]
        scale = float(DK) ** -0.5
        HB = B // 2
        norm = Norm(nc, c, st, "ln2_")
        NQ = B // 2

        with nc.Block() as block:
            @block.sync
            def _(sp):
                later_loads(sp, c, c.s)
                sp.dma_start(WO[:, :, :], c.Wo.rearrange("(h p) n -> p h n", p=DK)).then_inc(s["wo_ld"], 16)
                with sp.Fori(1, H0 // 2) as j:
                    for p in range(2):
                        sp.wait_ge(s["w_lo"], 2 * j + p - 1)
                        sp.wait_ge(s["pj_done"], 12 * j + 6 * p - 6)
                        load_qkv(sp, c, 2 * j + p, p)

            @block.gpsimd
            def _(pool):
                pool.memset(PR[:, :, :], 0.0).then_inc(s["const"], 1)
                pool.memset(SK[:, :, SEG:SEG + 1], 1.0 / DK).then_inc(s["const"], 1)
                pool.wait_ge(s["const"], 2)

                def split_low(h, p):
                    pool.wait_ge(s["w_hi"], h + 1)
                    pool.tensor_tensor(WL[:, :, :, :], WQ[p][:, 0:2, :, :], WH[:, :, :, :].bitcast(F32), ALU.subtract).then_inc(s["w_lo"], 1)

                def head(h, p, more=True):
                    pool.wait_ge(s["maxed"], h + 1)
                    pool.tensor_tensor(SM[:, :, :], SM[:, :, :], bcast(MX[:, :], 2, SEG), ALU.subtract).then_inc(s["shifted"], 1)
                    pool.wait_ge(s["rsum"], h + 1)
                    pool.wait_ge(s["p_free"], h + 1)
                    pool.tensor_tensor(PR[SEG:P, :, SEG:S], EX[SEG:P, :, :], bcast(RS[SEG:P, :], 2, SEG), ALU.mult).then_inc(s["p_pool"], 1)
                    pool.wait_ge(s["p_pool"], h + 1)
                    if more:
                        split_low(h + 2, p)

                split_low(0, 0)
                split_low(1, 1)
                with pool.Fori(0, H0 // 2 - 1) as j:
                    head(2 * j, 0)
                    head(2 * j + 1, 1)
                head(H0 - 2, 0, False)
                head(H0 - 1, 1, False)

            @block.scalar
            def _(act):
                def evac_qk(h):
                    for t in range(4):
                        act.wait_ge(s["pj_done"], 6 * h + t + 1)
                        dst = (QT, KT)[t // 2][:, (t % 2) * HB:(t % 2 + 1) * HB, :]
                        act.activation(dst, PJ[t % 3][:, :].rearrange("p (b t) -> p b t", b=HB), ACT.Copy).then_inc(s["qk_ev"], 1)

                def sigma_exp(h):
                    act.wait_ge(s["qk_ev"], 4 * h + 4)
                    act.activation(EQ[:, 0, :, :], QT[:, :, SEG:S], ACT.Relu, scale=-1.0).then_inc(s["neg_done"], 1)
                    act.activation(EQ[:, 1, :, :], KT[:, :, 0:SEG], ACT.Relu, scale=-1.0).then_inc(s["neg_done"], 1)
                    act.wait_ge(s["neg_done"], 2 * h + 2)
                    act.activation(EQ[:, :, :, :], EQ[:, :, :, :], ACT.Exp, scale=-1.0).then_inc(s["exp_done"], 1)

                def split_high(h, p, n):
                    act.wait_ge(c.wqkv_ld[p], 48 * n)
                    if not isinstance(h, int) or h:
                        act.wait_ge(s["pj_done"], 6 * h)
                    act.activation(WH[:, :, :, :], WQ[p][:, 0:2, :, :], ACT.Copy).then_inc(s["w_hi"], 1)

                def head(h, p, n=None, nxt=True):
                    act.wait_ge(s["shifted"], h + 1)
                    act.activation(EX[:, :, :], SM[:, :, :], ACT.Exp).then_inc(s["exped"], 1)
                    if nxt:
                        evac_qk(h + 1)
                    act.wait_ge(s["pt_done"], 2 * h + 1)
                    act.activation(PTS[:, 0:HB, :], AD[0][:, :].rearrange("p (b t) -> p b t", b=HB), ACT.Copy).then_inc(s["pts0"], 1)
                    if nxt:
                        sigma_exp(h + 1)
                    if n is not None:
                        split_high(h + 2, p, n)
                    for g in range(2):
                        act.wait_ge(s["pv_done"], 2 * h + g + 1)
                        src = OB[g][:, :].rearrange("p (b i m j) -> p b i m j", b=HB, i=2, j=NJ)
                        for i in range(2):
                            at = 4 * h + i * SEG
                            rows = slice(at, at + 4) if isinstance(h, int) else bass.ds(at, 4)
                            act.activation(ATT[:, :, g * HB:(g + 1) * HB, rows].rearrange("p j b m -> p b m j"),
                                           src[:, :, i, :, :], ACT.Copy).then_inc(s["att_ev"], 1)

                act.sem_inc(s["att_ev"], 4)
                act.sem_inc(s["pts0"], 1)
                split_high(0, 0, 1)
                for q in range(NQ):
                    before.root(act, q)
                for q in range(NQ):
                    before.copy(act, q, c.bank[q])
                    before.high(act, q, c.bank[q])
                act.wait_ge(c.s["beta_ld"], 16)
                act.wait_ge(c.s["sign"], 2)
                act.activation(BTM[:, :, :], c.BTR[:, :, :], ACT.Sigmoid, scale=c.SIGN[:, 0:1]).then_inc(c.s["beta"], 1)
                evac_qk(0)
                sigma_exp(0)
                split_high(1, 1, 1)
                with act.Fori(0, H0 // 2 - 1) as j:
                    head(2 * j, 0, j + 2)
                    head(2 * j + 1, 1, j + 2)
                head(H0 - 2, 0)
                head(H0 - 1, 1, None, False)
                norm.root(act, 0)
                for q in range(1, NQ):
                    norm.root(act, q)
                    norm.copy(act, q - 1, c.bank[q - 1])
                norm.copy(act, NQ - 1, c.bank[NQ - 1])

            @block.tensor
            def _(pe):
                def project_qk(h, first=False):
                    pe.wait_ge(s["w_lo"], h + 1)
                    for t in range(4):
                        if t == 0 and not first:
                            pe.wait_ge(s["qk_ev"], 4 * h)
                        if t in (1, 2) and not first:
                            pe.wait_ge(s["v_ev"], 4 * h - 4 + 2 * t)
                        if t == 3:
                            pe.wait_ge(s["qk_ev"], 4 * h + 1)
                        half = slice((t % 2) * HB * S, (t % 2 + 1) * HB * S)
                        mm = split_product(pe, PJ[t % 3][:, :], [[w[:, t // 2, k, :] for k in range(KC)] for w in (WH, WL)],
                                           [[x[:, k, half] for k in range(KC)] for x in (c.XNTH, c.XNTL)])
                        mm.then_inc(s["pj_done"], 1)

                def project_v(h, p):
                    for t in range(4, 6):
                        pe.wait_ge(s["qk_ev"], 4 * h + t - 2)
                        for i in range(HB):
                            b = (t - 4) * HB + i
                            for k in range(KC):
                                mm = pe.matmul(PJ[t % 3][:, i * DK:(i + 1) * DK], c.XNT[:, k, b * S:(b + 1) * S],
                                               WQ[p][:, 2, k, :], start=(k == 0), stop=(k == KC - 1))
                        mm.then_inc(s["pj_done"], 1)

                def head(h, p, nxt=True):
                    pe.wait_ge(s["qk_ev"], 4 * h + 4)
                    pe.wait_ge(s["s_free"], h + 1)
                    for b in range(B):
                        for g in range(2):
                            r = slice(g * SEG, (g + 1) * SEG)
                            mm = pe.matmul(SC[r, b * SEG:(b + 1) * SEG], QT[:, b, r], KT[:, b, r], start=True, stop=True)
                    mm.then_inc(s["s_done"], 1)
                    pe.wait_ge(s["sig_done"], 2 * h + 2)
                    pe.wait_ge(s["pts0"], h + 1)
                    pe.wait_ge(s["pts1"], h + 1)
                    for b in range(B):
                        mm = pe.matmul(AD[b // HB][SEG:P, (b % HB) * (SEG + 1):(b % HB + 1) * (SEG + 1)],
                                       SQ[:, b, :], SK[:, b, :], start=True, stop=True)
                    mm.then_inc(s["ad_done"], 1)
                    if nxt:
                        project_qk(h + 1)
                    pe.wait_ge(s["p_pool"], h + 1)
                    pe.wait_ge(s["p_mem"], 3 * h + 3)
                    for g in range(2):
                        for i in range(HB):
                            mm = pe.transpose(AD[g][:, i * S:(i + 1) * S], PR[:, g * HB + i, :], c.IDN[:, :])
                        mm.then_inc(s["pt_done"], 1)
                    pe.drain().then_inc(s["p_free"], 1)
                    if nxt:
                        project_v(h + 1, 1 - p)
                    pe.wait_ge(s["v_ev"], 4 * h + 4)
                    for g in range(2):
                        pe.wait_ge(s["pts0" if g == 0 else "pts1"], h + 2)
                        pe.wait_ge(s["att_ev"], 4 * h + 2 + 2 * g)
                        for i in range(HB):
                            b = g * HB + i
                            pe.matmul(OB[g][:, i * S:i * S + SEG], VD[p][:, b, :], PTS[0:SEG, b, 0:SEG], start=True, stop=True)
                            mm = pe.matmul(OB[g][:, i * S + SEG:(i + 1) * S], VX[p][:, b, :], PTS[:, b, SEG:S], start=True, stop=True)
                        mm.then_inc(s["pv_done"], 1)

                def project_out():
                    pe.wait_ge(s["wo_ld"], 16)
                    pe.wait_ge(s["att_ev"], 4 * H0 + 4)
                    for q in range(B // 2):
                        if q >= 2:
                            pe.wait_ge(s["x_add"], q - 1)
                        for i in range(2):
                            for j in range(NJ):
                                mm = pe.matmul(OB[q % 2][:, i * D:(i + 1) * D], ATT[:, j, 2 * q + i, :], WO[:, j, :],
                                               start=(j == 0), stop=(j == NJ - 1))
                        mm.then_inc(s["out_done"], 1)
                        if q:
                            norm.turn(pe, q - 1, c.bank[q - 1])
                    norm.turn(pe, NQ - 1, c.bank[NQ - 1])

                pe.sem_inc(s["p_free"], 1)
                pe.wait_ge(c.s["const"], 3)
                for q in range(NQ):
                    before.turn(pe, q, c.bank[q])
                pe.wait_ge(before.s["low"], NQ)
                pe.wait_ge(s["const"], 2)
                project_qk(0, True)
                project_v(0, 0)
                with pe.Fori(0, H0 // 2 - 1) as j:
                    head(2 * j, 0)
                    head(2 * j + 1, 1)
                head(H0 - 2, 0)
                head(H0 - 1, 1, False)
                project_out()

            @block.vector
            def _(dve):
                def sigma(h):
                    dve.wait_ge(s["exp_done"], h + 1)
                    dve.scalar_tensor_tensor(SQ[:, :, :], QT[:, :, SEG:S], 0.0, EQ[:, 0, :, :], ALU.max, ALU.add).then_inc(s["sig_done"], 1)
                    dve.scalar_tensor_tensor(SK[:, :, 0:SEG], KT[:, :, 0:SEG], 0.0, EQ[:, 1, :, :], ALU.max, ALU.add).then_inc(s["sig_done"], 1)

                def evac_v(h, p):
                    for t in range(4, 6):
                        dve.wait_ge(s["pj_done"], 6 * h + t + 1)
                        b = slice((t - 4) * HB, (t - 3) * HB)
                        src = PJ[t % 3][:, :].rearrange("p (b n) -> p b n", b=HB)
                        if isinstance(h, int):
                            bm, bc = BTM[:, h, :], BTC[0:SEG, h, :]
                        else:
                            bm, bc = BTM[:, bass.ds(h, 1), :].squeeze(1), BTC[0:SEG, bass.ds(h, 1), :].squeeze(1)
                        dve.tensor_tensor(VX[p][:, b, :], src, bcast(bm, 1, HB), ALU.mult).then_inc(s["v_ev"], 1)
                        dve.tensor_tensor(VD[p][:, b, :], src[0:SEG], bcast(bc, 1, HB), ALU.mult).then_inc(s["v_ev"], 1)

                def head(h, p, nxt=True):
                    dve.wait_ge(s["s_done"], h + 1)
                    dve.scalar_tensor_tensor(SM[:, :, :], SC[:, :].rearrange("p (b k) -> p b k", b=B), scale,
                                             bcast(c.MASK0[:, :], 1, B), ALU.mult, ALU.add).then_inc(s["masked"], 1)
                    dve.wait_ge(s["masked"], h + 1)
                    dve.tensor_reduce(MX[:, :], SM[:, :, :], AX.X, ALU.max).then_inc(s["maxed"], 1)
                    dve.sem_inc(s["s_free"], 1)
                    dve.wait_ge(s["ad_done"], h + 1)
                    lin = [AD[g][SEG:P, 0:HB * (SEG + 1)].rearrange("p (b k) -> p b k", b=HB) for g in range(2)]
                    for g in range(2):
                        dve.tensor_reduce(RD[SEG:P, g * HB:(g + 1) * HB], lin[g], AX.X, ALU.add).then_inc(s["den"], 1)
                    dve.wait_ge(s["den"], 2 * h + 2)
                    dve.reciprocal(RD[SEG:P, :], RD[SEG:P, :]).then_inc(s["rden"], 1)
                    dve.wait_ge(s["rden"], h + 1)
                    dve.wait_ge(s["p_free"], h + 1)
                    for g in range(2):
                        dve.tensor_tensor(PR[SEG:P, g * HB:(g + 1) * HB, 0:SEG], lin[g][:, :, 0:SEG],
                                          bcast(RD[SEG:P, g * HB:(g + 1) * HB], 2, SEG), ALU.mult).then_inc(s["p_mem"], 1)
                    dve.wait_ge(s["exped"], h + 1)
                    dve.tensor_reduce(RS[:, :], EX[:, :, :], AX.X, ALU.add).then_inc(s["summed"], 1)
                    dve.wait_ge(s["summed"], h + 1)
                    dve.reciprocal(RS[:, :], RS[:, :]).then_inc(s["rsum"], 1)
                    dve.wait_ge(s["rsum"], h + 1)
                    dve.tensor_tensor(PR[0:SEG, :, 0:SEG], EX[0:SEG, :, :], bcast(RS[0:SEG, :], 2, SEG), ALU.mult).then_inc(s["p_mem"], 1)
                    dve.wait_ge(s["pt_done"], 2 * h + 2)
                    dve.tensor_copy(PTS[:, HB:B, :], AD[1][:, :].rearrange("p (b t) -> p b t", b=HB)).then_inc(s["pts1"], 1)
                    if nxt:
                        sigma(h + 1)
                        evac_v(h + 1, 1 - p)

                def add_out():
                    for q in range(B // 2):
                        dve.wait_ge(s["out_done"], q + 1)
                        xs = c.X[:, 2 * q:2 * q + 2, :]
                        dve.tensor_tensor(xs, xs, OB[q % 2][:, :].rearrange("p (b n) -> p b n", b=2), ALU.add).then_inc(s["x_add"], 1)
                        dve.wait_ge(s["x_add"], q + 1)
                        norm.stats(dve, q)
                        norm.scale(dve, q)

                dve.sem_inc(s["s_free"], 1)
                dve.sem_inc(s["pts1"], 1)
                dve.wait_ge(c.s["x_loaded"], 16)
                for q in range(NQ):
                    before.stats(dve, q)
                for q in range(NQ):
                    before.scale(dve, q)
                for q in range(NQ):
                    before.low(dve, q, c.bank[q])
                dve.wait_ge(s["const"], 2)
                dve.wait_ge(c.s["beta"], 1)
                dve.tensor_scalar(BTC[0:SEG, :, :], BTM[0:SEG, :, :], -1.0, 1.0, ALU.mult, ALU.add).then_inc(s["beta_c"], 1)
                sigma(0)
                dve.wait_ge(s["beta_c"], 1)
                evac_v(0, 0)
                with dve.Fori(0, H0 // 2 - 1) as j:
                    head(2 * j, 0)
                    head(2 * j + 1, 1)
                head(H0 - 2, 0)
                head(H0 - 1, 1, False)
                add_out()


def later_weights(nc, c, st):
    c.WT = sb(nc, st, "at_wt", [P, KC, 3 * D])
    c.WOT = sb(nc, st, "at_wot", [P, KC, D])
    c.QWT = sb(nc, st, "cr_qwt", [P, 1, S])
    c.KWT = sb(nc, st, "cr_kwt", [P, 1, S])
    c.VWT = sb(nc, st, "cr_vwt", [P, 1, S])
    c.WG = [sb(nc, st, f"sw_wg{n}", [P, KC, HID], F32R) for n in range(2)]
    c.WU = [sb(nc, st, f"sw_wu{n}", [P, KC, HID], F32R) for n in range(2)]
    c.WD = [sb(nc, st, f"sw_wd{n}", [P, MC, D], F32R) for n in range(2)]
    c.ROUTER = sb(nc, st, "mo_wg", [P, KC, E0])
    c.B1R = sb(nc, st, "mo_b1r", [E0 * MC, P])
    c.jobs = [(c.wqkv, 3 * KC, KC, c.WT), (c.wout, KC, KC, c.WOT), (c.QW, 1, 1, c.QWT), (c.KW, 1, 1, c.KWT),
              (c.VW, 1, 1, c.VWT), (c.wgate, MC, KC, c.WG), (c.wup, MC, KC, c.WU), (c.wdown, KC, MC, c.WD)]
    c.groups = []
    for i, (_, r, k, _) in enumerate(c.jobs):
        nk = min(k, 2 if r > 2 else 4)
        nr = min(r, 4 // nk)
        c.groups += [(i, k0, nk, r0, nr) for r0 in range(0, r, nr) for k0 in range(0, k, nk)]


def raw_weights(nc, c, st):
    c.raw = [sb(nc, st, f"raw{i}", [P, r, k * P]) for i, (_, r, k, _) in enumerate(c.jobs)]
    c.raw_ld = [st.enter_context(nc.semaphore(f"raw_ld{i}")) for i in range(len(c.jobs))]


def load_later_weights(sp, c):
    sp.dma_start(c.ROUTER[:, :, :], c.wg.rearrange("(k p) e -> p k e", p=P)).then_inc(c.s["router_ld"], 16)
    sp.dma_start(c.B1R[:, :], c.fc1b.rearrange("e (m p) -> (e m) p", p=P)).then_inc(c.s["b1_ld"], 16)
    for i, (src, r, k, _) in enumerate(c.jobs):
        sp.dma_start(c.raw[i][:, :, :], src.rearrange("(r p) d -> p r d", p=P)).then_inc(c.raw_ld[i], 16)


def turn_weights(pe, c, s):
    for g, (i, k0, nk, r0, nr) in enumerate(c.groups):
        if g >= 4:
            pe.wait_ge(s["w_out"], g - 3)
        pe.wait_ge(c.raw_ld[i], 16)
        for k in range(nk):
            for r in range(nr):
                mm = pe.transpose(c.bank[4 + g % 4][:, (k * nr + r) * P:(k * nr + r + 1) * P],
                                  c.raw[i][:, r0 + r, (k0 + k) * P:(k0 + k + 1) * P], c.IDN[:, :])
        mm.then_inc(s["w_turned"], 1)


def group_views(c, g, dst):
    i, k0, nk, r0, nr = c.groups[g]
    return (dst[:, k0:k0 + nk, r0 * P:(r0 + nr) * P],
            c.bank[4 + g % 4][:, 0:nk * nr * P].rearrange("p (k t) -> p k t", k=nk))


def turned_high(act, c, s):
    for g, group in enumerate(c.groups):
        dst = c.jobs[group[0]][3]
        if isinstance(dst, list):
            act.wait_ge(s["w_turned"], g + 1)
            act.activation(*group_views(c, g, dst[0]), ACT.Copy).then_inc(s["w_high"], 1)


def turned_rest(dve, c, s):
    n = 0
    for g, group in enumerate(c.groups):
        dst = c.jobs[group[0]][3]
        if isinstance(dst, list):
            n += 1
            dve.wait_ge(s["w_high"], n)
            low, turned = group_views(c, g, dst[1])
            dve.tensor_tensor(low, turned, group_views(c, g, dst[0])[0].bitcast(F32), ALU.subtract).then_inc(s["w_out"], 1)
        else:
            dve.wait_ge(s["w_turned"], g + 1)
            dve.tensor_copy(*group_views(c, g, dst)).then_inc(s["w_out"], 1)


def long_conv(nc, c):
    with ExitStack() as st:
        s = sems(nc, st, "lc_", "toe_ld0 toe_ld1 d_ld anti rev turned_c cr_ev toe0 toe1 kv y0 y1 prod red turned_o x_add")
        norm = Norm(nc, c, st, "ln3_")
        TOE = sb(nc, st, "lc_toe", [P, HC, D])
        TB = [sb(nc, st, f"lc_tb{p}", [P, D]) for p in range(2)]
        DB = sb(nc, st, "lc_d", [P, HC])
        ANTI = sb(nc, st, "lc_anti", [P, P])
        CR = sb(nc, st, "lc_cr", [P, KC, B, S])
        CREV = c.XN
        KV = [sb(nc, st, f"lc_kv{p}", [P, KC, B, HD, HD]) for p in range(2)]
        PD = sb(nc, st, "lc_pd", [P, KC, B, HD * HD])
        OT = sb(nc, st, "lc_ot", [P, KC, B, S])
        with nc.Block() as block:
            @block.sync
            def _(sp):
                sp.wait_ge(c.s["pad_st"], 32)
                for n, (h0, h1) in enumerate(((0, 2), (2, HC))):
                    sp.dma_start(TOE[:, h0:h1, :], bass.AP(tensor=c.pad.tensor, offset=384 * h0, ap=[[1, P], [384, h1 - h0], [1, D]])
                                 ).then_inc((s["toe_ld0"], s["toe_ld1"])[n], 16)
                sp.dma_start(DB[:, :], c.convD.rearrange("(a h) -> a h", a=1).broadcast_to([P, HC])).then_inc(s["d_ld"], 16)
                load_later_weights(sp, c)

            @block.gpsimd
            def _(pool):
                pool.memset(ANTI[:, :], 0.0).then_inc(s["anti"], 1)
                pool.wait_ge(s["anti"], 1)
                pool.affine_select(out=ANTI[:, :], in_=ANTI[:, :], compare_op=ALU.not_equal, fill=1.0,
                                   base=1 - P, pattern=[[1, P]], channel_multiplier=1).then_inc(s["anti"], 1)
                pool.wait_ge(s["cr_ev"], 8)

                pool.sem_inc(s["y1"], 2)
                with pool.Fori(0, HC // 2) as j:
                    for p in range(2):
                        h = 2 * j + p
                        pool.wait_ge(s["y1"], h + 1)
                        for k in range(KC):
                            pool.wait_ge(s["cr_ev"], 8)
                            v = CR[:, k, :, bass.ds(HD * h, HD)]
                            pool.tensor_tensor(KV[p][:, k, :, :, :], bcast(v, 3, HD), bcast(v, 2, HD), ALU.mult).then_inc(s["kv"], 1)

            @block.scalar
            def _(act):
                for g in range(0, 4):
                    act.wait_ge(s["turned_c"], g + 1)
                    act.activation(CR[:, :, 2 * g:2 * g + 2, :], c.bank[g][:, :].rearrange("p (k b t) -> p k b t", k=KC, b=2), ACT.Copy).then_inc(s["cr_ev"], 2)

                def toeplitz(h, p):
                    act.wait_ge(s["y1"], h + 1)
                    src = TOE[:, h, P:D] if isinstance(h, int) else TOE[:, bass.ds(h, 1), P:D].squeeze(1)
                    act.activation(TB[p][:, P:D], src, ACT.Copy).then_inc(s["toe1"], 1)

                act.wait_ge(s["toe_ld0"], 16)
                toeplitz(0, 0)
                toeplitz(1, 1)
                act.wait_ge(s["toe_ld1"], 16)
                with act.Fori(1, HC // 2) as j:
                    for p in range(2):
                        toeplitz(2 * j + p, p)
                for q in range(B // 2):
                    norm.root(act, q)
                for q in range(B // 2):
                    norm.copy(act, q, c.bank[q])

            @block.tensor
            def _(pe):
                for g in range(4):
                    pe.wait_ge(s["rev"], 2 * g + 2)
                    for i in range(2):
                        for k in range(KC):
                            mm = pe.transpose(c.bank[g][:, (2 * k + i) * S:(2 * k + i + 1) * S],
                                              CREV[:, 2 * g + i, k * P:(k + 1) * P], c.IDN[:, :])
                    mm.then_inc(s["turned_c"], 1)
                pe.wait_ge(s["cr_ev"], 8)
                with pe.Fori(0, HC // 2) as j:
                    for p in range(2):
                        h = 2 * j + p
                        y = [c.bank[2 * p], c.bank[2 * p + 1]]
                        kv = [KV[p][:, k, :, :, :].rearrange("p b j i -> p (b j i)") for k in range(KC)]
                        pe.wait_ge(s["kv"], 2 * h + 2)
                        pe.wait_ge(s["toe0"], h + 1)
                        pe.wait_ge(s["toe1"], h + 1)
                        pe.wait_ge(s["prod"], 2 * h + 1)
                        pe.matmul(y[0][:, :], TB[p][:, 0:P], kv[0], start=True, stop=True).then_inc(s["y0"], 1)
                        pe.wait_ge(s["prod"], 2 * h + 2)
                        pe.matmul(y[1][:, :], TB[p][:, P:D], kv[0], start=True, stop=False)
                        pe.matmul(y[1][:, :], TB[p][:, 0:P], kv[1], start=False, stop=True).then_inc(s["y1"], 1)
                pe.wait_ge(s["red"], 2 * HC + 2)
                for q in range(B // 2):
                    for i in range(2):
                        for k in range(KC):
                            mm = pe.transpose(c.bank[4 + q][:, i * D + k * P:i * D + (k + 1) * P], OT[:, k, 2 * q + i, :], c.IDN[:, :])
                    mm.then_inc(s["turned_o"], 1)
                for q in range(B // 2):
                    norm.turn(pe, q, c.bank[q])

            @block.vector
            def _(dve):
                dve.wait_ge(c.s["ctx_loaded"], 16)
                for b in range(B):
                    src = c.CTX[:, b, :].rearrange("p (k t) -> p k t", k=KC)[:, :, ::-1]
                    dve.tensor_copy(CREV[:, b, :].rearrange("p (k t) -> p k t", k=KC), src).then_inc(s["rev"], 1)
                dve.wait_ge(s["anti"], 2)
                dve.wait_ge(s["toe_ld0"], 16)
                dve.wait_ge(s["d_ld"], 16)
                dve.sem_inc(s["prod"], 4)
                dve.sem_inc(s["red"], 2)

                def toeplitz(h, p):
                    dve.wait_ge(s["y1"], h + 1)
                    at, d = (TOE[:, h, 0:P], DB[:, h:h + 1]) if isinstance(h, int) else \
                        (TOE[:, bass.ds(h, 1), 0:P].squeeze(1), DB[:, bass.ds(h, 1)])
                    dve.scalar_tensor_tensor(TB[p][:, 0:P], ANTI[:, :], d, at, ALU.mult, ALU.add).then_inc(s["toe0"], 1)

                q = c.XNT[:, :, :].rearrange("p k (b t) -> p k b t", b=B)

                def head(h, p, more=True):
                    rows = slice(HD * h, HD * h + HD) if isinstance(h, int) else bass.ds(HD * h, HD)
                    pd = [PD[:, k, :, :].rearrange("p b (j i) -> p b j i", j=HD) for k in range(KC)]
                    for k in range(KC):
                        dve.wait_ge(s["red"], 2 * h + k + 1)
                        dve.wait_ge((s["y0"], s["y1"])[k], h + 1 + 2 * k)
                        dve.tensor_tensor(pd[k], c.bank[2 * p + k][:, :].rearrange("p (b j i) -> p b j i", b=B, j=HD),
                                          bcast(q[:, k, :, rows], 2, HD), ALU.mult).then_inc(s["prod"], 1)
                    if more:
                        toeplitz(h + 2, p)
                    for k in range(KC):
                        dve.wait_ge(s["prod"], 2 * h + k + 5)
                        dve.tensor_reduce(OT[:, k, :, rows], pd[k], AX.X, ALU.add).then_inc(s["red"], 1)

                toeplitz(0, 0)
                toeplitz(1, 1)
                dve.wait_ge(s["toe_ld1"], 16)
                with dve.Fori(0, HC // 2 - 1) as j:
                    head(2 * j, 0)
                    head(2 * j + 1, 1)
                head(HC - 2, 0, False)
                head(HC - 1, 1, False)
                for g in range(B // 2):
                    dve.wait_ge(s["turned_o"], g + 1)
                    xs = c.X[:, 2 * g:2 * g + 2, :]
                    dve.tensor_tensor(xs, xs, c.bank[4 + g][:, :].rearrange("p (b n) -> p b n", b=2), ALU.add).then_inc(s["x_add"], 1)
                    dve.wait_ge(s["x_add"], g + 1)
                    norm.stats(dve, g)
                    if g:
                        norm.scale(dve, g - 1)
                norm.scale(dve, B // 2 - 1)


class Experts:

    def __init__(self, nc, c, st):
        self.F1 = [sb(nc, st, f"mo_f1{p}", [P, KC, HID]) for p in range(2)]
        self.F2 = [sb(nc, st, f"mo_f2{p}", [P, MC, D]) for p in range(2)]
        self.B1 = sb(nc, st, "mo_b1", [P, E0 * MC])
        self.B2 = [sb(nc, st, f"mo_b2{p}", [P, D]) for p in range(2)]
        self.f1_ld = sem_row(nc, st, "mo_f1_ld", 2)
        self.f2_ld = sem_row(nc, st, "mo_f2_ld", 2)
        self.b2_ld = sem_row(nc, st, "mo_b2_ld", 2)
        self.fc1 = c.fc1.rearrange("e (k p) n -> e p k n", p=P)
        self.fc2 = c.fc2.rearrange("e (m p) n -> e p m n", p=P)
        self.fc2b = c.fc2b

    def pick(self, a, e):
        return a[e] if isinstance(e, int) else a[bass.ds(e, 1)].squeeze(0)

    def load_f1(self, sp, e, p):
        sp.dma_start(self.F1[p][:, :, :], self.pick(self.fc1, e)).then_inc(self.f1_ld[p], 16)

    def load_f2(self, sp, e, p):
        sp.dma_start(self.F2[p][:, :, :], self.pick(self.fc2, e)).then_inc(self.f2_ld[p], 16)

    def load_b2(self, sp, e, p):
        row = self.fc2b[e:e + 1, :] if isinstance(e, int) else self.fc2b[bass.ds(e, 1), :]
        sp.dma_start(self.B2[p][:, :], row.broadcast_to([P, D])).then_inc(self.b2_ld[p], 16)


def layer0_rest(nc, c, outer):
    later_weights(nc, c, outer)
    c.G = sb(nc, outer, "mo_gate", [P, TOPK, B])
    c.GIX = sb(nc, outer, "mo_gix", [P, TOPK, B], I32)
    with ExitStack() as st:
        x = Experts(nc, c, st)

        def first_loads(sp):
            for p in range(2):
                x.load_f1(sp, p, p)
                x.load_f2(sp, p, p)
                x.load_b2(sp, p, p)

        with ExitStack() as raw:
            raw_weights(nc, c, raw)
            long_conv(nc, c)
            route(nc, c, x.B1, c.G, c.GIX, first_loads)
        experts(nc, c, x)


def route(nc, c, B1, G, GIX, first_loads):
    NB = TOPK * B
    with ExitStack() as st:
        s = sems(nc, st, "mr_", "w_out w_high w_turned b1_t const logits lg maxed shifted exped summed rsum prob top idx idxf onehot "
                 "gsum gsafe grec gate0 counted tot scan base pos0 pos1 pos valid slot0 slot1 big pv0 pv1 ready")
        TRI = sb(nc, st, "mr_tri", [P, P])
        ONES = sb(nc, st, "mr_ones", [P, P])
        IOTA = sb(nc, st, "mr_iota", [P, E0])
        RST = sb(nc, st, "mr_rst", [P, E0, NB])
        PRB = sb(nc, st, "mr_prb", [P, B, E0])
        MX = sb(nc, st, "mr_mx", [P, B])
        SU = sb(nc, st, "mr_su", [P, B])
        V8 = sb(nc, st, "mr_v8", [P, B, 8])
        I8 = sb(nc, st, "mr_i8", [P, B, 8], U32)
        EID = sb(nc, st, "mr_eid", [P, TOPK, B])
        OH = sb(nc, st, "mr_oh", [P, TOPK, B, E0])
        TOT = sb(nc, st, "mr_tot", [P, E0, NB])
        SCN = sb(nc, st, "mr_scn", [P, E0, NB])
        POE = sb(nc, st, "mr_poe", [P, NB, E0])
        POS = sb(nc, st, "mr_pos", [P, NB])
        VAL = sb(nc, st, "mr_val", [P, NB])
        SLT = sb(nc, st, "mr_slt", [P, NB])
        SLG = sb(nc, st, "mr_slg", [P, NB])
        SIX = sb(nc, st, "mr_six", [P, NB], I32)
        LGB, PRE, TTB = c.bank[0], c.bank[1], c.bank[2]
        with nc.Block() as block:
            @block.sync
            def _(sp):
                first_loads(sp)

            @block.gpsimd
            def _(pool):
                pool.memset(TRI[:, :], 1.0).then_inc(s["const"], 1)
                pool.memset(ONES[:, :], 1.0).then_inc(s["const"], 1)
                pool.memset(RST[:, :, :], 1.0).then_inc(s["const"], 1)
                pool.iota(IOTA[:, :], [[1, E0]], base=0, channel_multiplier=0,
                          allow_small_or_imprecise_dtypes=True).then_inc(s["const"], 1)
                pool.wait_ge(s["const"], 4)
                pool.memset(RST[:, :, 0:1], 0.0).then_inc(s["const"], 1)
                pool.affine_select(out=TRI[:, :], in_=TRI[:, :], compare_op=ALU.is_gt, fill=0.0, base=0,
                                   pattern=[[1, P]], channel_multiplier=-1).then_inc(s["const"], 1)
                pool.wait_ge(s["ready"], 2)
                pool.wait_ge(c.s["disp_zeroed"], 16 * E0)
                for n in range(NB):
                    pool.indirect_dma_start(c.disp, bass.IndirectOffsetOnAxis(ap=SIX[:, n:n + 1], axis=0), c.XN[:, n % B, :], None,
                                            bounds_check=E0 * CAP - 1, oob_is_err=False).then_inc(c.s["scattered"], 16)
                pool.wait_ge(c.s["scattered"], 16 * NB)

            @block.scalar
            def _(act):
                act.wait_ge(s["shifted"], 1)
                act.activation(PRB[:, :, :], PRB[:, :, :], ACT.Exp).then_inc(s["exped"], 1)
                act.wait_ge(s["b1_t"], 1)
                act.activation(B1[:, :], c.bank[3][:, 0:E0 * MC], ACT.Copy)
                turned_high(act, c, s)

            @block.tensor
            def _(pe):
                pe.wait_ge(c.s["router_ld"], 16)
                for b in range(B):
                    for k in range(KC):
                        mm = pe.matmul(LGB[:, b * E0:(b + 1) * E0], c.XNT[:, k, b * S:(b + 1) * S], c.ROUTER[:, k, :],
                                       start=(k == 0), stop=(k == KC - 1))
                mm.then_inc(s["logits"], 1)
                pe.wait_ge(c.s["b1_ld"], 16)
                pe.transpose(c.bank[3][:, 0:E0 * MC], c.B1R[:, :], c.IDN[0:E0 * MC, 0:E0 * MC]).then_inc(s["b1_t"], 1)
                pe.wait_ge(s["const"], 6)
                pe.wait_ge(s["onehot"], 2)
                oh = OH[:, :, :, :].rearrange("p s b e -> p (s b e)")
                pe.matmul(PRE[:, 0:NB * E0], TRI[:, :], oh, start=True, stop=True).then_inc(s["counted"], 1)
                pe.matmul(TTB[:, 0:NB * E0], ONES[:, :], oh, start=True, stop=True).then_inc(s["counted"], 1)
                turn_weights(pe, c, s)

            @block.vector
            def _(dve):
                dve.wait_ge(s["logits"], 1)
                lg = LGB[:, 0:B * E0].rearrange("p (b e) -> p b e", b=B)
                dve.tensor_reduce(MX[:, :], lg, AX.X, ALU.max).then_inc(s["maxed"], 1)
                dve.wait_ge(s["maxed"], 1)
                dve.tensor_tensor(PRB[:, :, :], lg, bcast(MX[:, :], 2, E0), ALU.subtract).then_inc(s["shifted"], 1)
                dve.wait_ge(s["exped"], 1)
                dve.tensor_reduce(SU[:, :], PRB[:, :, :], AX.X, ALU.add).then_inc(s["summed"], 1)
                dve.wait_ge(s["summed"], 1)
                dve.reciprocal(SU[:, :], SU[:, :]).then_inc(s["rsum"], 1)
                dve.wait_ge(s["rsum"], 1)
                dve.tensor_tensor(PRB[:, :, :], PRB[:, :, :], bcast(SU[:, :], 2, E0), ALU.mult).then_inc(s["prob"], 1)
                dve.wait_ge(s["prob"], 1)
                for b in range(B):
                    dve.max(V8[:, b, :], PRB[:, b, :]).then_inc(s["top"], 1)
                for b in range(B):
                    dve.wait_ge(s["top"], b + 1)
                    dve.max_index(I8[:, b, :], V8[:, b, :], PRB[:, b, :]).then_inc(s["idx"], 1)
                dve.wait_ge(s["idx"], B)
                dve.wait_ge(s["const"], 6)
                for t in range(TOPK):
                    dve.tensor_copy(EID[:, t, :], I8[:, :, t]).then_inc(s["idxf"], 1)
                for t in range(TOPK):
                    dve.wait_ge(s["idxf"], t + 1)
                    dve.tensor_tensor(OH[:, t, :, :], bcast(IOTA[:, :], 1, B), bcast(EID[:, t, :], 2, E0), ALU.is_equal).then_inc(s["onehot"], 1)
                dve.tensor_tensor(MX[:, :], V8[:, :, 0], V8[:, :, 1], ALU.add).then_inc(s["gsum"], 1)
                dve.wait_ge(s["gsum"], 1)
                dve.tensor_scalar(MX[:, :], MX[:, :], 1e-9, None, ALU.max).then_inc(s["gsafe"], 1)
                dve.wait_ge(s["gsafe"], 1)
                dve.reciprocal(MX[:, :], MX[:, :]).then_inc(s["grec"], 1)
                dve.wait_ge(s["grec"], 1)
                for t in range(TOPK):
                    dve.tensor_tensor(G[:, t, :], V8[:, :, t], MX[:, :], ALU.mult).then_inc(s["gate0"], 1)
                dve.wait_ge(s["counted"], 2)
                tot = TTB[:, 0:NB * E0].rearrange("p (n e) -> p e n", e=E0)
                dve.tensor_copy(TOT[:, :, :], tot).then_inc(s["tot"], 1)
                dve.wait_ge(s["tot"], 1)
                flat = [a[:, :, :].rearrange("p e n -> p (e n)") for a in (SCN, RST, TOT)]
                dve.tensor_tensor_scan(flat[0], flat[1], flat[2], 0.0, ALU.mult, ALU.add).then_inc(s["scan"], 1)
                dve.wait_ge(s["scan"], 1)
                dve.tensor_tensor(SCN[:, :, :], SCN[:, :, :], TOT[:, :, :], ALU.subtract).then_inc(s["base"], 1)
                dve.wait_ge(s["base"], 1)
                dve.tensor_tensor(POE[:, :, :], PRE[:, 0:NB * E0].rearrange("p (n e) -> p n e", e=E0),
                                  SCN[:, :, :].rearrange("p e n -> p n e"), ALU.add).then_inc(s["pos0"], 1)
                dve.wait_ge(s["pos0"], 1)
                dve.tensor_tensor(POE[:, :, :], POE[:, :, :], OH[:, :, :, :].rearrange("p s b e -> p (s b) e"), ALU.mult).then_inc(s["pos1"], 1)
                dve.wait_ge(s["pos1"], 1)
                dve.tensor_reduce(POS[:, :], POE[:, :, :], AX.X, ALU.add).then_inc(s["pos"], 1)
                dve.wait_ge(s["pos"], 1)
                dve.tensor_scalar(VAL[:, :], POS[:, :], float(CAP), None, ALU.is_lt).then_inc(s["valid"], 1)
                eid = EID[:, :, :].rearrange("p s b -> p (s b)")
                dve.scalar_tensor_tensor(SLT[:, :], eid, float(CAP), POS[:, :], ALU.mult, ALU.add).then_inc(s["slot0"], 1)
                dve.wait_ge(s["valid"], 1)
                dve.tensor_tensor(SLG[:, :], POS[:, :], VAL[:, :], ALU.mult).then_inc(s["pv0"], 1)
                dve.wait_ge(s["pv0"], 1)
                dve.scalar_tensor_tensor(SLG[:, :], eid, float(CAP), SLG[:, :], ALU.mult, ALU.add).then_inc(s["pv1"], 1)
                dve.wait_ge(s["gate0"], TOPK)
                g = G[:, :, :].rearrange("p s b -> p (s b)")
                dve.tensor_tensor(g, g, VAL[:, :], ALU.mult).then_inc(s["gate0"], 1)
                dve.wait_ge(s["gate0"], TOPK + 1)
                dve.tensor_scalar(VAL[:, :], VAL[:, :], -float(BIG), float(BIG), ALU.mult, ALU.add).then_inc(s["big"], 1)
                dve.wait_ge(s["big"], 1)
                dve.wait_ge(s["slot0"], 1)
                dve.tensor_tensor(SLT[:, :], SLT[:, :], VAL[:, :], ALU.add).then_inc(s["slot1"], 1)
                dve.wait_ge(s["slot1"], 1)
                dve.tensor_copy(SIX[:, :], SLT[:, :]).then_inc(s["ready"], 1)
                dve.wait_ge(s["pv1"], 1)
                dve.tensor_copy(GIX[:, :, :].rearrange("p s b -> p (s b)"), SLG[:, :]).then_inc(s["ready"], 1)
                turned_rest(dve, c, s)


def experts(nc, c, x):
    CT = CAP // P
    with ExitStack() as st:
        s = sems(nc, st, "me_", "in0 in1 xt_done xt_high xt_low f1_high f1_low f2_high f2_low h_done h_ev h_high h_low o_done o_ev")
        XE = [c.XN[:, CT * p:CT * p + CT, :] for p in range(2)]
        EO = [c.XN[:, CT * (2 + p):CT * (3 + p), :] for p in range(2)]
        HF = [c.XNT[:, m // 4, (m % 4) * CAP:(m % 4 + 1) * CAP] for m in range(MC)]
        XET = [sb(nc, st, f"me_xet{n}", [P, KC, CAP], F32R) for n in range(2)]
        HT = [sb(nc, st, f"me_ht{n}", [P, MC, CAP], F32R) for n in range(2)]
        W1 = [sb(nc, st, f"me_w1{n}", [P, KC, HID], F32R) for n in range(2)]
        W2 = [[sb(nc, st, f"me_w2{p}{n}", [P, MC, D], F32R) for n in range(2)] for p in range(2)]
        disp = c.disp.rearrange("(e t p) d -> e p t d", p=P, t=CT)
        eo = c.eo.rearrange("(e t p) d -> e p t d", p=P, t=CT)
        XTB, OB = c.bank[0], c.bank[5]
        HB = [c.bank[1], c.bank[2], c.bank[3], c.bank[4]]
        pick = x.pick
        with nc.Block() as block:
            @block.sync
            def _(sp):
                for p in range(2):
                    sp.dma_start(XE[p], pick(disp, p)).then_inc((s["in0"], s["in1"])[p], 16)
                with sp.Fori(1, E0 // 2) as j:
                    for p in range(2):
                        e = 2 * j + p
                        sp.wait_ge(s["xt_done"], e - 1)
                        sp.dma_start(XE[p], pick(disp, e)).then_inc((s["in0"], s["in1"])[p], 16)
                        sp.wait_ge(s["f1_low"], 2 * e - 2)
                        x.load_f1(sp, e, p)
                        sp.wait_ge(s["f2_low"], e - 1)
                        x.load_f2(sp, e, p)
                        sp.wait_ge(s["o_ev"], e)
                        x.load_b2(sp, e, p)

            @block.gpsimd
            def _(pool):
                def split_f2(e, p, n):
                    pool.wait_ge(x.f2_ld[p], 16 * n)
                    if not isinstance(e, int) or e > 1:
                        pool.wait_ge(s["o_done"], e - 1)
                    pool.tensor_tensor(W2[p][0][:, :, :], x.F2[p][:, :, :], bcast(c.ZERO[:, 0:D], 1, MC), ALU.add).then_inc(s["f2_high"], 1)
                    pool.wait_ge(s["f2_high"], e + 1)
                    pool.tensor_tensor(W2[p][1][:, :, :], x.F2[p][:, :, :], W2[p][0][:, :, :].bitcast(F32), ALU.subtract).then_inc(s["f2_low"], 1)

                def store(e, p):
                    pool.wait_ge(s["o_ev"], e + 2)
                    pool.dma_start(pick(eo, e), EO[p]).then_inc((c.s["st0"], c.s["st1"])[p], 16)

                split_f2(0, 0, 1)
                split_f2(1, 1, 1)
                with pool.Fori(0, E0 // 2 - 1) as j:
                    for p in range(2):
                        store(2 * j + p, p)
                        split_f2(2 * j + p + 2, p, j + 2)
                store(E0 - 2, 0)
                store(E0 - 1, 1)
                for p in range(2):
                    pool.wait_ge((c.s["st0"], c.s["st1"])[p], 16 * (E0 // 2))

            @block.tensor
            def _(pe):
                def turn(e, p, n):
                    pe.wait_ge((s["in0"], s["in1"])[p], 16 * n)
                    pe.wait_ge(s["xt_low"], e + 1)
                    for k in range(KC):
                        for t in range(CT):
                            mm = pe.transpose(XTB[:, k * CAP + t * P:k * CAP + (t + 1) * P], XE[p][:, t, k * P:(k + 1) * P], c.IDN[:, :])
                    mm.then_inc(s["xt_done"], 1)

                def expert(e, p, n, nxt=True):
                    pe.wait_ge(s["f1_low"], 2 * e + 2)
                    pe.wait_ge(s["xt_low"], e + 2)
                    for q in range(MC // 2):
                        pe.wait_ge(s["h_ev"], 8 * e + 2 * q + 2)
                        for i in range(2):
                            m = 2 * q + i
                            mm = split_product(pe, HB[q][:, i * CAP:(i + 1) * CAP],
                                               [[w[:, k, m * P:(m + 1) * P] for k in range(KC)] for w in W1],
                                               [[a[:, k, :] for k in range(KC)] for a in XET])
                        mm.then_inc(s["h_done"], 1)
                    if nxt:
                        turn(e + 1, 1 - p, n + p)
                    pe.wait_ge(s["o_ev"], e + 1)
                    pe.wait_ge(s["f2_low"], e + 1)
                    for t in range(CT):
                        for m in range(MC):
                            if t == 0:
                                pe.wait_ge(s["h_low"], 8 * e + m + 9)
                            mm = split_product(pe, OB[:, t * D:(t + 1) * D], [[a[:, m, t * P:(t + 1) * P]] for a in HT],
                                               [[w[:, m, :]] for w in W2[p]], first=(m == 0), last=(m == MC - 1))
                    mm.then_inc(s["o_done"], 1)

                turn(0, 0, 1)
                with pe.Fori(0, E0 // 2 - 1) as j:
                    expert(2 * j, 0, j + 1)
                    expert(2 * j + 1, 1, j + 1)
                expert(E0 - 2, 0, E0 // 2)
                expert(E0 - 1, 1, E0 // 2, False)

            @block.scalar
            def _(act):
                act.sem_inc(s["h_ev"], 8)

                def split_f1(e, p, n):
                    act.wait_ge(x.f1_ld[p], 16 * n)
                    if not isinstance(e, int) or e:
                        act.wait_ge(s["h_done"], 4 * e)
                    for k in range(KC):
                        act.activation(W1[0][:, k, :], x.F1[p][:, k, :], ACT.Copy).then_inc(s["f1_high"], 1)

                def turned(e):
                    act.wait_ge(s["xt_done"], e + 1)
                    act.activation(XET[0][:, :, :], XTB[:, :].rearrange("p (k t) -> p k t", k=KC), ACT.Copy).then_inc(s["xt_high"], 1)

                def high(e, m):
                    act.wait_ge(s["h_ev"], 8 * e + m + 9)
                    act.activation(HT[0][:, m, :], HF[m], ACT.Copy).then_inc(s["h_high"], 1)

                def expert(e, p, n=None):
                    for m in range(MC):
                        act.wait_ge(s["h_done"], 4 * e + m // 2 + 1)
                        act.wait_ge(s["h_low"], 8 * e + m + 1)
                        act.activation(HF[m], HB[m // 2][:, (m % 2) * CAP:(m % 2 + 1) * CAP], ACT.Gelu,
                                       bias=x.B1[:, e * MC + m:e * MC + m + 1] if isinstance(e, int) else x.B1[:, bass.ds(e * MC + m, 1)]).then_inc(s["h_ev"], 1)
                        if m:
                            high(e, m - 1)
                    high(e, MC - 1)
                    if n is not None:
                        turned(e + 1)
                        split_f1(e + 1, 1 - p, n)

                split_f1(0, 0, 1)
                turned(0)
                with act.Fori(0, E0 // 2 - 1) as j:
                    expert(2 * j, 0, j + 1)
                    expert(2 * j + 1, 1, j + 2)
                expert(E0 - 2, 0, E0 // 2)
                expert(E0 - 1, 1)

            @block.vector
            def _(dve):
                dve.sem_inc(s["o_ev"], 1)
                dve.sem_inc(s["xt_low"], 1)
                dve.sem_inc(s["h_low"], 8)

                def turned(e):
                    dve.wait_ge(s["xt_high"], e + 1)
                    dve.tensor_tensor(XET[1][:, :, :], XTB[:, :].rearrange("p (k t) -> p k t", k=KC), XET[0][:, :, :].bitcast(F32), ALU.subtract).then_inc(s["xt_low"], 1)

                def split_f1(e, p):
                    for k in range(KC):
                        dve.wait_ge(s["f1_high"], 2 * e + k + 1)
                        dve.tensor_tensor(W1[1][:, k, :], x.F1[p][:, k, :], W1[0][:, k, :].bitcast(F32), ALU.subtract).then_inc(s["f1_low"], 1)

                def expert(e, p, n, stored=None, nxt=True):
                    for m in range(MC):
                        dve.wait_ge(s["h_high"], 8 * e + m + 1)
                        dve.tensor_tensor(HT[1][:, m, :], HF[m], HT[0][:, m, :].bitcast(F32), ALU.subtract).then_inc(s["h_low"], 1)
                    if nxt:
                        turned(e + 1)
                        split_f1(e + 1, 1 - p)
                    dve.wait_ge(s["o_done"], e + 1)
                    dve.wait_ge(x.b2_ld[p], 16 * n)
                    if stored is not None:
                        dve.wait_ge((c.s["st0"], c.s["st1"])[p], 16 * stored)
                    dve.tensor_tensor(EO[p], OB[:, :].rearrange("p (t n) -> p t n", t=CT),
                                      bcast(x.B2[p][:, :], 1, CT), ALU.add).then_inc(s["o_ev"], 1)

                split_f1(0, 0)
                turned(0)
                for p in range(2):
                    expert(p, p, 1)
                with dve.Fori(1, E0 // 2 - 1) as j:
                    for p in range(2):
                        expert(2 * j + p, p, j + 1, j)
                expert(E0 - 2, 0, E0 // 2, E0 // 2 - 1)
                expert(E0 - 1, 1, E0 // 2, E0 // 2 - 1, False)


def attention1(nc, c, before, norm):
    HPC = P // HD1
    VW = HD1 + 1
    with ExitStack() as st:
        WT, WOT = c.WT, c.WOT
        s = sems(nc, st, "at_", "bias_ld const xb qk_done qk_ev kx kx_d v_done v_ev sc_done masked maxed sub_d sub_p exped "
                 "pt_done pt_ev pv_done rsum norm ot_done ot_ev out_done x_add x_b x_add0 x_add1 own")
        GA = sb(nc, st, "mc_ga", [P, B, TOPK, D])
        BQK = sb(nc, st, "at_bqk", [P, 4])
        BV = sb(nc, st, "at_bv", [P, D])
        BO = sb(nc, st, "at_bo", [P, D])
        OWN = sb(nc, st, "at_own", [P, HPC])
        MASK = sb(nc, st, "at_mask", [P, S])
        XB = [sb(nc, st, f"at_xb{p}", [P, KC, S]) for p in range(2)]
        QK = sb(nc, st, "at_qk", [P, 4, S])
        KX = sb(nc, st, "at_kx", [P, H1, S])
        VA = [sb(nc, st, f"at_v{p}", [P, H1, VW]) for p in range(2)]
        SM = [sb(nc, st, f"at_sm{p}", [P, H1, S]) for p in range(2)]
        MX = [sb(nc, st, f"at_mx{p}", [P, H1]) for p in range(2)]
        PT = sb(nc, st, "at_pt", [P, H1, S])
        RS = sb(nc, st, "at_rs", [P, H1])
        AO = sb(nc, st, "at_ao", [P, H1, HD1])
        AOT = sb(nc, st, "at_aot", [P, KC, S])
        SCB = c.bank[0:4]
        QKB, VOB = c.bank[4], c.bank[5]
        PTB = [c.bank[6], c.bank[7]]
        HH = H1 // 2
        TB = [c.bank[5], c.bank[7], c.bank[7], c.bank[7]]
        with nc.Block() as block:
            @block.sync
            def _(sp):
                with nc.allow_non_contiguous_dma(reason="four columns"):
                    sp.dma_start(BQK[:, :], c.bqkv[0:2 * D].rearrange("(m p) -> p m", p=P)).then_inc(s["bias_ld"], 16)
                sp.dma_start(BV[:, :], c.bqkv[2 * D:3 * D].rearrange("(a n) -> a n", a=1).broadcast_to([P, D])).then_inc(s["bias_ld"], 16)
                sp.dma_start(BO[:, :], c.bout.rearrange("(a n) -> a n", a=1).broadcast_to([P, D])).then_inc(s["bias_ld"], 16)

            @block.gpsimd
            def _(pool):
                def gather(b):
                    for t in range(TOPK):
                        pool.indirect_dma_start(GA[:, b, t, :], None, c.eo, bass.IndirectOffsetOnAxis(ap=c.GIX[:, t, b:b + 1], axis=0),
                                                bounds_check=E0 * CAP - 1, oob_is_err=False).then_inc(c.got[b], 16)

                gather(0)
                pool.memset(MASK[:, :], 0.0).then_inc(s["const"], 1)
                for p in range(2):
                    pool.memset(VA[p][:, :, HD1:VW], 1.0).then_inc(s["const"], 1)
                pool.wait_ge(s["const"], 3)
                pool.affine_select(out=MASK[:, :], in_=MASK[:, :], compare_op=ALU.is_ge, fill=NEG, base=0,
                                   pattern=[[-1, S]], channel_multiplier=1).then_inc(s["const"], 1)

                def take(b, p):
                    if isinstance(b, int):
                        pool.wait_ge(before.s["evac"], b // 2 + 1)
                    pool.wait_ge(s["const"], 3)
                    src = c.XNT[:, :, b * S:(b + 1) * S] if isinstance(b, int) else c.XNT[:, :, bass.ds(b * S, S)]
                    pool.tensor_copy(XB[p][:, :, :], src).then_inc(s["xb"], 1)

                def spread_keys(b):
                    pool.wait_ge(s["qk_ev"], 4 * b + 4)
                    if not isinstance(b, int) or b:
                        pool.wait_ge(s["sc_done"], b)
                    pool.tensor_tensor(KX[:, 0:HPC, :], bcast(QK[:, KC, :], 1, HPC),
                                       bcast(OWN[:, :], 2, S), ALU.mult).then_inc(s["kx"], 1)

                def subtract(b, p):
                    pool.wait_ge(s["maxed"], b + 1)
                    pool.tensor_tensor(SM[p][:, HH:H1, :], SM[p][:, HH:H1, :], bcast(MX[p][:, HH:H1], 2, S), ALU.subtract).then_inc(s["sub_p"], 1)

                def batch(b, p, more=2, take_more=True):
                    if more > 1:
                        spread_keys(b + 2)
                    if more:
                        subtract(b + 1, 1 - p)
                    if take_more:
                        pool.wait_ge(s["v_done"], b + 2)
                        take(b + 3, 1 - p)

                for b in range(1, 4):
                    gather(b)
                take(0, 0)
                take(1, 1)
                gather(4)
                pool.wait_ge(s["own"], 1)
                spread_keys(0)
                for b in range(5, B):
                    gather(b)
                pool.wait_ge(s["v_done"], 1)
                take(2, 0)
                spread_keys(1)
                subtract(0, 0)
                batch(0, 0)
                batch(1, 1)
                pool.wait_ge(before.s["evac"], B // 2)
                with pool.Fori(1, B // 2 - 2) as j:
                    batch(2 * j, 0)
                    batch(2 * j + 1, 1)
                batch(B - 4, 0)
                batch(B - 3, 1, 2, False)
                batch(B - 2, 0, 1, False)

            @block.tensor
            def _(pe):
                def project_qk(b, p):
                    pe.wait_ge(s["xb"], b + 1)
                    if not isinstance(b, int) or b:
                        pe.wait_ge(s["qk_ev"], 4 * b)
                    for m in range(4):
                        for k in range(KC):
                            mm = pe.matmul(QKB[:, m * S:(m + 1) * S], WT[:, k, m * P:(m + 1) * P], XB[p][:, k, :],
                                           start=(k == 0), stop=(k == KC - 1))
                    mm.then_inc(s["qk_done"], 1)

                def project_v(b, p):
                    if isinstance(b, int) and b == 1:
                        pe.wait_ge(s["v_ev"], 1)
                    for k in range(KC):
                        mm = pe.matmul(PTB[0][:, 0:D], XB[p][:, k, :], WT[:, k, 2 * D:3 * D], start=(k == 0), stop=(k == KC - 1))
                    mm.then_inc(s["v_done"], 1)

                def scores(b):
                    pe.wait_ge(s["qk_ev"], 4 * b + 4)
                    pe.wait_ge(s["kx"], b + 1)
                    pe.wait_ge(s["kx_d"], b + 1)
                    for j in range(4):
                        if not isinstance(b, int) or b:
                            pe.wait_ge(s["masked"], 4 * b + j - 3)
                        mm = pe.matmul(SCB[j][:, :], QK[:, j // 2, :], KX[:, 4 * j:4 * j + 4, :].rearrange("p h t -> p (h t)"),
                                       start=True, stop=True)
                    mm.then_inc(s["sc_done"], 1)

                def attend(b, p, v_next):
                    pe.wait_ge(s["v_ev"], b + 1 + v_next)
                    for g in range(4):
                        pe.wait_ge(s["exped"], 2 * b + 1 + g // 2)
                        pe.wait_ge(s["pt_ev"], 4 * b + g + 1)
                        for i in range(4):
                            mm = pe.transpose(PTB[g % 2][:, i * S:(i + 1) * S], SM[p][:, 4 * g + i, :], c.IDN[:, :])
                        mm.then_inc(s["pt_done"], 1)
                    pe.wait_ge(s["x_add"], b + 1)
                    for h in range(H1):
                        if h % 4 == 0:
                            pe.wait_ge(s["pt_ev"], 4 * b + h // 4 + 3)
                        mm = pe.matmul(VOB[:, h * VW:(h + 1) * VW], PT[:, h, :], VA[p][:, h, :], start=True, stop=True)
                    mm.then_inc(s["pv_done"], 1)

                def turn_result(b):
                    pe.wait_ge(s["norm"], b + 1)
                    for k in range(KC):
                        mm = pe.transpose(VOB[:, k * S:(k + 1) * S], AO[:, k * HPC:(k + 1) * HPC, :].rearrange("p h d -> p (h d)"), c.IDN[:, :])
                    mm.then_inc(s["ot_done"], 1)

                def output(b):
                    pe.wait_ge(s["ot_ev"], b + 1)
                    for k in range(KC):
                        mm = pe.matmul(VOB[:, 0:D], AOT[:, k, :], WOT[:, k, :], start=(k == 0), stop=(k == KC - 1))
                    mm.then_inc(s["out_done"], 1)

                def batch(b, p, more=2):
                    if more:
                        scores(b + 1)
                    attend(b, p, 1 if more else 0)
                    if more > 1:
                        project_qk(b + 2, p)
                    turn_result(b)
                    if more > 1:
                        project_v(b + 2, p)
                    if isinstance(b, int) and b < 2:
                        pe.wait_ge(s["pt_ev"], 4 * b + 6)
                        before.turn(pe, b + 2, TB[b + 2])
                    output(b)
                    if isinstance(b, int) and b < 2:
                        pe.wait_ge(before.s["evac"], b + 3)

                before.turn(pe, 0, TB[0])
                project_qk(0, 0)
                project_v(0, 0)
                scores(0)
                before.turn(pe, 1, TB[1])
                project_qk(1, 1)
                project_v(1, 1)
                pe.wait_ge(before.s["evac"], 2)
                batch(0, 0)
                batch(1, 1)
                with pe.Fori(1, B // 2 - 1) as j:
                    batch(2 * j, 0)
                    batch(2 * j + 1, 1)
                batch(B - 2, 0, 1)
                batch(B - 1, 1, 0)

            @block.scalar
            def _(act):
                act.sem_inc(s["pt_ev"], 2)

                def projected(b):
                    act.wait_ge(s["qk_done"], b + 1)
                    if not isinstance(b, int) or b > 0:
                        act.wait_ge(s["sc_done"], b)
                        act.wait_ge(s["kx"], b)
                        act.wait_ge(s["kx_d"], b)
                    for m in (2, 3, 0, 1):
                        act.activation(QK[:, m, :], QKB[:, m * S:(m + 1) * S], ACT.Identity, bias=BQK[:, m:m + 1]).then_inc(s["qk_ev"], 1)

                def exps(b, p):
                    act.wait_ge(s["sub_d"], b + 1)
                    act.activation(SM[p][:, 0:HH, :], SM[p][:, 0:HH, :], ACT.Exp).then_inc(s["exped"], 1)
                    act.wait_ge(s["sub_p"], b + 1)
                    act.activation(SM[p][:, HH:H1, :], SM[p][:, HH:H1, :], ACT.Exp).then_inc(s["exped"], 1)

                def batch(b, p, more=2):
                    for g in range(4):
                        act.wait_ge(s["pt_done"], 4 * b + g + 1)
                        act.activation(PT[:, 4 * g:4 * g + 4, :], PTB[g % 2][:, :].rearrange("p (h t) -> p h t", h=4), ACT.Copy).then_inc(s["pt_ev"], 1)
                    if more > 1:
                        projected(b + 2)
                    act.wait_ge(s["ot_done"], b + 1)
                    act.activation(AOT[:, :, :], VOB[:, 0:KC * S].rearrange("p (k t) -> p k t", k=KC), ACT.Copy).then_inc(s["ot_ev"], 1)
                    if isinstance(b, int) and b < 2:
                        before.copy(act, b + 2, TB[b + 2])
                    if more:
                        exps(b + 1, 1 - p)
                    if isinstance(b, int) and b == 0:
                        before.root(act, 3)

                before.root(act, 0)
                before.copy(act, 0, TB[0])
                act.wait_ge(s["bias_ld"], 48)
                projected(0)
                before.root(act, 1)
                before.copy(act, 1, TB[1])
                projected(1)
                exps(0, 0)
                before.root(act, 2)
                batch(0, 0)
                batch(1, 1)
                with act.Fori(1, B // 2 - 1) as j:
                    batch(2 * j, 0)
                    batch(2 * j + 1, 1)
                batch(B - 2, 0, 1)
                batch(B - 1, 1, 0)

            @block.vector
            def _(dve):
                dve.sem_inc(s["x_add"], 1)
                dve.tensor_reduce(OWN[:, :], c.IDN[:, :].rearrange("p (h r) -> p h r", h=HPC), AX.X, ALU.add).then_inc(s["own"], 1)

                def combine(q):
                    for b in (2 * q, 2 * q + 1):
                        dve.wait_ge(c.got[b], 16 * TOPK)
                        x = c.X[:, b, :]
                        dve.scalar_tensor_tensor(x, GA[:, b, 0, :], c.G[:, 0, b:b + 1], x, ALU.mult, ALU.add).then_inc(s["x_add0"], 1)
                        dve.wait_ge(s["x_add0"], b + 1)
                        dve.scalar_tensor_tensor(x, GA[:, b, 1, :], c.G[:, 1, b:b + 1], x, ALU.mult, ALU.add).then_inc(s["x_add1"], 1)
                    dve.wait_ge(s["x_add1"], 2 * q + 2)
                    before.stats(dve, q)
                    before.scale(dve, q)
                    dve.wait_ge(s["bias_ld"], 48)
                    dve.wait_ge(before.s["xn"], 2 * q + 2)
                    x = c.X[:, 2 * q:2 * q + 2, :]
                    dve.tensor_tensor(x, x, bcast(BO[:, :], 1, 2), ALU.add).then_inc(s["x_b"], 1)

                def values(b, p):
                    dve.wait_ge(s["v_done"], b + 1)
                    dve.tensor_tensor(VA[p][:, :, 0:HD1], PTB[0][:, 0:D].rearrange("p (h d) -> p h d", h=H1),
                                      BV[:, :].rearrange("p (h d) -> p h d", h=H1), ALU.add).then_inc(s["v_ev"], 1)

                def spread_keys(b):
                    dve.wait_ge(s["qk_ev"], 4 * b + 4)
                    if not isinstance(b, int) or b:
                        dve.wait_ge(s["sc_done"], b)
                    dve.tensor_tensor(KX[:, HPC:H1, :], bcast(QK[:, KC + 1, :], 1, HPC),
                                      bcast(OWN[:, :], 2, S), ALU.mult).then_inc(s["kx_d"], 1)

                def softmax(b, p):
                    dve.wait_ge(s["sc_done"], b + 1)
                    for j in range(4):
                        dve.scalar_tensor_tensor(SM[p][:, 4 * j:4 * j + 4, :], SCB[j][:, :].rearrange("p (h t) -> p h t", h=4),
                                                 float(HD1) ** -0.5, bcast(MASK[:, :], 1, 4), ALU.mult, ALU.add).then_inc(s["masked"], 1)
                    dve.wait_ge(s["masked"], 4 * b + 4)
                    dve.tensor_reduce(MX[p][:, :], SM[p][:, :, :], AX.X, ALU.max).then_inc(s["maxed"], 1)
                    dve.wait_ge(s["maxed"], b + 1)
                    dve.tensor_tensor(SM[p][:, 0:HH, :], SM[p][:, 0:HH, :], bcast(MX[p][:, 0:HH], 2, S), ALU.subtract).then_inc(s["sub_d"], 1)

                def batch(b, p, more=2):
                    if more:
                        softmax(b + 1, 1 - p)
                    dve.wait_ge(s["pv_done"], b + 1)
                    ov = VOB[:, 0:H1 * VW].rearrange("p (h d) -> p h d", h=H1)
                    dve.reciprocal(RS[:, :], ov[:, :, HD1]).then_inc(s["rsum"], 1)
                    dve.wait_ge(s["rsum"], b + 1)
                    dve.tensor_tensor(AO[:, :, :], ov[:, :, 0:HD1], bcast(RS[:, :], 2, HD1), ALU.mult).then_inc(s["norm"], 1)
                    if more > 1:
                        spread_keys(b + 2)
                        values(b + 2, p)
                    dve.wait_ge(s["out_done"], b + 1)
                    x = c.X[:, b, :] if isinstance(b, int) else c.X[:, bass.ds(b, 1), :].squeeze(1)
                    dve.tensor_tensor(x, x, VOB[:, 0:D], ALU.add).then_inc(s["x_add"], 1)
                    dve.wait_ge(s["x_add"], b + 2)
                    norm.moments(dve, b)

                combine(0)
                dve.wait_ge(s["const"], 4)
                dve.wait_ge(s["own"], 1)
                values(0, 0)
                spread_keys(0)
                combine(1)
                softmax(0, 0)
                values(1, 1)
                spread_keys(1)
                dve.wait_ge(s["x_b"], 2)
                combine(2)
                batch(0, 0)
                combine(3)
                batch(1, 1)
                dve.wait_ge(s["x_b"], B // 2)
                with dve.Fori(1, B // 2 - 1) as j:
                    batch(2 * j, 0)
                    batch(2 * j + 1, 1)
                batch(B - 2, 0, 1)
                batch(B - 1, 1, 0)


def cross1(nc, c, before, norm):
    LT = D // P
    with ExitStack() as st:
        QWT, KWT, VWT = c.QWT, c.KWT, c.VWT
        s = sems(nc, st, "cr_", "bias_ld cb q_done k_done v_done q_ev k_ev v_ev sc_done maxed negated exped "
                 "rsum norm pt_done pt_ev h_done x_add")
        BI = sb(nc, st, "cr_bi", [P, 3])
        CB = [sb(nc, st, f"cr_cb{p}", [P, D]) for p in range(2)]
        Q = sb(nc, st, "cr_q", [P, D])
        K = sb(nc, st, "cr_k", [P, D])
        V = [sb(nc, st, f"cr_v{p}", [P, LT, S]) for p in range(2)]
        PR = [sb(nc, st, f"cr_pr{p}", [P, LT, D]) for p in range(2)]
        MX = sb(nc, st, "cr_mx", [P, LT])
        NM = [sb(nc, st, f"cr_nm{p}", [P, LT]) for p in range(2)]
        RS = [sb(nc, st, f"cr_rs{p}", [P, LT]) for p in range(2)]
        PT = sb(nc, st, "cr_pt", [P, LT, D])
        QB, KB, VB, SB0, SB1, PTB, HB = c.bank[0], c.bank[1], c.bank[2], c.bank[3], c.bank[4], c.bank[5], c.bank[6]
        SCB = [SB0, SB1]
        with nc.Block() as block:
            @block.sync
            def _(sp):
                with nc.allow_non_contiguous_dma(reason="three columns"):
                    for i, bias in enumerate((c.Qb, c.Kb, c.Vb)):
                        sp.dma_start(BI[:, i:i + 1], bias.rearrange("(p a) -> p a", a=1)).then_inc(s["bias_ld"], 16)

            @block.gpsimd
            def _(pool):
                def take(b, p):
                    src = c.CTX[:, b, :] if isinstance(b, int) else c.CTX[:, bass.ds(b, 1), :].squeeze(1)
                    pool.tensor_copy(CB[p][:, :], src).then_inc(s["cb"], 1)

                pool.wait_ge(c.s["ctx_loaded"], 16)
                take(0, 0)
                take(1, 1)
                with pool.Fori(1, B // 2) as j:
                    for p in range(2):
                        pool.wait_ge(s["v_done"], 2 * j + p - 1)
                        take(2 * j + p, p)

            @block.tensor
            def _(pe):
                def project(b, p):
                    pe.wait_ge(s["cb"], b + 1)
                    pe.wait_ge(s["k_ev"], b + 1)
                    pe.matmul(KB[:, 0:D], KWT[:, 0, :], CB[p][:, :], start=True, stop=True).then_inc(s["k_done"], 1)
                    pe.wait_ge(s["v_ev"], b + 1)
                    for t in range(LT):
                        mm = pe.matmul(VB[:, t * S:(t + 1) * S], CB[p][:, t * P:(t + 1) * P], VWT[:, 0, :], start=True, stop=True)
                    mm.then_inc(s["v_done"], 1)
                    if isinstance(b, int):
                        pe.wait_ge(before.s["xn"], b + 1)
                    xn = c.XN[:, b, :] if isinstance(b, int) else c.XN[:, bass.ds(b, 1), :].squeeze(1)
                    pe.wait_ge(s["q_ev"], b + 1)
                    pe.matmul(QB[:, 0:D], QWT[:, 0, :], xn, start=True, stop=True).then_inc(s["q_done"], 1)

                def scores(b, p):
                    pe.wait_ge(s["q_ev"], b + 2)
                    pe.wait_ge(s["k_ev"], b + 2)
                    for t in range(LT):
                        mm = pe.matmul(SCB[p][:, t * D:(t + 1) * D], Q[:, t * P:(t + 1) * P], K[:, :], start=True, stop=True)
                    mm.then_inc(s["sc_done"], 1)

                def attend(b, p):
                    pe.wait_ge(s["norm"], 2 * b + 2)
                    pe.wait_ge(s["pt_ev"], b + 1)
                    for u in range(LT):
                        for t in range(LT):
                            mm = pe.transpose(PTB[:, u * D + t * P:u * D + (t + 1) * P], PR[p][:, t, u * P:(u + 1) * P], c.IDN[:, :])
                    mm.then_inc(s["pt_done"], 1)

                def output(b, p):
                    pe.wait_ge(s["pt_ev"], b + 2)
                    pe.wait_ge(s["v_ev"], b + 2)
                    pe.wait_ge(s["x_add"], b + 1)
                    for u in range(LT):
                        mm = pe.matmul(HB[:, 0:D], V[p][:, u, :], PT[:, u, :], start=(u == 0), stop=(u == LT - 1))
                    mm.then_inc(s["h_done"], 1)

                def batch(b, p, more=True):
                    if more:
                        project(b + 2, p)
                    attend(b, p)
                    if more:
                        scores(b + 2, p)
                    output(b, p)

                for b in range(2):
                    project(b, b)
                    scores(b, b)
                pe.wait_ge(before.s["xn"], B)
                with pe.Fori(0, B // 2 - 1) as j:
                    batch(2 * j, 0)
                    batch(2 * j + 1, 1)
                batch(B - 2, 0, False)
                batch(B - 1, 1, False)

            @block.scalar
            def _(act):
                act.sem_inc(s["q_ev"], 1)
                act.sem_inc(s["k_ev"], 1)
                act.sem_inc(s["pt_ev"], 1)
                for q in range(B // 2):
                    before.root(act, q)
                act.wait_ge(s["bias_ld"], 48)

                def project(b):
                    act.wait_ge(s["k_done"], b + 1)
                    if not isinstance(b, int) or b:
                        act.wait_ge(s["sc_done"], b)
                    act.activation(K[:, :], KB[:, 0:D], ACT.Identity, bias=BI[:, 1:2]).then_inc(s["k_ev"], 1)
                    act.wait_ge(s["q_done"], b + 1)
                    act.activation(Q[:, :], QB[:, 0:D], ACT.Identity, bias=BI[:, 0:1]).then_inc(s["q_ev"], 1)

                def exps(b, p):
                    act.wait_ge(s["negated"], b + 1)
                    for t in range(LT):
                        act.activation(PR[p][:, t, :], SCB[p][:, t * D:(t + 1) * D], ACT.Exp, bias=NM[p][:, t:t + 1],
                                       accum_out=RS[p][:, t:t + 1]).then_inc(s["exped"], 1)

                def batch(b, p, more=True):
                    if more:
                        project(b + 2)
                    act.wait_ge(s["pt_done"], b + 1)
                    act.activation(PT[:, :, :], PTB[:, :].rearrange("p (u q) -> p u q", u=LT), ACT.Copy).then_inc(s["pt_ev"], 1)
                    if more:
                        exps(b + 2, p)

                for b in range(2):
                    project(b)
                    exps(b, b)
                with act.Fori(0, B // 2 - 1) as j:
                    batch(2 * j, 0)
                    batch(2 * j + 1, 1)
                batch(B - 2, 0, False)
                batch(B - 1, 1, False)

            @block.vector
            def _(dve):
                dve.sem_inc(s["v_ev"], 1)
                dve.sem_inc(s["x_add"], 1)
                for q in range(B // 2):
                    before.join(dve, q)
                for q in range(B // 2):
                    before.scale(dve, q)
                dve.wait_ge(s["bias_ld"], 48)

                def greatest(b, p):
                    dve.wait_ge(s["sc_done"], b + 1)
                    dve.tensor_reduce(MX[:, :], SCB[p][:, :].rearrange("p (t k) -> p t k", t=LT), AX.X, ALU.max).then_inc(s["maxed"], 1)
                    dve.wait_ge(s["maxed"], b + 1)
                    dve.tensor_scalar(NM[p][:, :], MX[:, :], -1.0, None, ALU.mult).then_inc(s["negated"], 1)

                def values(b, p):
                    dve.wait_ge(s["v_done"], b + 1)
                    dve.tensor_copy(V[p][:, :, :], VB[:, 0:LT * S].rearrange("p (t e) -> p t e", t=LT)).then_inc(s["v_ev"], 1)

                def normalise(b, p):
                    dve.wait_ge(s["exped"], 2 * b + 2)
                    dve.reciprocal(RS[p][:, :], RS[p][:, :]).then_inc(s["rsum"], 1)
                    dve.wait_ge(s["rsum"], b + 1)
                    for t in range(LT):
                        dve.tensor_scalar(PR[p][:, t, :], PR[p][:, t, :], RS[p][:, t:t + 1], None, ALU.mult).then_inc(s["norm"], 1)

                def add(b):
                    dve.wait_ge(s["h_done"], b + 1)
                    x = c.X[:, b, :] if isinstance(b, int) else c.X[:, bass.ds(b, 1), :].squeeze(1)
                    dve.scalar_tensor_tensor(x, HB[:, 0:D], BI[:, 2:3], x, ALU.add, ALU.add).then_inc(s["x_add"], 1)

                def batch(b, p, more=True):
                    if more:
                        greatest(b + 2, p)
                    add(b)
                    if more:
                        values(b + 2, p)
                        normalise(b + 2, p)
                    dve.wait_ge(s["x_add"], b + 2)
                    norm.moments(dve, b)

                for b in range(2):
                    values(b, b)
                    greatest(b, b)
                    normalise(b, b)
                with dve.Fori(0, B // 2 - 1) as j:
                    batch(2 * j, 0)
                    batch(2 * j + 1, 1)
                batch(B - 2, 0, False)
                batch(B - 1, 1, False)


def layer1(nc, c):
    with ExitStack() as st:
        ln6 = Norm(nc, c, st, "ln6_")
        with ExitStack() as st5:
            ln5 = Norm(nc, c, st5, "ln5_")
            with ExitStack() as st4:
                attention1(nc, c, Norm(nc, c, st4, "ln4_"), ln5)
            cross1(nc, c, ln5, ln6)
        c.XNTH = sb(nc, st, "xnth6", [P, KC, T], F32R)
        c.XNTL = sb(nc, st, "xntl6", [P, KC, T], F32R)
        swiglu(nc, c, ln6)


def swiglu(nc, c, before):
    NT = 256
    NQ = T // NT
    QT = NT // S
    with ExitStack() as st:
        s = sems(nc, st, "sw_", "gu_done sig h_ev h_high h_low o_done x_add")
        SG = sb(nc, st, "sw_sg", [P, MC, NT])
        HF = sb(nc, st, "sw_hf", [P, MC, NT])
        HH = [sb(nc, st, f"sw_hh{p}", [P, MC, NT], F32R) for p in range(2)]
        HL = [sb(nc, st, f"sw_hl{p}", [P, MC, NT], F32R) for p in range(2)]
        OB = c.bank[6]
        TB = [c.bank[4], c.bank[5], c.bank[7], c.bank[6]]
        with nc.Block() as block:
            @block.sync
            def _(sp):
                for n in range(NQ):
                    sp.wait_ge(s["x_add"], n + 2)
                    sp.dma_start(c.out[n * QT:(n + 1) * QT].rearrange("b p d -> p b d"), c.X[:, n * QT:(n + 1) * QT, :]).then_inc(c.s["out"], 16)
                sp.wait_ge(c.s["out"], 16 * NQ)
                sp.wait_ge(c.s["disp_zeroed"], 16 * E0)

            @block.tensor
            def _(pe):
                def hidden(n):
                    at = slice(n * NT, (n + 1) * NT) if isinstance(n, int) else bass.ds(n * NT, NT)
                    x = [a[:, :, at] for a in (c.XNTH, c.XNTL)]
                    pe.wait_ge(before.s["low"], n + 1)
                    for m in range(MC):
                        pe.wait_ge(s["h_ev"], 8 * n + m + 5)
                        for i, w in enumerate((c.WG, c.WU)):
                            mm = split_product(pe, c.bank[m % 4][:, i * NT:(i + 1) * NT],
                                               [[a[:, k, m * P:(m + 1) * P] for k in range(KC)] for a in w],
                                               [[a[:, k, :] for k in range(KC)] for a in x])
                        mm.then_inc(s["gu_done"], 1)

                def down(n, p):
                    pe.wait_ge(s["h_low"], 8 * n + 16)
                    pe.wait_ge(s["x_add"], n + 1)
                    for t in range(QT):
                        mm = split_product(pe, OB[:, t * D:(t + 1) * D],
                                           [[a[:, m, t * P:(t + 1) * P] for m in range(MC)] for a in (HH[p], HL[p])],
                                           [[a[:, m, :] for m in range(MC)] for a in c.WD])
                    mm.then_inc(s["o_done"], 1)

                for q in range(B // 2):
                    before.turn(pe, q, TB[q])
                hidden(0)
                with pe.Fori(0, NQ // 2 - 1) as j:
                    hidden(2 * j + 1)
                    down(2 * j, 0)
                    hidden(2 * j + 2)
                    down(2 * j + 1, 1)
                hidden(NQ - 1)
                down(NQ - 2, 0)
                down(NQ - 1, 1)

            @block.scalar
            def _(act):
                def high(n, m, p):
                    act.wait_ge(s["h_ev"], 8 * n + m + 9)
                    act.activation(HH[p][:, m, :], HF[:, m, :], ACT.Copy).then_inc(s["h_high"], 1)

                for q in range(B // 2):
                    before.root(act, q)
                for q in range(B // 2):
                    before.high(act, q, TB[q])
                with act.Fori(0, NQ // 2) as j:
                    for p in range(2):
                        n = 2 * j + p
                        for m in range(MC):
                            act.wait_ge(s["gu_done"], 8 * n + m + 1)
                            act.wait_ge(s["h_ev"], 8 * n + m + 1)
                            act.activation(SG[:, m, :], c.bank[m % 4][:, 0:NT], ACT.Silu).then_inc(s["sig"], 1)
                            if m:
                                high(n, m - 1, p)
                        high(n, MC - 1, p)

            @block.gpsimd
            def _(pool):
                pool.sem_inc(s["h_low"], 8)
                with pool.Fori(0, NQ // 2) as j:
                    for p in range(2):
                        for m in range(MC):
                            pool.wait_ge(s["h_high"], 16 * j + 8 * p + m + 1)
                            pool.tensor_tensor(HL[p][:, m, :], HF[:, m, :], HH[p][:, m, :].bitcast(F32), ALU.subtract).then_inc(s["h_low"], 1)

            @block.vector
            def _(dve):
                dve.sem_inc(s["h_ev"], 8)
                dve.sem_inc(s["x_add"], 1)
                for q in range(B // 2):
                    before.join(dve, q)
                for q in range(B // 2):
                    before.scale(dve, q)
                for q in range(B // 2):
                    before.low(dve, q, TB[q])

                def quarter(n):
                    for m in range(MC):
                        dve.wait_ge(s["sig"], 8 * n + m + 1)
                        dve.wait_ge(s["h_low"], 8 * n + m + 1)
                        dve.tensor_tensor(HF[:, m, :], SG[:, m, :], c.bank[m % 4][:, NT:2 * NT], ALU.mult).then_inc(s["h_ev"], 1)

                def add(n):
                    dve.wait_ge(s["o_done"], n + 1)
                    x = c.X[:, n * QT:(n + 1) * QT, :] if isinstance(n, int) else c.X[:, bass.ds(n * QT, QT), :]
                    dve.tensor_tensor(x, x, OB[:, :].rearrange("p (t n) -> p t n", t=QT), ALU.add).then_inc(s["x_add"], 1)

                quarter(0)
                with dve.Fori(0, NQ - 1) as n:
                    quarter(n + 1)
                    add(n)
                add(NQ - 1)


def build(nc, c):
    with ExitStack() as stack:
        c.s = {n: stack.enter_context(nc.semaphore(n)) for n in
               "x_loaded ctx_loaded const zeros_ready disp_zeroed pad_st beta_ld sign beta router_ld b1_ld scattered st0 st1 out".split()}
        c.got = [stack.enter_context(nc.semaphore(f"got{b}")) for b in range(B)]
        c.bank = [stack.enter_context(nc.psum_tensor(f"bank{i}", [P, 512], F32)) for i in range(8)]
        c.X = sb(nc, stack, "X", [P, B, D])
        c.CTX = sb(nc, stack, "CTX", [P, B, D])
        c.XN = sb(nc, stack, "XN", [P, B, D])
        c.XNT = sb(nc, stack, "XNT", [P, KC, T])
        c.IDN = sb(nc, stack, "IDN", [P, P])
        c.MASK0 = sb(nc, stack, "MASK0", [P, SEG])
        c.ZERO = sb(nc, stack, "ZERO", [P, 2 * D])
        c.disp = nc.dram_tensor("disp", [E0 * CAP, D], F32, kind="Internal").ap()
        c.eo = nc.dram_tensor("eo", [E0 * CAP, D], F32, kind="Internal").ap()
        c.pad = nc.dram_tensor("pad", [HC, 384], F32, kind="Internal").ap()
        attend_infini(nc, c)
        layer0_rest(nc, c, stack)
        layer1(nc, c)


def kernel(**inputs):
    import numpy as _np
    import concourse.bacc as _bacc
    from concourse.bass_utils import run_bass_kernel_spmd as _run

    nc = _bacc.Bacc("TRN2", target_bir_lowering=False, num_devices=1)
    arrays = {}

    def given(name):
        a = _np.ascontiguousarray(inputs[name])
        arrays[f"in_{name}"] = a
        return nc.dram_tensor(f"in_{name}", a.shape, mybir.dt.from_np(a.dtype), kind="ExternalInput").ap()

    c = Core()
    c.x = given("x")
    c.ctx = given("ctx_2048")
    c.Wq = given("L0_attn_Wq")
    c.Wk = given("L0_attn_Wk")
    c.Wv = given("L0_attn_Wv")
    c.Wo = given("L0_attn_Wo")
    c.betas = given("L0_attn_betas")
    c.ssm = given("L0_xattn_ssm_kernel")
    c.convD = given("L0_xattn_D")
    c.wg = given("L0_ffn_wg")
    c.fc1 = given("L0_ffn_fc1_w")
    c.fc1b = given("L0_ffn_fc1_b")
    c.fc2 = given("L0_ffn_fc2_w")
    c.fc2b = given("L0_ffn_fc2_b")
    c.wqkv = given("L1_attn_w_qkv")
    c.bqkv = given("L1_attn_b_qkv")
    c.wout = given("L1_attn_w_out")
    c.bout = given("L1_attn_b_out")
    c.QW = given("L1_xattn_QW")
    c.Qb = given("L1_xattn_Qb")
    c.KW = given("L1_xattn_KW")
    c.Kb = given("L1_xattn_Kb")
    c.VW = given("L1_xattn_VW")
    c.Vb = given("L1_xattn_Vb")
    c.wgate = given("L1_ffn_w_gate")
    c.wup = given("L1_ffn_w_up")
    c.wdown = given("L1_ffn_w_down")
    c.out = nc.dram_tensor("out", (B, S, D), F32, kind="ExternalOutput").ap()
    build(nc, c)
    return _run(nc, [arrays], core_ids=[0]).results[0]["out"]
```
